# Optimizing a Trainium2 kernel written in Bass

```python
import numpy as np
import jax
import jax.numpy as jnp

def _softmax(x, axis=-1):
    return jax.nn.softmax(x, axis=axis)

def _gelu(x):
    return jax.nn.gelu(x, approximate=True)

def _silu(x):
    return jax.nn.silu(x)

def _sigmoid(x):
    return jax.nn.sigmoid(x)

def _layernorm(x, axis=-1, eps=1e-05):
    m = jnp.mean(x, axis=axis, keepdims=True)
    v = jnp.var(x, axis=axis, keepdims=True)
    return (x - m) / jnp.sqrt(v + eps)

def _scatter_add(tgt, idx, src, axis=0):
    return tgt.at[idx].add(src)

def _segment_sum(src, seg, n):
    return jax.ops.segment_sum(src, seg, n)
kernel_name = 'mk_decoder_preln_d4_seqx_r8_040d6f'

def setup_inputs(seed: int=0):
    np.random.seed(seed)
    _w = jnp.asarray

    def _rec_inputs():
        import jax
        import jax.numpy as jnp
        _rk = jax.random.key(seed)
        x = 7.22e-05 + 1 * jax.random.normal(jax.random.fold_in(_rk, 1), (8, 128, 128), jnp.float32)
        _lenS = 128 - jax.random.randint(jax.random.fold_in(_rk, 7), (8,), 0, max(1, 128 // 4) + 1, jnp.int32)
        _lenS2 = 128 - jax.random.randint(jax.random.fold_in(_rk, 8), (8,), 0, max(1, 128 // 4) + 1, jnp.int32)
        _ctx_1024P = jax.random.normal(jax.random.fold_in(_rk, 11), (8, 16, 128), jnp.float32)
        _ctx_1024c = jax.random.dirichlet(jax.random.fold_in(_rk, 511), 0.3 * jnp.ones((16,), jnp.float32), (8, 128))
        _ctx_1024t = jnp.einsum('bsk,bkd->bsd', _ctx_1024c, _ctx_1024P)
        _ctx_1024t = _ctx_1024t * jax.lax.rsqrt(jnp.mean(jnp.square(_ctx_1024t)) + 1e-12) * 0.953939
        ctx_1024 = 4.13588e-05 + 0.999923 * (_ctx_1024t + 0.3 * jax.random.normal(jax.random.fold_in(_rk, 611), (8, 128, 128), jnp.float32))
        _validS = jnp.arange(128)[None, :] < _lenS[:, None]
        _validS2 = jnp.arange(128)[None, :] < _lenS2[:, None]
        _causal = jnp.tril(jnp.ones((128, 128), dtype=bool))
        mask_BxS2_bf1 = jnp.ones((8, 128), dtype=bool)
        return (x, ctx_1024, mask_BxS2_bf1)
    x, ctx_1024, mask_BxS2_bf1 = _rec_inputs()

    def _L0_attn_setup():
        import jax, jax.numpy as jnp
        import numpy as np
        B, L, D_MODEL = (4, 256, 128)
        D_INNER = 2 * D_MODEL
        D_STATE = 64
        D_CONV = 4
        DT_RANK = D_MODEL // 16

        def _mamba_block(x, ln_w, ln_b, W_in, conv_w, conv_b, W_xproj, W_dt, b_dt, A_log, D, W_out):
            residual = x
            mu = jnp.mean(x, axis=-1, keepdims=True)
            var = jnp.mean(jnp.square(x - mu), axis=-1, keepdims=True)
            xn = (x - mu) * jax.lax.rsqrt(var + 1e-05) * ln_w + ln_b
            xz = xn @ W_in
            xi, z = jnp.split(xz, 2, axis=-1)
            xc = jnp.transpose(xi, (0, 2, 1))
            xc = jax.lax.conv_general_dilated(xc, conv_w, window_strides=(1,), padding=[(D_CONV - 1, 0)], feature_group_count=D_INNER, dimension_numbers=('NCH', 'OIH', 'NCH'))
            xc = jnp.transpose(xc, (0, 2, 1)) + conv_b
            u = jax.nn.silu(xc)
            x_dbl = u @ W_xproj
            dt_r = x_dbl[..., :DT_RANK]
            Bm = x_dbl[..., DT_RANK:DT_RANK + D_STATE]
            Cm = x_dbl[..., DT_RANK + D_STATE:]
            delta = jax.nn.softplus(dt_r @ W_dt + b_dt)
            A = -jnp.exp(A_log)

            def step(h, inputs):
                d_t, B_t, C_t, u_t = inputs
                dA = jnp.exp(d_t[:, :, None] * A)
                h = h * dA + (d_t * u_t)[:, :, None] * B_t[:, None, :]
                y_t = jnp.einsum('bdn,bn->bd', h, C_t)
                return (h, y_t)
            h0 = jnp.zeros((x.shape[0], D_INNER, D_STATE), x.dtype)
            seq = (jnp.transpose(delta, (1, 0, 2)), jnp.transpose(Bm, (1, 0, 2)), jnp.transpose(Cm, (1, 0, 2)), jnp.transpose(u, (1, 0, 2)))
            _, ys = jax.lax.scan(step, h0, seq)
            y = jnp.transpose(ys, (1, 0, 2)) + u * D
            y = y * jax.nn.silu(z)
            out = y @ W_out
            return residual + out
        key = jax.random.key(seed)
        ks = jax.random.split(key, 10)
        inp = {}
        inp['x'] = jax.random.normal(ks[0], (B, L, D_MODEL), dtype=jnp.float32)
        inp['ln_w'] = jnp.ones((D_MODEL,), jnp.float32)
        inp['ln_b'] = jnp.zeros((D_MODEL,), jnp.float32)
        inp['W_in'] = jax.random.normal(ks[1], (D_MODEL, 2 * D_INNER), jnp.float32) / np.sqrt(D_MODEL)
        inp['conv_w'] = jax.random.normal(ks[2], (D_INNER, 1, D_CONV), jnp.float32) / np.sqrt(D_CONV)
        inp['conv_b'] = jax.random.normal(ks[3], (D_INNER,), jnp.float32) * 0.01
        inp['W_xproj'] = jax.random.normal(ks[4], (D_INNER, DT_RANK + 2 * D_STATE), jnp.float32) / np.sqrt(D_INNER)
        inp['W_dt'] = jax.random.normal(ks[5], (DT_RANK, D_INNER), jnp.float32) / np.sqrt(DT_RANK)
        inp['b_dt'] = jax.random.normal(ks[6], (D_INNER,), jnp.float32) * 0.1 - 4.0
        inp['A_log'] = jnp.log(jnp.broadcast_to(jnp.arange(1, D_STATE + 1, dtype=jnp.float32), (D_INNER, D_STATE)))
        inp['D'] = jnp.ones((D_INNER,), jnp.float32)
        inp['W_out'] = jax.random.normal(ks[7], (D_INNER, D_MODEL), jnp.float32) / np.sqrt(D_INNER)
        return inp
    _L0_attn_all = _L0_attn_setup()
    _L0_attn_in = {k: v for k, v in _L0_attn_all.items() if k in ('ln_w', 'ln_b', 'W_in', 'conv_w', 'conv_b', 'W_xproj', 'W_dt', 'b_dt', 'A_log', 'D', 'W_out')}
    del _L0_attn_all

    def _L0_xattn_setup():
        import jax, jax.numpy as jnp
        import numpy as np
        THETA = 10000.0

        def _rope_tables(T, head_dim, dtype):
            exps = jnp.arange(1, head_dim + 1, 2, dtype=jnp.float32)[:head_dim // 2] / head_dim
            w = 1.0 / THETA ** exps
            t = jnp.arange(1, T + 1, dtype=jnp.float32)
            angles = t[:, None] * w[None, :]
            return (jnp.sin(angles).astype(dtype), jnp.cos(angles).astype(dtype))

        def _rotate(x, sin, cos):
            x1 = x[..., ::2]
            x2 = x[..., 1::2]
            x1p = x1 * cos - x2 * sin
            x2p = x1 * sin + x2 * cos
            return jnp.stack((x1p, x2p), axis=-1).reshape(x.shape)
        key = jax.random.key(seed)
        B, Tq, Tkv, C = (4, 256, 256, 128)
        k1, k2, k3, k4, k5 = jax.random.split(key, 5)
        s = 1.0 / np.sqrt(C)
        return {'x_q': jax.random.normal(k1, (B, Tq, C), dtype=jnp.float32), 'x_kv': jax.random.normal(k2, (B, Tkv, C), dtype=jnp.float32), 'q_tok_mask': jnp.ones((B, Tq), dtype=bool), 'kv_tok_mask': jnp.ones((B, Tkv), dtype=bool), 'W_q': jax.random.normal(k3, (C, C), dtype=jnp.float32) * s, 'W_kv': jax.random.normal(k4, (C, 2 * C), dtype=jnp.float32) * s, 'W_c': jax.random.normal(k5, (C, C), dtype=jnp.float32) * s}
    _L0_xattn_all = _L0_xattn_setup()
    _L0_xattn_in = {k: v for k, v in _L0_xattn_all.items() if k in ('W_q', 'W_kv', 'W_c')}
    del _L0_xattn_all

    def _L0_ffn_setup():
        import jax, jax.numpy as jnp
        import numpy as np
        H = 128
        I = 64
        E = 8
        TOP_K = 2
        N_SHARED = 2
        SHARED_I = I * N_SHARED
        SCALE = 2.5
        NORM_TOPK = True
        B, S = (2, 128)

        def _swiglu(x, wg, wu, wd):
            g = x @ wg.T
            u = x @ wu.T
            return jax.nn.silu(g) * u @ wd.T
        key = jax.random.key(seed)
        ks = jax.random.split(key, 8)
        std = 0.02
        return {'hidden_states': jax.random.normal(ks[0], (B, S, H), jnp.float32), 'gate_weight': jax.random.normal(ks[1], (E, H), jnp.float32) * std, 'w_gate': jax.random.normal(ks[2], (E, I, H), jnp.float32) * std, 'w_up': jax.random.normal(ks[3], (E, I, H), jnp.float32) * std, 'w_down': jax.random.normal(ks[4], (E, H, I), jnp.float32) * std, 'ws_gate': jax.random.normal(ks[5], (SHARED_I, H), jnp.float32) * std, 'ws_up': jax.random.normal(ks[6], (SHARED_I, H), jnp.float32) * std, 'ws_down': jax.random.normal(ks[7], (H, SHARED_I), jnp.float32) * std}
    _L0_ffn_all = _L0_ffn_setup()
    _L0_ffn_in = {k: v for k, v in _L0_ffn_all.items() if k in ('gate_weight', 'w_gate', 'w_up', 'w_down', 'ws_gate', 'ws_up', 'ws_down')}
    del _L0_ffn_all

    def _L1_attn_setup():
        import jax, jax.numpy as jnp
        import numpy as np
        N_HEADS = 16
        MAX_LEN = 128
        key = jax.random.key(seed)
        ks = jax.random.split(key, 6)
        B, T, C = (4, 128, 128)
        scale = 0.02
        return {'x': jax.random.normal(ks[0], (B, T, C), dtype=jnp.float32), 'qkv_w': jax.random.normal(ks[1], (3 * C, C), dtype=jnp.float32) * scale, 'qkv_b': jax.random.normal(ks[2], (3 * C,), dtype=jnp.float32) * scale, 'proj_w': jax.random.normal(ks[3], (C, C), dtype=jnp.float32) * scale, 'proj_b': jax.random.normal(ks[4], (C,), dtype=jnp.float32) * scale, 'rel_pos_emb': jax.random.normal(ks[5], (2 * MAX_LEN - 1, C), dtype=jnp.float32) * scale}
    _L1_attn_all = _L1_attn_setup()
    _L1_attn_in = {k: v for k, v in _L1_attn_all.items() if k in ('qkv_w', 'qkv_b', 'proj_w', 'proj_b', 'rel_pos_emb')}
    del _L1_attn_all

    def _L1_xattn_setup():
        import jax, jax.numpy as jnp
        import numpy as np
        D1, D2, D3 = (128, 128, 128)
        key = jax.random.key(seed)
        k1, k2, kw, kb = jax.random.split(key, 4)
        x1 = jax.random.normal(k1, (8, 256, D1), dtype=jnp.float32)
        x2 = jax.random.normal(k2, (8, 256, D2), dtype=jnp.float32)
        bound = 1.0 / np.sqrt(D1 + D2)
        W = jax.random.uniform(kw, (D3, D1 + D2), minval=-bound, maxval=bound, dtype=jnp.float32)
        b = jax.random.uniform(kb, (D3,), minval=-bound, maxval=bound, dtype=jnp.float32)
        return {'x1': x1, 'x2': x2, 'W': W, 'b': b}
    _L1_xattn_all = _L1_xattn_setup()
    _L1_xattn_in = {k: v for k, v in _L1_xattn_all.items() if k in ('W', 'b')}
    del _L1_xattn_all

    def _L1_ffn_setup():
        import jax, jax.numpy as jnp
        import numpy as np
        D_MODEL, EXPERT_DIM, NUM_EXPERTS, TOP_K = (128, 256, 16, 2)
        SEQ_LEN, BATCH = (256, 2)
        key = jax.random.key(seed)
        ks = jax.random.split(key, 8)
        s_d = 1.0 / np.sqrt(D_MODEL)
        s_h = 1.0 / np.sqrt(EXPERT_DIM)
        return {'x': jax.random.normal(ks[0], (SEQ_LEN, BATCH, D_MODEL), jnp.float32), 'Wg': jax.random.uniform(ks[1], (D_MODEL, NUM_EXPERTS), jnp.float32, -s_d, s_d), 'bg': jax.random.uniform(ks[2], (NUM_EXPERTS,), jnp.float32, -s_d, s_d), 'bias': jnp.zeros((NUM_EXPERTS,), jnp.float32), 'W1': jax.random.uniform(ks[3], (NUM_EXPERTS, D_MODEL, EXPERT_DIM), jnp.float32, -s_d, s_d), 'b1': jax.random.uniform(ks[4], (NUM_EXPERTS, EXPERT_DIM), jnp.float32, -s_d, s_d), 'W2': jax.random.uniform(ks[5], (NUM_EXPERTS, EXPERT_DIM, D_MODEL), jnp.float32, -s_h, s_h), 'b2': jax.random.uniform(ks[6], (NUM_EXPERTS, D_MODEL), jnp.float32, -s_h, s_h)}
    _L1_ffn_all = _L1_ffn_setup()
    _L1_ffn_in = {k: v for k, v in _L1_ffn_all.items() if k in ('Wg', 'bg', 'bias', 'W1', 'b1', 'W2', 'b2')}
    del _L1_ffn_all

    def _L2_attn_setup():
        import jax, jax.numpy as jnp
        import numpy as np
        B, S, D = (2, 256, 128)
        N_HEADS, N_KV_HEADS = (16, 4)
        HEAD_DIM = D // N_HEADS
        KV_GROUPS = N_HEADS // N_KV_HEADS
        ROPE_BASE = 10000.0

        def _apply_rope(t, cos, sin):
            t1, t2 = jnp.split(t, 2, axis=-1)
            return jnp.concatenate([t1 * cos - t2 * sin, t1 * sin + t2 * cos], axis=-1)
        key = jax.random.key(seed)
        ks = jax.random.split(key, 5)
        s = 0.02
        return {'x': jax.random.normal(ks[0], (B, S, D), dtype=jnp.float32), 'wq': jax.random.normal(ks[1], (D, D), dtype=jnp.float32) * s, 'wk': jax.random.normal(ks[2], (D, N_KV_HEADS * HEAD_DIM), dtype=jnp.float32) * s, 'wv': jax.random.normal(ks[3], (D, N_KV_HEADS * HEAD_DIM), dtype=jnp.float32) * s, 'wo': jax.random.normal(ks[4], (D, D), dtype=jnp.float32) * s}
    _L2_attn_all = _L2_attn_setup()
    _L2_attn_in = {k: v for k, v in _L2_attn_all.items() if k in ('wq', 'wk', 'wv', 'wo')}
    del _L2_attn_all

    def _L2_xattn_setup():
        import jax, jax.numpy as jnp
        import numpy as np
        B, L_ENC, L_DEC, D = (16, 64, 128, 128)
        key = jax.random.key(seed)
        k1, k2, k3, k4, k5, k6 = jax.random.split(key, 6)
        encoder_hc = jax.random.normal(k1, (B, L_ENC, D), dtype=jnp.float32)
        decoder_hq = jax.random.normal(k2, (B, L_DEC, D), dtype=jnp.float32)
        w_sim = jax.random.normal(k3, (3 * D,), dtype=jnp.float32) * 0.02
        b_sim = jax.random.normal(k4, (1,), dtype=jnp.float32) * 0.02
        W_qv = jax.random.normal(k5, (4 * D, D), dtype=jnp.float32) * 0.02
        b_qv = jax.random.normal(k6, (D,), dtype=jnp.float32) * 0.02
        return {'encoder_hc': encoder_hc, 'decoder_hq': decoder_hq, 'w_sim': w_sim, 'b_sim': b_sim, 'W_qv': W_qv, 'b_qv': b_qv}
    _L2_xattn_all = _L2_xattn_setup()
    _L2_xattn_in = {k: v for k, v in _L2_xattn_all.items() if k in ('w_sim', 'b_sim', 'W_qv', 'b_qv')}
    del _L2_xattn_all

    def _L2_ffn_setup():
        import jax, jax.numpy as jnp
        import numpy as np
        D_MODEL = 128
        N_HEADS = 16
        HEAD_DIM = D_MODEL // N_HEADS
        FFN_DIM = 512
        N_EXPERTS = 8
        TOP_K = 2
        BATCH = 4
        SEQ = 128

        def _layernorm(x, w, b, eps=1e-05):
            mu = jnp.mean(x, axis=-1, keepdims=True)
            var = jnp.mean(jnp.square(x - mu), axis=-1, keepdims=True)
            return (x - mu) * jax.lax.rsqrt(var + eps) * w + b

        def _causal_attention(nx, Wqkv, bqkv, Wo, bo):
            B, S, D = nx.shape
            qkv = nx @ Wqkv + bqkv
            q, k, v = jnp.split(qkv, 3, axis=-1)
            q = q.reshape(B, S, N_HEADS, HEAD_DIM)
            k = k.reshape(B, S, N_HEADS, HEAD_DIM)
            v = v.reshape(B, S, N_HEADS, HEAD_DIM)
            scores = jnp.einsum('bqhd,bkhd->bhqk', q, k) / jnp.sqrt(jnp.float32(HEAD_DIM))
            causal = jnp.tril(jnp.ones((S, S), bool))
            scores = jnp.where(causal, scores, jnp.finfo(scores.dtype).min)
            attn = jax.nn.softmax(scores, axis=-1)
            out = jnp.einsum('bhqk,bkhd->bqhd', attn, v).reshape(B, S, D)
            return out @ Wo + bo

        def _moe_ffn(nx, gate_W, fc1_w, fc1_b, fc2_w, fc2_b):
            gate_logits = nx @ gate_W
            topk_vals, topk_idx = jax.lax.top_k(gate_logits, TOP_K)
            gate_w = jax.nn.softmax(topk_vals, axis=-1)
            dense_gates = jnp.sum(jax.nn.one_hot(topk_idx, N_EXPERTS, dtype=nx.dtype) * gate_w[..., None], axis=-2)
            moe_out = jnp.zeros_like(nx)
            for e in range(N_EXPERTS):
                h = jax.nn.gelu(jnp.einsum('bsd,fd->bsf', nx, fc1_w[e]) + fc1_b[e], approximate=False)
                y = jnp.einsum('bsf,df->bsd', h, fc2_w[e]) + fc2_b[e]
                moe_out = moe_out + y * dense_gates[..., e:e + 1]
            return moe_out
        key = jax.random.key(seed)
        ks = jax.random.split(key, 12)
        s = lambda k, shape, scale: jax.random.normal(k, shape, dtype=jnp.float32) * scale
        inp = {'x': s(ks[0], (BATCH, SEQ, D_MODEL), 1.0), 'ln1_w': jnp.ones((D_MODEL,), jnp.float32), 'ln1_b': jnp.zeros((D_MODEL,), jnp.float32), 'ln2_w': jnp.ones((D_MODEL,), jnp.float32), 'ln2_b': jnp.zeros((D_MODEL,), jnp.float32), 'Wqkv': s(ks[1], (D_MODEL, 3 * D_MODEL), 0.02), 'bqkv': jnp.zeros((3 * D_MODEL,), jnp.float32), 'Wo': s(ks[2], (D_MODEL, D_MODEL), 0.02), 'bo': jnp.zeros((D_MODEL,), jnp.float32), 'gate_W': s(ks[3], (D_MODEL, N_EXPERTS), 0.02), 'fc1_w': s(ks[4], (N_EXPERTS, FFN_DIM, D_MODEL), (2.0 / D_MODEL) ** 0.5), 'fc1_b': jnp.zeros((N_EXPERTS, FFN_DIM), jnp.float32), 'fc2_w': s(ks[5], (N_EXPERTS, D_MODEL, FFN_DIM), (1.0 / FFN_DIM) ** 0.5), 'fc2_b': jnp.zeros((N_EXPERTS, D_MODEL), jnp.float32)}
        return inp
    _L2_ffn_all = _L2_ffn_setup()
    _L2_ffn_in = {k: v for k, v in _L2_ffn_all.items() if k in ('ln1_w', 'ln1_b', 'ln2_w', 'ln2_b', 'Wqkv', 'bqkv', 'Wo', 'bo', 'gate_W', 'fc1_w', 'fc1_b', 'fc2_w', 'fc2_b')}
    del _L2_ffn_all

    def _L3_attn_setup():
        import jax, jax.numpy as jnp
        import numpy as np
        import math
        N_HEAD = 16

        def _causal_attn(q, k, v):
            d_k = q.shape[-1]
            s = jnp.einsum('bhqd,bhkd->bhqk', q, k) / math.sqrt(d_k)
            L, S = (q.shape[-2], k.shape[-2])
            mask = jnp.tril(jnp.ones((L, S), dtype=bool))
            s = jnp.where(mask, s, -jnp.inf)
            a = jax.nn.softmax(s, axis=-1)
            return jnp.einsum('bhqk,bhkd->bhqd', a, v)
        key = jax.random.key(seed)
        ks = jax.random.split(key, 8)
        B, T, C = (2, 256, 128)
        scale = 0.02
        return {'x': jax.random.normal(ks[0], (B, T, C), dtype=jnp.float32), 'W_attn': jax.random.normal(ks[1], (C, 2 * C), dtype=jnp.float32) * scale, 'b_attn': jnp.zeros((2 * C,), dtype=jnp.float32), 'W_k2': jax.random.normal(ks[2], (C, C), dtype=jnp.float32) * scale, 'b_k2': jnp.zeros((C,), dtype=jnp.float32), 'W_proj': jax.random.normal(ks[3], (C, C), dtype=jnp.float32) * scale, 'b_proj': jnp.zeros((C,), dtype=jnp.float32)}
    _L3_attn_all = _L3_attn_setup()
    _L3_attn_in = {k: v for k, v in _L3_attn_all.items() if k in ('W_attn', 'b_attn', 'W_k2', 'b_k2', 'W_proj', 'b_proj')}
    del _L3_attn_all

    def _L3_xattn_setup():
        import jax, jax.numpy as jnp
        import numpy as np
        import math
        B, L, D, H = (8, 512, 128, 16)
        DK = D // H
        FACTOR = 1

        def _linear(x, W, b):
            return jnp.einsum('bld,od->blo', x, W) + b
        rng = jax.random.key(seed)
        ks = jax.random.split(rng, 11)
        s = 0.02
        return {'query': jax.random.normal(ks[0], (B, L, D), jnp.float32), 'key': jax.random.normal(ks[1], (B, L, D), jnp.float32), 'value': jax.random.normal(ks[2], (B, L, D), jnp.float32), 'Wq': jax.random.normal(ks[3], (D, D), jnp.float32) * s, 'bq': jax.random.normal(ks[4], (D,), jnp.float32) * s, 'Wk': jax.random.normal(ks[5], (D, D), jnp.float32) * s, 'bk': jax.random.normal(ks[6], (D,), jnp.float32) * s, 'Wv': jax.random.normal(ks[7], (D, D), jnp.float32) * s, 'bv': jax.random.normal(ks[8], (D,), jnp.float32) * s, 'Wo': jax.random.normal(ks[9], (D, D), jnp.float32) * s, 'bo': jax.random.normal(ks[10], (D,), jnp.float32) * s}
    _L3_xattn_all = _L3_xattn_setup()
    _L3_xattn_in = {k: v for k, v in _L3_xattn_all.items() if k in ('Wq', 'bq', 'Wk', 'bk', 'Wv', 'bv', 'Wo', 'bo')}
    del _L3_xattn_all

    def _L3_ffn_setup():
        import jax, jax.numpy as jnp
        import numpy as np
        H = 128
        DFF = 512
        E_ROUTED = 7
        TOP_K = 2

        def _swiglu(flat, gate_w, up_w, down_w):
            g = flat @ gate_w.T
            up = flat @ up_w.T
            return jax.nn.silu(g) * up @ down_w.T
        key = jax.random.key(seed)
        ks = jax.random.split(key, 8)
        s = 0.02
        return {'x': jax.random.normal(ks[0], (4, 256, H), jnp.float32), 'shared_up': jax.random.normal(ks[1], (DFF, H), jnp.float32) * s, 'shared_gate': jax.random.normal(ks[2], (DFF, H), jnp.float32) * s, 'shared_down': jax.random.normal(ks[3], (H, DFF), jnp.float32) * s, 'routed_up': jax.random.normal(ks[4], (E_ROUTED, DFF, H), jnp.float32) * s, 'routed_gate': jax.random.normal(ks[5], (E_ROUTED, DFF, H), jnp.float32) * s, 'routed_down': jax.random.normal(ks[6], (E_ROUTED, H, DFF), jnp.float32) * s, 'router_w': jax.random.normal(ks[7], (E_ROUTED, H), jnp.float32) * 0.02}
    _L3_ffn_all = _L3_ffn_setup()
    _L3_ffn_in = {k: v for k, v in _L3_ffn_all.items() if k in ('shared_up', 'shared_gate', 'shared_down', 'routed_up', 'routed_gate', 'routed_down', 'router_w')}
    del _L3_ffn_all
    return {'x': x, 'ctx_1024': ctx_1024, 'mask_BxS2_bf1': mask_BxS2_bf1, 'L0_attn_ln_w': _L0_attn_in['ln_w'], 'L0_attn_ln_b': _L0_attn_in['ln_b'], 'L0_attn_W_in': _L0_attn_in['W_in'], 'L0_attn_conv_w': _L0_attn_in['conv_w'], 'L0_attn_conv_b': _L0_attn_in['conv_b'], 'L0_attn_W_xproj': _L0_attn_in['W_xproj'], 'L0_attn_W_dt': _L0_attn_in['W_dt'], 'L0_attn_b_dt': _L0_attn_in['b_dt'], 'L0_attn_A_log': _L0_attn_in['A_log'], 'L0_attn_D': _L0_attn_in['D'], 'L0_attn_W_out': _L0_attn_in['W_out'], 'L0_xattn_W_q': _L0_xattn_in['W_q'], 'L0_xattn_W_kv': _L0_xattn_in['W_kv'], 'L0_xattn_W_c': _L0_xattn_in['W_c'], 'L0_ffn_gate_weight': _L0_ffn_in['gate_weight'], 'L0_ffn_w_gate': _L0_ffn_in['w_gate'], 'L0_ffn_w_up': _L0_ffn_in['w_up'], 'L0_ffn_w_down': _L0_ffn_in['w_down'], 'L0_ffn_ws_gate': _L0_ffn_in['ws_gate'], 'L0_ffn_ws_up': _L0_ffn_in['ws_up'], 'L0_ffn_ws_down': _L0_ffn_in['ws_down'], 'L1_attn_qkv_w': _L1_attn_in['qkv_w'], 'L1_attn_qkv_b': _L1_attn_in['qkv_b'], 'L1_attn_proj_w': _L1_attn_in['proj_w'], 'L1_attn_proj_b': _L1_attn_in['proj_b'], 'L1_attn_rel_pos_emb': _L1_attn_in['rel_pos_emb'], 'L1_xattn_W': _L1_xattn_in['W'], 'L1_xattn_b': _L1_xattn_in['b'], 'L1_ffn_Wg': _L1_ffn_in['Wg'], 'L1_ffn_bg': _L1_ffn_in['bg'], 'L1_ffn_bias': _L1_ffn_in['bias'], 'L1_ffn_W1': _L1_ffn_in['W1'], 'L1_ffn_b1': _L1_ffn_in['b1'], 'L1_ffn_W2': _L1_ffn_in['W2'], 'L1_ffn_b2': _L1_ffn_in['b2'], 'L2_attn_wq': _L2_attn_in['wq'], 'L2_attn_wk': _L2_attn_in['wk'], 'L2_attn_wv': _L2_attn_in['wv'], 'L2_attn_wo': _L2_attn_in['wo'], 'L2_xattn_w_sim': _L2_xattn_in['w_sim'], 'L2_xattn_b_sim': _L2_xattn_in['b_sim'], 'L2_xattn_W_qv': _L2_xattn_in['W_qv'], 'L2_xattn_b_qv': _L2_xattn_in['b_qv'], 'L2_ffn_ln1_w': _L2_ffn_in['ln1_w'], 'L2_ffn_ln1_b': _L2_ffn_in['ln1_b'], 'L2_ffn_ln2_w': _L2_ffn_in['ln2_w'], 'L2_ffn_ln2_b': _L2_ffn_in['ln2_b'], 'L2_ffn_Wqkv': _L2_ffn_in['Wqkv'], 'L2_ffn_bqkv': _L2_ffn_in['bqkv'], 'L2_ffn_Wo': _L2_ffn_in['Wo'], 'L2_ffn_bo': _L2_ffn_in['bo'], 'L2_ffn_gate_W': _L2_ffn_in['gate_W'], 'L2_ffn_fc1_w': _L2_ffn_in['fc1_w'], 'L2_ffn_fc1_b': _L2_ffn_in['fc1_b'], 'L2_ffn_fc2_w': _L2_ffn_in['fc2_w'], 'L2_ffn_fc2_b': _L2_ffn_in['fc2_b'], 'L3_attn_W_attn': _L3_attn_in['W_attn'], 'L3_attn_b_attn': _L3_attn_in['b_attn'], 'L3_attn_W_k2': _L3_attn_in['W_k2'], 'L3_attn_b_k2': _L3_attn_in['b_k2'], 'L3_attn_W_proj': _L3_attn_in['W_proj'], 'L3_attn_b_proj': _L3_attn_in['b_proj'], 'L3_xattn_Wq': _L3_xattn_in['Wq'], 'L3_xattn_bq': _L3_xattn_in['bq'], 'L3_xattn_Wk': _L3_xattn_in['Wk'], 'L3_xattn_bk': _L3_xattn_in['bk'], 'L3_xattn_Wv': _L3_xattn_in['Wv'], 'L3_xattn_bv': _L3_xattn_in['bv'], 'L3_xattn_Wo': _L3_xattn_in['Wo'], 'L3_xattn_bo': _L3_xattn_in['bo'], 'L3_ffn_shared_up': _L3_ffn_in['shared_up'], 'L3_ffn_shared_gate': _L3_ffn_in['shared_gate'], 'L3_ffn_shared_down': _L3_ffn_in['shared_down'], 'L3_ffn_routed_up': _L3_ffn_in['routed_up'], 'L3_ffn_routed_gate': _L3_ffn_in['routed_gate'], 'L3_ffn_routed_down': _L3_ffn_in['routed_down'], 'L3_ffn_router_w': _L3_ffn_in['router_w']}

def reference(x, ctx_1024, mask_BxS2_bf1, L0_attn_ln_w, L0_attn_ln_b, L0_attn_W_in, L0_attn_conv_w, L0_attn_conv_b, L0_attn_W_xproj, L0_attn_W_dt, L0_attn_b_dt, L0_attn_A_log, L0_attn_D, L0_attn_W_out, L0_xattn_W_q, L0_xattn_W_kv, L0_xattn_W_c, L0_ffn_gate_weight, L0_ffn_w_gate, L0_ffn_w_up, L0_ffn_w_down, L0_ffn_ws_gate, L0_ffn_ws_up, L0_ffn_ws_down, L1_attn_qkv_w, L1_attn_qkv_b, L1_attn_proj_w, L1_attn_proj_b, L1_attn_rel_pos_emb, L1_xattn_W, L1_xattn_b, L1_ffn_Wg, L1_ffn_bg, L1_ffn_bias, L1_ffn_W1, L1_ffn_b1, L1_ffn_W2, L1_ffn_b2, L2_attn_wq, L2_attn_wk, L2_attn_wv, L2_attn_wo, L2_xattn_w_sim, L2_xattn_b_sim, L2_xattn_W_qv, L2_xattn_b_qv, L2_ffn_ln1_w, L2_ffn_ln1_b, L2_ffn_ln2_w, L2_ffn_ln2_b, L2_ffn_Wqkv, L2_ffn_bqkv, L2_ffn_Wo, L2_ffn_bo, L2_ffn_gate_W, L2_ffn_fc1_w, L2_ffn_fc1_b, L2_ffn_fc2_w, L2_ffn_fc2_b, L3_attn_W_attn, L3_attn_b_attn, L3_attn_W_k2, L3_attn_b_k2, L3_attn_W_proj, L3_attn_b_proj, L3_xattn_Wq, L3_xattn_bq, L3_xattn_Wk, L3_xattn_bk, L3_xattn_Wv, L3_xattn_bv, L3_xattn_Wo, L3_xattn_bo, L3_ffn_shared_up, L3_ffn_shared_gate, L3_ffn_shared_down, L3_ffn_routed_up, L3_ffn_routed_gate, L3_ffn_routed_down, L3_ffn_router_w):
    import jax
    import jax.numpy as jnp

    def _L0_attn_ref(x, ln_w, ln_b, W_in, conv_w, conv_b, W_xproj, W_dt, b_dt, A_log, D, W_out):
        import jax, jax.numpy as jnp
        import numpy as np
        B, L, D_MODEL = (4, 256, 128)
        D_INNER = 2 * D_MODEL
        D_STATE = 64
        D_CONV = 4
        DT_RANK = D_MODEL // 16

        def _mamba_block(x, ln_w, ln_b, W_in, conv_w, conv_b, W_xproj, W_dt, b_dt, A_log, D, W_out):
            residual = x
            mu = jnp.mean(x, axis=-1, keepdims=True)
            var = jnp.mean(jnp.square(x - mu), axis=-1, keepdims=True)
            xn = (x - mu) * jax.lax.rsqrt(var + 1e-05) * ln_w + ln_b
            xz = xn @ W_in
            xi, z = jnp.split(xz, 2, axis=-1)
            xc = jnp.transpose(xi, (0, 2, 1))
            xc = jax.lax.conv_general_dilated(xc, conv_w, window_strides=(1,), padding=[(D_CONV - 1, 0)], feature_group_count=D_INNER, dimension_numbers=('NCH', 'OIH', 'NCH'))
            xc = jnp.transpose(xc, (0, 2, 1)) + conv_b
            u = jax.nn.silu(xc)
            x_dbl = u @ W_xproj
            dt_r = x_dbl[..., :DT_RANK]
            Bm = x_dbl[..., DT_RANK:DT_RANK + D_STATE]
            Cm = x_dbl[..., DT_RANK + D_STATE:]
            delta = jax.nn.softplus(dt_r @ W_dt + b_dt)
            A = -jnp.exp(A_log)

            def step(h, inputs):
                d_t, B_t, C_t, u_t = inputs
                dA = jnp.exp(d_t[:, :, None] * A)
                h = h * dA + (d_t * u_t)[:, :, None] * B_t[:, None, :]
                y_t = jnp.einsum('bdn,bn->bd', h, C_t)
                return (h, y_t)
            h0 = jnp.zeros((x.shape[0], D_INNER, D_STATE), x.dtype)
            seq = (jnp.transpose(delta, (1, 0, 2)), jnp.transpose(Bm, (1, 0, 2)), jnp.transpose(Cm, (1, 0, 2)), jnp.transpose(u, (1, 0, 2)))
            _, ys = jax.lax.scan(step, h0, seq)
            y = jnp.transpose(ys, (1, 0, 2)) + u * D
            y = y * jax.nn.silu(z)
            out = y @ W_out
            return residual + out
        return _mamba_block(x, ln_w, ln_b, W_in, conv_w, conv_b, W_xproj, W_dt, b_dt, A_log, D, W_out)

    def _L0_xattn_ref(x_q, x_kv, q_tok_mask, kv_tok_mask, W_q, W_kv, W_c):
        import jax, jax.numpy as jnp
        import numpy as np
        THETA = 10000.0

        def _rope_tables(T, head_dim, dtype):
            exps = jnp.arange(1, head_dim + 1, 2, dtype=jnp.float32)[:head_dim // 2] / head_dim
            w = 1.0 / THETA ** exps
            t = jnp.arange(1, T + 1, dtype=jnp.float32)
            angles = t[:, None] * w[None, :]
            return (jnp.sin(angles).astype(dtype), jnp.cos(angles).astype(dtype))

        def _rotate(x, sin, cos):
            x1 = x[..., ::2]
            x2 = x[..., 1::2]
            x1p = x1 * cos - x2 * sin
            x2p = x1 * sin + x2 * cos
            return jnp.stack((x1p, x2p), axis=-1).reshape(x.shape)
        B, Tq, C = x_q.shape
        Tkv = x_kv.shape[1]
        H = 16
        D = C // H
        q = (x_q @ W_q).reshape(B, Tq, H, D).transpose(0, 2, 1, 3)
        kv = x_kv @ W_kv
        k, v = (kv[..., :C], kv[..., C:])
        k = k.reshape(B, Tkv, H, D).transpose(0, 2, 1, 3)
        v = v.reshape(B, Tkv, H, D).transpose(0, 2, 1, 3)
        sin_q, cos_q = _rope_tables(Tq, D, x_q.dtype)
        sin_k, cos_k = _rope_tables(Tkv, D, x_q.dtype)
        q = _rotate(q, sin_q, cos_q)
        k = _rotate(k, sin_k, cos_k)
        att = jnp.einsum('bhqd,bhkd->bhqk', q, k) / jnp.sqrt(jnp.asarray(D, x_q.dtype))
        mask = (q_tok_mask[:, :, None] & kv_tok_mask[:, None, :])[:, None, :, :]
        att = jnp.where(mask, att, jnp.asarray(-1000000000.0, att.dtype))
        att = jax.nn.softmax(att, axis=-1)
        y = jnp.einsum('bhqk,bhkd->bhqd', att, v)
        y = y.transpose(0, 2, 1, 3).reshape(B, Tq, C)
        return y @ W_c

    def _L0_ffn_ref(hidden_states, gate_weight, w_gate, w_up, w_down, ws_gate, ws_up, ws_down):
        import jax, jax.numpy as jnp
        import numpy as np
        H = 128
        I = 64
        E = 8
        TOP_K = 2
        N_SHARED = 2
        SHARED_I = I * N_SHARED
        SCALE = 2.5
        NORM_TOPK = True
        B, S = (2, 128)

        def _swiglu(x, wg, wu, wd):
            g = x @ wg.T
            u = x @ wu.T
            return jax.nn.silu(g) * u @ wd.T
        b, s, h = hidden_states.shape
        x = hidden_states.reshape(-1, h)
        shared_out = _swiglu(x, ws_gate, ws_up, ws_down)
        logits = x.astype(jnp.float32) @ gate_weight.astype(jnp.float32).T
        scores = jax.nn.sigmoid(logits)
        topk_w, topk_idx = jax.lax.top_k(scores, TOP_K)
        if TOP_K > 1 and NORM_TOPK:
            topk_w = topk_w / (topk_w.sum(-1, keepdims=True) + 1e-20)
        topk_w = topk_w * SCALE
        onehot = jax.nn.one_hot(topk_idx, E, dtype=topk_w.dtype)
        combine = jnp.einsum('tk,tke->te', topk_w, onehot)
        g = jnp.einsum('th,eih->tei', x, w_gate)
        u = jnp.einsum('th,eih->tei', x, w_up)
        hmid = jax.nn.silu(g) * u
        y = jnp.einsum('tei,ehi->teh', hmid, w_down)
        routed_out = jnp.einsum('te,teh->th', combine, y)
        out = (routed_out + shared_out).reshape(b, s, h)
        return out

    def _L1_attn_ref(x, qkv_w, qkv_b, proj_w, proj_b, rel_pos_emb):
        import jax, jax.numpy as jnp
        import numpy as np
        N_HEADS = 16
        MAX_LEN = 128
        B, T, C = x.shape
        H = N_HEADS
        D = C // H
        qkv = (x @ qkv_w.T + qkv_b).reshape(B, T, 3, H, D)
        qkv = jnp.transpose(qkv, (2, 0, 3, 1, 4))
        q, k, v = (qkv[0], qkv[1], qkv[2])
        att = jnp.einsum('bhtd,bhsd->bhts', q, k) / np.sqrt(D).astype(np.float32)
        table = rel_pos_emb.reshape(2 * MAX_LEN - 1, H, D).sum(axis=-1)
        pos = jnp.arange(T)
        rel_idx = pos[:, None] - pos[None, :] + (MAX_LEN - 1)
        bias = jnp.transpose(table[rel_idx], (2, 0, 1))
        att = att + bias[None]
        causal = pos[None, :] > pos[:, None]
        att = jnp.where(causal[None, None], -jnp.inf, att)
        att = jax.nn.softmax(att, axis=-1)
        out = jnp.einsum('bhts,bhsd->bhtd', att, v)
        out = jnp.transpose(out, (0, 2, 1, 3)).reshape(B, T, C)
        return out @ proj_w.T + proj_b

    def _L1_xattn_ref(x1, x2, W, b):
        import jax, jax.numpy as jnp
        import numpy as np
        D1, D2, D3 = (128, 128, 128)
        d1 = x1.shape[-1]
        W1 = W[:, :d1]
        W2 = W[:, d1:]
        part1 = jnp.einsum('bld,ed->ble', x1, W1)
        part2 = jnp.einsum('bld,ed->be', x2, W2) / x2.shape[1]
        return part1 + part2[:, None, :] + b

    def _L1_ffn_ref(x, Wg, bg, bias, W1, b1, W2, b2):
        import jax, jax.numpy as jnp
        import numpy as np
        D_MODEL, EXPERT_DIM, NUM_EXPERTS, TOP_K = (128, 256, 16, 2)
        SEQ_LEN, BATCH = (256, 2)
        logits = jnp.einsum('sbd,de->sbe', x, Wg) + bg + bias
        vals, idx = jax.lax.top_k(logits, TOP_K)
        w = jax.nn.softmax(vals - jnp.max(vals, axis=-1, keepdims=True), axis=-1)
        cw = jnp.einsum('sbk,sbke->sbe', w, jax.nn.one_hot(idx, NUM_EXPERTS, dtype=x.dtype))
        h = jax.nn.relu(jnp.einsum('sbd,edh->esbh', x, W1) + b1[:, None, None, :])
        y = jnp.einsum('esbh,ehd->esbd', h, W2) + b2[:, None, None, :]
        out = jnp.einsum('esbd,sbe->sbd', y, cw)
        return out

    def _L2_attn_ref(x, wq, wk, wv, wo):
        import jax, jax.numpy as jnp
        import numpy as np
        B, S, D = (2, 256, 128)
        N_HEADS, N_KV_HEADS = (16, 4)
        HEAD_DIM = D // N_HEADS
        KV_GROUPS = N_HEADS // N_KV_HEADS
        ROPE_BASE = 10000.0

        def _apply_rope(t, cos, sin):
            t1, t2 = jnp.split(t, 2, axis=-1)
            return jnp.concatenate([t1 * cos - t2 * sin, t1 * sin + t2 * cos], axis=-1)
        Bx, Sx, Dx = x.shape
        q = (x @ wq).reshape(Bx, Sx, N_HEADS, HEAD_DIM)
        k = (x @ wk).reshape(Bx, Sx, N_KV_HEADS, HEAD_DIM)
        v = (x @ wv).reshape(Bx, Sx, N_KV_HEADS, HEAD_DIM)
        half = HEAD_DIM // 2
        inv_freq = 1.0 / ROPE_BASE ** (jnp.arange(0, half, dtype=jnp.float32) / half)
        pos = jnp.arange(Sx, dtype=jnp.float32)
        ang = pos[:, None] * inv_freq[None, :]
        cos = jnp.cos(ang)[:, None, :]
        sin = jnp.sin(ang)[:, None, :]
        q = _apply_rope(q, cos, sin)
        k = _apply_rope(k, cos, sin)
        k = jnp.broadcast_to(k[:, :, None, :, :], (Bx, Sx, KV_GROUPS, N_KV_HEADS, HEAD_DIM)).reshape(Bx, Sx, N_HEADS, HEAD_DIM)
        v = jnp.broadcast_to(v[:, :, None, :, :], (Bx, Sx, KV_GROUPS, N_KV_HEADS, HEAD_DIM)).reshape(Bx, Sx, N_HEADS, HEAD_DIM)
        scale = 1.0 / jnp.sqrt(jnp.float32(HEAD_DIM))
        scores = jnp.einsum('bshd,bthd->bhst', q, k) * scale
        causal = jnp.tril(jnp.ones((Sx, Sx), dtype=bool))
        scores = jnp.where(causal[None, None, :, :], scores, jnp.float32(-jnp.inf))
        attn = jax.nn.softmax(scores, axis=-1)
        out = jnp.einsum('bhst,bthd->bshd', attn, v).reshape(Bx, Sx, Dx)
        return out @ wo

    def _L2_xattn_ref(encoder_hc, decoder_hq, w_sim, b_sim, W_qv, b_qv):
        import jax, jax.numpy as jnp
        import numpy as np
        B, L_ENC, L_DEC, D = (16, 64, 128, 128)
        d = encoder_hc.shape[-1]
        w1, w2, w3 = (w_sim[:d], w_sim[d:2 * d], w_sim[2 * d:])
        Sim = (encoder_hc @ w1)[:, :, None] + (decoder_hq @ w2)[:, None, :] + jnp.einsum('bid,bjd->bij', encoder_hc * w3, decoder_hq) + b_sim[0]
        A = jax.nn.softmax(Sim, axis=2)
        hq_hat = jnp.einsum('bij,bjd->bid', A, decoder_hq)
        Batt = jax.nn.softmax(jnp.max(Sim, axis=2), axis=1)
        hc_bar = jnp.einsum('bi,bid->bd', Batt, encoder_hc)[:, None, :]
        hc_hat = jnp.broadcast_to(hc_bar, encoder_hc.shape)
        feats = jnp.concatenate([encoder_hc, hq_hat, encoder_hc * hq_hat, encoder_hc * hc_hat], axis=-1)
        hcq = feats @ W_qv + b_qv
        return hcq

    def _L2_ffn_ref(x, ln1_w, ln1_b, ln2_w, ln2_b, Wqkv, bqkv, Wo, bo, gate_W, fc1_w, fc1_b, fc2_w, fc2_b):
        import jax, jax.numpy as jnp
        import numpy as np
        D_MODEL = 128
        N_HEADS = 16
        HEAD_DIM = D_MODEL // N_HEADS
        FFN_DIM = 512
        N_EXPERTS = 8
        TOP_K = 2
        BATCH = 4
        SEQ = 128

        def _layernorm(x, w, b, eps=1e-05):
            mu = jnp.mean(x, axis=-1, keepdims=True)
            var = jnp.mean(jnp.square(x - mu), axis=-1, keepdims=True)
            return (x - mu) * jax.lax.rsqrt(var + eps) * w + b

        def _causal_attention(nx, Wqkv, bqkv, Wo, bo):
            B, S, D = nx.shape
            qkv = nx @ Wqkv + bqkv
            q, k, v = jnp.split(qkv, 3, axis=-1)
            q = q.reshape(B, S, N_HEADS, HEAD_DIM)
            k = k.reshape(B, S, N_HEADS, HEAD_DIM)
            v = v.reshape(B, S, N_HEADS, HEAD_DIM)
            scores = jnp.einsum('bqhd,bkhd->bhqk', q, k) / jnp.sqrt(jnp.float32(HEAD_DIM))
            causal = jnp.tril(jnp.ones((S, S), bool))
            scores = jnp.where(causal, scores, jnp.finfo(scores.dtype).min)
            attn = jax.nn.softmax(scores, axis=-1)
            out = jnp.einsum('bhqk,bkhd->bqhd', attn, v).reshape(B, S, D)
            return out @ Wo + bo

        def _moe_ffn(nx, gate_W, fc1_w, fc1_b, fc2_w, fc2_b):
            gate_logits = nx @ gate_W
            topk_vals, topk_idx = jax.lax.top_k(gate_logits, TOP_K)
            gate_w = jax.nn.softmax(topk_vals, axis=-1)
            dense_gates = jnp.sum(jax.nn.one_hot(topk_idx, N_EXPERTS, dtype=nx.dtype) * gate_w[..., None], axis=-2)
            moe_out = jnp.zeros_like(nx)
            for e in range(N_EXPERTS):
                h = jax.nn.gelu(jnp.einsum('bsd,fd->bsf', nx, fc1_w[e]) + fc1_b[e], approximate=False)
                y = jnp.einsum('bsf,df->bsd', h, fc2_w[e]) + fc2_b[e]
                moe_out = moe_out + y * dense_gates[..., e:e + 1]
            return moe_out
        nx = _layernorm(x, ln1_w, ln1_b)
        attn_out = _causal_attention(nx, Wqkv, bqkv, Wo, bo)
        x = x + attn_out
        nx2 = _layernorm(x, ln2_w, ln2_b)
        moe_out = _moe_ffn(nx2, gate_W, fc1_w, fc1_b, fc2_w, fc2_b)
        return x + moe_out

    def _L3_attn_ref(x, W_attn, b_attn, W_k2, b_k2, W_proj, b_proj):
        import jax, jax.numpy as jnp
        import numpy as np
        import math
        N_HEAD = 16

        def _causal_attn(q, k, v):
            d_k = q.shape[-1]
            s = jnp.einsum('bhqd,bhkd->bhqk', q, k) / math.sqrt(d_k)
            L, S = (q.shape[-2], k.shape[-2])
            mask = jnp.tril(jnp.ones((L, S), dtype=bool))
            s = jnp.where(mask, s, -jnp.inf)
            a = jax.nn.softmax(s, axis=-1)
            return jnp.einsum('bhqk,bhkd->bhqd', a, v)
        B, T, C = x.shape
        H = N_HEAD
        d = C // H
        qk = x @ W_attn + b_attn
        q, k = (qk[..., :C], qk[..., C:])
        q = q.reshape(B, T, H, d).transpose(0, 2, 1, 3)
        k = k.reshape(B, T, H, d).transpose(0, 2, 1, 3)
        v = x.reshape(B, T, H, d).transpose(0, 2, 1, 3)
        y = _causal_attn(q, k, v)
        e = v[:, :, 1:, :] - y[:, :, :-1, :]
        k2 = (x[:, :-1] @ W_k2 + b_k2).reshape(B, T - 1, H, d).transpose(0, 2, 1, 3)
        q2 = q[:, :, 1:, :]
        y2 = _causal_attn(q2, k2, e)
        y2 = jnp.concatenate([jnp.zeros_like(y2[:, :, :1, :]), y2], axis=2)

        def proj(t):
            return t.transpose(0, 2, 1, 3).reshape(B, T, C) @ W_proj + b_proj
        return proj(y) + proj(y2)

    def _L3_xattn_ref(query, key, value, Wq, bq, Wk, bk, Wv, bv, Wo, bo):
        import jax, jax.numpy as jnp
        import numpy as np
        import math
        B, L, D, H = (8, 512, 128, 16)
        DK = D // H
        FACTOR = 1

        def _linear(x, W, b):
            return jnp.einsum('bld,od->blo', x, W) + b
        Bx, Lx, _ = query.shape
        Q = _linear(query, Wq, bq).reshape(Bx, Lx, H, DK).transpose(0, 2, 1, 3)
        K = _linear(key, Wk, bk).reshape(Bx, Lx, H, DK).transpose(0, 2, 1, 3)
        V = _linear(value, Wv, bv).reshape(Bx, Lx, H, DK).transpose(0, 2, 1, 3)
        Qf = jnp.fft.rfft(Q, axis=2)
        Kf = jnp.fft.rfft(K, axis=2)
        corr = jnp.fft.irfft(Qf * jnp.conj(Kf), n=Lx, axis=2)
        corr_mean = corr.mean(axis=-1)
        top_k = max(1, int(FACTOR * math.log(Lx + 1)))
        top_k = min(top_k, Lx)
        top_w, top_idx = jax.lax.top_k(corr_mean, top_k)
        top_w = jax.nn.softmax(top_w, axis=-1)
        pos = jnp.arange(Lx)
        out = jnp.zeros_like(V)
        for i in range(top_k):
            gidx = (pos[None, None, :] - top_idx[:, :, i, None]) % Lx
            rolled = jnp.take_along_axis(V, gidx[..., None], axis=2)
            out = out + top_w[:, :, i, None, None] * rolled
        out = out.transpose(0, 2, 1, 3).reshape(Bx, Lx, D)
        out = _linear(out, Wo, bo)
        return out

    def _L3_ffn_ref(x, shared_up, shared_gate, shared_down, routed_up, routed_gate, routed_down, router_w):
        import jax, jax.numpy as jnp
        import numpy as np
        H = 128
        DFF = 512
        E_ROUTED = 7
        TOP_K = 2

        def _swiglu(flat, gate_w, up_w, down_w):
            g = flat @ gate_w.T
            up = flat @ up_w.T
            return jax.nn.silu(g) * up @ down_w.T
        orig_shape = x.shape
        flat = x.reshape(-1, H)
        out = _swiglu(flat, shared_gate, shared_up, shared_down)
        logits = flat @ router_w.T
        probs = jax.nn.softmax(logits, axis=-1)
        top_vals, top_idx = jax.lax.top_k(probs, TOP_K)
        top_vals = top_vals / (top_vals.sum(-1, keepdims=True) + 1e-09)
        combine = jnp.sum(jax.nn.one_hot(top_idx, E_ROUTED, dtype=flat.dtype) * top_vals[..., None], axis=1)
        routed = jnp.zeros_like(flat)
        for e in range(E_ROUTED):
            eo = _swiglu(flat, routed_gate[e], routed_up[e], routed_down[e])
            routed = routed + combine[:, e:e + 1] * eo
        return (out + routed).reshape(orig_shape)
    x = x + _L0_attn_ref(_layernorm(x, axis=-1), L0_attn_ln_w, L0_attn_ln_b, L0_attn_W_in, L0_attn_conv_w, L0_attn_conv_b, L0_attn_W_xproj, L0_attn_W_dt, L0_attn_b_dt, L0_attn_A_log, L0_attn_D, L0_attn_W_out)
    x = x + _L0_xattn_ref(_layernorm(x, axis=-1), ctx_1024, mask_BxS2_bf1, mask_BxS2_bf1, L0_xattn_W_q, L0_xattn_W_kv, L0_xattn_W_c)
    x = x + _L0_ffn_ref(_layernorm(x, axis=-1), L0_ffn_gate_weight, L0_ffn_w_gate, L0_ffn_w_up, L0_ffn_w_down, L0_ffn_ws_gate, L0_ffn_ws_up, L0_ffn_ws_down)
    x = x + _L1_attn_ref(_layernorm(x, axis=-1), L1_attn_qkv_w, L1_attn_qkv_b, L1_attn_proj_w, L1_attn_proj_b, L1_attn_rel_pos_emb)
    x = x + _L1_xattn_ref(_layernorm(x, axis=-1), ctx_1024, L1_xattn_W, L1_xattn_b)
    x = x + _L1_ffn_ref(_layernorm(x, axis=-1), L1_ffn_Wg, L1_ffn_bg, L1_ffn_bias, L1_ffn_W1, L1_ffn_b1, L1_ffn_W2, L1_ffn_b2)
    x = x + _L2_attn_ref(_layernorm(x, axis=-1), L2_attn_wq, L2_attn_wk, L2_attn_wv, L2_attn_wo)
    x = x + _L2_xattn_ref(_layernorm(x, axis=-1), ctx_1024, L2_xattn_w_sim, L2_xattn_b_sim, L2_xattn_W_qv, L2_xattn_b_qv)
    x = x + _L2_ffn_ref(_layernorm(x, axis=-1), L2_ffn_ln1_w, L2_ffn_ln1_b, L2_ffn_ln2_w, L2_ffn_ln2_b, L2_ffn_Wqkv, L2_ffn_bqkv, L2_ffn_Wo, L2_ffn_bo, L2_ffn_gate_W, L2_ffn_fc1_w, L2_ffn_fc1_b, L2_ffn_fc2_w, L2_ffn_fc2_b)
    x = x + _L3_attn_ref(_layernorm(x, axis=-1), L3_attn_W_attn, L3_attn_b_attn, L3_attn_W_k2, L3_attn_b_k2, L3_attn_W_proj, L3_attn_b_proj)
    x = x + _L3_xattn_ref(_layernorm(x, axis=-1), ctx_1024, ctx_1024, L3_xattn_Wq, L3_xattn_bq, L3_xattn_Wk, L3_xattn_bk, L3_xattn_Wv, L3_xattn_bv, L3_xattn_Wo, L3_xattn_bo)
    x = x + _L3_ffn_ref(_layernorm(x, axis=-1), L3_ffn_shared_up, L3_ffn_shared_gate, L3_ffn_shared_down, L3_ffn_routed_up, L3_ffn_routed_gate, L3_ffn_routed_down, L3_ffn_router_w)
    return x

_drawn_inputs = setup_inputs


def setup_inputs(seed=0):
    import zlib

    import numpy as np

    out = dict(_drawn_inputs(seed))
    spreads = {'L0_attn_ln_w': (1.0, 0.2),
     'L0_attn_ln_b': (0.0, 0.1),
     'L0_attn_D': (1.0, 0.2),
     'L1_ffn_bias': (0.0, 0.1),
     'L2_ffn_ln1_w': (1.0, 0.6),
     'L2_ffn_ln1_b': (0.0, 0.615),
     'L2_ffn_ln2_w': (1.0, 0.2),
     'L2_ffn_ln2_b': (0.0, 0.1),
     'L2_ffn_bqkv': (0.0, 0.1),
     'L2_ffn_bo': (0.0, 0.1),
     'L2_ffn_fc1_b': (0.0, 0.526),
     'L2_ffn_fc2_b': (0.0, 0.372),
     'L3_attn_b_attn': (0.0, 0.8),
     'L3_attn_b_k2': (0.0, 2.0),
     'L3_attn_b_proj': (0.0, 0.1)}
    factors = {'L0_attn_conv_b': 7.308,
     'L0_attn_b_dt': 56.0,
     'L0_ffn_gate_weight': 6.438,
     'L0_ffn_w_gate': 4.151,
     'L0_ffn_w_up': 3.433,
     'L0_ffn_w_down': 4.318,
     'L0_ffn_ws_gate': 4.999,
     'L0_ffn_ws_up': 5.499,
     'L0_ffn_ws_down': 5.095,
     'L1_attn_qkv_w': 2.949,
     'L1_attn_qkv_b': 7.932,
     'L1_attn_proj_w': 3.102,
     'L1_attn_rel_pos_emb': 8.0,
     'L1_ffn_b1': 3.43,
     'L2_attn_wq': 8.0,
     'L2_attn_wk': 8.0,
     'L2_attn_wv': 2.953,
     'L2_attn_wo': 2.874,
     'L2_xattn_w_sim': 3.009,
     'L2_xattn_b_qv': 2.962,
     'L3_attn_W_attn': 8.0,
     'L3_attn_W_k2': 8.0,
     'L3_xattn_Wq': 8.0,
     'L3_xattn_bq': 64.0,
     'L3_xattn_Wk': 8.0,
     'L3_xattn_bk': 64.0,
     'L3_xattn_Wv': 5.544,
     'L3_xattn_bv': 8.0,
     'L3_xattn_Wo': 5.549,
     'L3_xattn_bo': 8.0,
     'L3_ffn_shared_up': 8.0,
     'L3_ffn_shared_gate': 8.0,
     'L3_ffn_shared_down': 8.0,
     'L3_ffn_routed_up': 8.0,
     'L3_ffn_routed_gate': 8.0,
     'L3_ffn_routed_down': 8.0,
     'L3_ffn_router_w': 8.0,
     'L0_attn_W_xproj': 8.0,
     'L0_attn_W_dt': 8.0}
    for name, (base, spread) in spreads.items():
        noise = np.random.default_rng([zlib.crc32(name.encode()), seed]).standard_normal(out[name].shape)
        drawn = base * np.exp(spread * noise) if base else spread * noise
        out[name] = jnp.asarray(drawn.astype(out[name].dtype))
    for name, factor in factors.items():
        out[name] = (out[name] * factor).astype(out[name].dtype)
    return out
```

```python
from contextlib import ExitStack

import numpy as np

import concourse.bass as bass
from concourse import mybir

F32 = mybir.dt.float32
BF16 = mybir.dt.bfloat16
U8 = mybir.dt.uint8
U32 = mybir.dt.uint32
ACT = mybir.ActivationFunctionType
ALU = mybir.AluOpType
AX = mybir.AxisListType

B, S, D = 8, 128, 128
T = B * S
HALF = 512
H, DH = 16, 8
HG = 4
NG = H // HG
EPS = 1e-5
NEG = -1.0e30
BIG = float(2 ** 30)
INNER, STATE, RANK, TAPS = 256, 64, 8, 4
IC = INNER // 128
FREQ = S // 2 + 1


class Steps:

    def __init__(self, sem):
        self.sem, self.n, self.i, self.k = sem, 0, None, 0

    def inc(self, instruction):
        instruction.then_inc(self.sem, 1)
        if self.i is None:
            self.n += 1
            return self.n
        self.k += 1
        return self.i * self.per + (self.n + self.k)

    def done(self, engine, instruction):
        engine.wait_ge(self.sem, self.inc(instruction))

    def enter(self, i, per):
        self.i, self.per, self.k = i, per, 0

    def leave(self, passes):
        assert self.k == self.per, (self.k, self.per)
        self.i = None
        self.n += passes * self.per


class Ring:

    def __init__(self, sem, depth, spare=0):
        self.sem, self.depth, self.spare = sem, depth, spare
        self.start = depth + spare

    def ended(self, n):
        return n + (self.start + 1)

    def free(self, n):
        return n + (self.spare + 1)


def layout(name_shapes):
    table, at = {}, 0
    for name, n in name_shapes:
        table[name] = (at, n)
        at += n
    return table, at


MAMBA = [("ident", 128), ("ln_w", 1), ("ln_b", 1), ("W_in", 2 * INNER), ("conv_w", IC * TAPS), ("conv_b", IC),
         ("W_xproj", IC * (RANK + 2 * STATE)), ("W_dt", INNER), ("b_dt", IC), ("A_log", IC * STATE), ("Dskip", IC),
         ("W_out", IC * D)]
SMALL = [("head_mask", H), ("neghalf", B), ("causal", S), ("strict", S), ("flip", S), ("causal_flip", S), ("row1", 1), ("iota16", 16), ("iota128", 128),
         ("rope0c", S), ("rope0s", S), ("rope2c", S), ("rope2s", S),
         ("L0x_q", D), ("L0x_qs", D), ("L0x_k", D), ("L0x_ks", D), ("L0x_v", D), ("L0x_o", D),
         ("L0f_router", 8), ("L0f_g", 640), ("L0f_u", 640), ("L0f_d", 640), ("L0f_sel", 512),
         ("L1a_q", D), ("L1a_k", D), ("L1a_v", D), ("L1a_o", D), ("L1a_bq", 1), ("L1a_bk", 1),
         ("L1x_w1", D), ("L1x_w2", D),
         ("L1f_router", 16), ("L1f_b2", D),
         ("L2a_q", D), ("L2a_qs", D), ("L2a_k", D), ("L2a_ks", D), ("L2a_v", D), ("L2a_o", D),
         ("L2x_w1", 1), ("L2x_w2", 1), ("L2x_w3", 1), ("L2x_wqv", 4 * D),
         ("L2n1_w", 1), ("L2n1_b", 1), ("L2n2_w", 1), ("L2n2_b", 1),
         ("L2f_q", D), ("L2f_k", D), ("L2f_v", D), ("L2f_o", D), ("L2f_bq", 1), ("L2f_bk", 1),
         ("L2f_router", 8), ("L2f_b2", D),
         ("L3a_q", D), ("L3a_k", D), ("L3a_k2", D), ("L3a_o", D), ("L3a_bq", 1), ("L3a_bk", 1), ("L3a_bk2", 1),
         ("L3x_q", D), ("L3x_k", D), ("L3x_v", D), ("L3x_o", D),
         ("dft_c", FREQ), ("dft_s", FREQ), ("inv_c", S), ("inv_s", S), ("invh_c", S), ("invh_s", S),
         ("L3f_router", 7)]
ROWS = [("L1a_bv", D), ("L1a_bo", D), ("L1x_b", D), ("L1f_bg", 16), ("L1f_bias", 16), ("L2x_b", D), ("L2x_bsim", 1),
        ("L2f_bv", D), ("L2f_bo", D), ("L3a_bo", D),
        ("L3x_bq", D), ("L3x_bk", D), ("L3x_bv", D), ("L3x_bo", D)]
MAMBA_AT, MAMBA_N = layout(MAMBA)
SMALL_AT, SMALL_N = layout(SMALL)
ROWS_AT, ROWS_N = layout(ROWS)


class Model:

    def __init__(self, nc, ctx, dram):
        self.nc, self.dram = nc, dram
        self.n_norm = self.n_attn = self.n_tail = self.n_moe = self.n_route = 0

        def sb(name, shape, dt=F32):
            return ctx.enter_context(nc.sbuf_tensor(name, shape, dt))

        def sem(name):
            return ctx.enter_context(nc.semaphore(name))

        self.X = sb("X", [S, B, D])
        self.XN = sb("XN", [S, B, D])
        self.XNT = sb("XNT", [D, T])
        self.CT = sb("CT", [D, T])
        self.CTOK = sb("CTOK", [S, B, D])
        self.O = sb("O", [S, B, D])
        self.mamba_pack = sb("mamba_pack", [128, MAMBA_N])
        self.small_pack = sb("small_pack", [128, SMALL_N])
        self.row_pack = sb("row_pack", [128, ROWS_N])
        self.ones = sb("ones", [128, 128])
        self.identb = sb("identb", [128, 128], BF16)
        self.causal4 = sb("causal4", [S, HG * S], BF16)
        self.strict4 = sb("strict4", [S, HG * S], BF16)
        self.loaded_x, self.loaded_mamba, self.loaded_rest = sem("loaded_x"), sem("loaded_mamba"), sem("loaded_rest")
        self.stored = sem("stored")
        self.pe_steps, self.act_steps = Steps(sem("pe_steps")), Steps(sem("act_steps"))
        self.dve_steps, self.pool_steps = Steps(sem("dve_steps")), Steps(sem("pool_steps"))
        self.stats_ready, self.rstd_ready = sem("stats_ready"), sem("rstd_ready")
        self.normed, self.turned = sem("normed"), sem("turned")
        self.kq = Ring(sem("kq_copied"), 2)
        self.scored = Ring(sem("scored"), 8)
        self.shifted = Ring(sem("shifted"), 4)
        self.exped = Ring(sem("exped"), 4)
        self.p_turned = Ring(sem("p_turned"), 4)
        self.pt_copied = Ring(sem("pt_copied"), 2)
        self.weighed = Ring(sem("weighed"), 2)
        self.out_done = Ring(sem("out_done"), 2)
        self.proj, self.evac = sem("proj"), sem("evac")
        self.n_proj = self.n_evac = 0
        self.w_loaded = [sem(f"w_loaded{e}") for e in range(2)]
        self.up_done = Ring(sem("up_done"), 2)
        self.act_done = Ring(sem("act_done"), 2)
        self.h_done = Ring(sem("h_done"), 2)
        self.y_done = Ring(sem("y_done"), 2, spare=1)
        self.added = Ring(sem("added"), 8)
        self.n_expert = self.n_unit = self.n_hunit = 0
        self.rings = {"pool": [self.kq], "tensor": [self.scored, self.p_turned, self.weighed, self.up_done, self.y_done],
                      "vector": [self.shifted, self.out_done, self.h_done, self.added],
                      "scalar": [self.exped, self.pt_copied, self.act_done]}
        self.sem = sem

    def w(self, name, rows=slice(0, 128)):
        for table, pack in ((MAMBA_AT, self.mamba_pack), (SMALL_AT, self.small_pack)):
            if name in table:
                at, n = table[name]
                return pack[rows, at:at + n]
        raise KeyError(name)

    def row(self, name):
        at, n = ROWS_AT[name]
        return self.row_pack[:, at:at + n]


def bcast_mid(ap, n):
    return ap.unsqueeze(1).to_broadcast([ap.shape[0], n, ap.shape[1]])


def bcast_last(ap, n):
    return ap.unsqueeze(2).to_broadcast([ap.shape[0], ap.shape[1], n])


def start_stage(nc, m):
    d = m.dram
    with nc.Block() as block:
        @block.sync
        def _(sp):
            sp.dma_start(m.X[:], d["x"]).then_inc(m.loaded_x, 16)
            sp.dma_start(m.mamba_pack[:], d["mamba"]).then_inc(m.loaded_mamba, 16)
            sp.dma_start(m.small_pack[:], d["small"]).then_inc(m.loaded_rest, 16)
            sp.dma_start(m.row_pack[:], d["rows"].to_broadcast([128, ROWS_N])).then_inc(m.loaded_rest, 16)
            sp.dma_start(m.CT[:], d["ctx_feat"]).then_inc(m.loaded_rest, 16)
            sp.dma_start(m.CTOK[:], d["ctx_tok"]).then_inc(m.loaded_rest, 16)

        @block.gpsimd
        def _(pool):
            for ring in m.rings["pool"]:
                pool.sem_inc(ring.sem, ring.start)
            nc.gpsimd.memset(m.ones[:], 1.0)

        @block.tensor
        def _(pe):
            for ring in m.rings["tensor"]:
                pe.sem_inc(ring.sem, ring.start)

        @block.scalar
        def _(act):
            for ring in m.rings["scalar"]:
                act.sem_inc(ring.sem, ring.start)

        @block.vector
        def _(dve):
            for ring in m.rings["vector"]:
                dve.sem_inc(ring.sem, ring.start)
            dve.wait_ge(m.loaded_x, 16)
            dve.wait_ge(m.loaded_mamba, 16)
            nc.vector.tensor_copy(m.identb[:], m.w("ident"))


def late_constants(nc, m):
    with nc.Block() as block:
        @block.vector
        def _(dve):
            dve.wait_ge(m.loaded_rest, 64)
            for tile, name in ((m.causal4, "causal"), (m.strict4, "strict")):
                nc.vector.tensor_copy(tile[:].rearrange("p (j k) -> p j k", j=HG), bcast_mid(m.w(name), HG))


def norm_stage(nc, m, src, dst, weight=None, bias=None):
    n = m.n_norm
    m.n_norm += 1
    with ExitStack() as ctx:
        stats = ctx.enter_context(nc.sbuf_tensor(f"stats{n}", [S, B, 6], F32))
        mv = ctx.enter_context(nc.sbuf_tensor(f"mv{n}", [S, B, 2], F32))
        ve = ctx.enter_context(nc.sbuf_tensor(f"ve{n}", [S, B], F32))
        rstd = ctx.enter_context(nc.sbuf_tensor(f"rstd{n}", [S, B], F32))
        ps = ctx.enter_context(nc.psum_tensor(f"norm_ps{n}", [D, T], F32))
        neghalf = ctx.enter_context(nc.sbuf_tensor(f"neghalf{n}", [S, B], F32))
        nh_steps = m.pool_steps
        block = ctx.enter_context(nc.Block())

        def copy_turned(engine, half):
            out, in_ = m.XNT[:, half * HALF:(half + 1) * HALF], ps[:, half * HALF:(half + 1) * HALF]
            if engine is nc.vector:
                if weight is None:
                    nc.vector.tensor_copy(out, in_)
                else:
                    nc.vector.tensor_scalar(out, in_, weight, bias, ALU.mult, ALU.add)
            elif weight is None:
                nc.scalar.activation(out, in_, ACT.Copy)
            else:
                nc.scalar.activation(out, in_, ACT.Identity, bias=bias, scale=weight)

        @block.vector
        def _(dve):
            for b in range(B):
                v = m.dve_steps.inc(nc.vector.bn_stats(stats[:, b, :], src[:, b, :]))
            dve.wait_ge(m.dve_steps.sem, v)
            for b in range(B):
                v = m.dve_steps.inc(nc.vector.bn_aggr(mv[:, b, :], stats[:, b, :]))
            dve.wait_ge(m.dve_steps.sem, v)
            nc.vector.tensor_scalar(ve[:], mv[:, :, 1], EPS, None, ALU.add).then_inc(m.stats_ready, 1)
            dve.wait_ge(m.rstd_ready, n + 1)
            for b in range(B):
                nc.vector.tensor_scalar(dst[:, b, :], src[:, b, :], mv[:, b, 0:1], rstd[:, b:b + 1],
                                        ALU.subtract, ALU.mult).then_inc(m.normed, 1)
            dve.wait_ge(m.turned, 2 * n + 1)
            copy_turned(nc.vector, 0)

        @block.gpsimd
        def _(pool):
            nh_steps.done(pool, nc.gpsimd.memset(neghalf[:], -0.5))
            pool.wait_ge(m.stats_ready, n + 1)
            nc.gpsimd.tensor_tensor(rstd[:], ve[:], neghalf[:], ALU.pow).then_inc(m.rstd_ready, 1)

        @block.tensor
        def _(pe):
            for b in range(B):
                pe.wait_ge(m.normed, n * B + b + 1)
                t = nc.tensor.transpose(ps[:, b * S:(b + 1) * S], dst[:, b, :], m.w("ident"))
                if b % 4 == 3:
                    t.then_inc(m.turned, 1)

        @block.scalar
        def _(act):
            act.wait_ge(m.turned, 2 * n + 2)
            copy_turned(nc.scalar, 1)


def project(nc, m, jobs):
    with ExitStack() as ctx:
        ps = [ctx.enter_context(nc.psum_tensor(f"proj_ps{m.n_proj}_{i}", [128, HALF], F32)) for i in range(4)]
        block = ctx.enter_context(nc.Block())
        base_p, base_e = m.n_proj, m.n_evac
        units = [(j, half) for j in range(len(jobs)) for half in range(T // HALF)]
        m.n_proj += len(units)
        m.n_evac += len(units)
        cols = lambda half: slice(half * HALF, (half + 1) * HALF)

        @block.tensor
        def _(pe):
            for u, (j, half) in enumerate(units):
                weights, sources = jobs[j][1:3]
                if u >= 4:
                    pe.wait_ge(m.evac, base_e + u - 3)
                for i, (w, s) in enumerate(zip(weights, sources)):
                    t = nc.tensor.matmul(ps[u % 4][0:w.shape[1], :], w, s[:, cols(half)], start=(i == 0),
                                         stop=(i == len(weights) - 1))
                t.then_inc(m.proj, 1)

        @block.scalar
        def _(act):
            for u, (j, half) in enumerate(units):
                out, weights, sources, bias, func = (*jobs[j], None)[:5]
                act.wait_ge(m.proj, base_p + u + 1)
                in_ = ps[u % 4][0:weights[0].shape[1], :]
                out = out(half) if callable(out) else out[:, cols(half)]
                if len(out.shape) == 3:
                    in_ = in_.rearrange("p (b s) -> p b s", b=out.shape[1])
                if bias is None:
                    c = nc.scalar.activation(out, in_, func or ACT.Copy)
                else:
                    c = nc.scalar.activation(out, in_, func or ACT.Identity, bias=bias)
                c.then_inc(m.evac, 1)


def rope(nc, m, parts):
    with nc.Block() as block:
        @block.vector
        def _(dve):
            for x, swapped, cos, sin in parts:
                xv, sv = (a.rearrange("p (b s) -> p b s", b=B) for a in (x, swapped))
                m.dve_steps.inc(nc.vector.tensor_tensor(xv, xv, bcast_mid(cos, B), ALU.mult))
                m.dve_steps.done(dve, nc.vector.tensor_tensor(sv, sv, bcast_mid(sin, B), ALU.mult))
                m.dve_steps.done(dve, nc.vector.tensor_tensor(x, x, swapped, ALU.add))


def values(nc, m, V, source, weight, bias_row=None):
    with ExitStack() as ctx:
        ps = ctx.enter_context(nc.psum_tensor(f"val_ps{m.n_proj}", [S, B, D], F32))
        block = ctx.enter_context(nc.Block())
        base = m.n_proj
        m.n_proj += 2

        @block.gpsimd
        def _(pool):
            nc.gpsimd.memset(V[:, :, :, DH:DH + 1], 1.0)

        @block.tensor
        def _(pe):
            for b in range(B):
                t = nc.tensor.matmul(ps[:, b, :], source[:, b * S:(b + 1) * S], weight, start=True, stop=True)
                if b % 4 == 3:
                    t.then_inc(m.proj, 1)

        @block.vector
        def _(dve):
            for b in range(B):
                if b % 4 == 0:
                    dve.wait_ge(m.proj, base + b // 4 + 1)
                out = V[:, b, :, 0:DH]
                in_ = ps[:, b, :].rearrange("p (h d) -> p h d", h=H)
                if bias_row is None:
                    nc.vector.tensor_copy(out, in_)
                else:
                    nc.vector.tensor_tensor(out, in_, bias_row.rearrange("p (h d) -> p h d", h=H), ALU.add)


def attend(nc, m, QT, KT, V, O, mask=None, bias=None, token_masks=None):
    call = m.n_attn
    m.n_attn += 1
    U0, B0 = call * B * NG, call * B
    scale = float(DH) ** -0.5
    with ExitStack() as ctx:
        sb = lambda name, shape, dt=F32: ctx.enter_context(nc.sbuf_tensor(f"{name}_a{call}", shape, dt))
        Qs = [sb(f"Qs{i}", [D, S]) for i in range(2)]
        KH = [sb(f"KH{i}", [D, H, S]) for i in range(2)]
        shifted = [sb(f"shifted{i}", [S, HG, S]) for i in range(4)]
        PTs = [sb(f"PTs{i}", [S, HG, S]) for i in range(2)]
        nmax = sb("nmax", [S, 2, HG])
        rsum = sb("rsum", [S, 2, H])
        scores = [ctx.enter_context(nc.psum_tensor(f"scores{call}_{i}", [S, HG, S], F32)) for i in range(4)]
        PT = [ctx.enter_context(nc.psum_tensor(f"PT{call}_{i}", [S, HG, S], F32)) for i in range(2)]
        PO = ctx.enter_context(nc.psum_tensor(f"PO{call}", [S, 2, HALF], F32))
        block = ctx.enter_context(nc.Block())
        ident = m.w("ident")
        SC = 2 * NG
        LAST = B // 2 - 1

        def passes(engine, body):
            with engine.Fori(0, LAST) as i:
                body(i, None)
            body(LAST, SC)

        def within(u, limit):
            return limit is None or u < limit

        @block.gpsimd
        def _(pool):
            with pool.Fori(0, B // 2) as i:
                for lane in range(2):
                    pool.wait_ge(m.scored.sem, i * SC + (U0 + NG * lane + NG))
                    at = bass.ds(i * (2 * S) + lane * S, S)
                    nc.gpsimd.tensor_copy(Qs[lane][:], QT[:, at]).then_inc(m.kq.sem, 1)
                    for g in range(NG):
                        heads = slice(g * HG, (g + 1) * HG)
                        nc.gpsimd.tensor_tensor(KH[lane][:, heads, :], bcast_mid(KT[:, at], HG),
                                                bcast_last(m.w("head_mask")[:, heads], S),
                                                ALU.mult).then_inc(m.kq.sem, 1)

        @block.tensor
        def _(pe):
            def score(i, u):
                lane, g = u // NG % 2, u % NG
                n = i * SC + (U0 + u)
                pe.wait_ge(m.kq.sem, i * (2 * (NG + 1)) + ((B0 + u // NG) * (NG + 1) + g + 2 + m.kq.depth))
                pe.wait_ge(m.shifted.sem, m.shifted.free(n))
                more = mask is not None or bias is not None or token_masks is not None
                t = nc.tensor.matmul(scores[u % 4][:], Qs[lane][:], KH[lane][:, g * HG:(g + 1) * HG, :],
                                     start=True, stop=not more)
                if mask is not None:
                    t = nc.tensor.matmul(scores[u % 4][:], m.identb[:], mask, start=False, stop=True)
                if bias is not None:
                    t = nc.tensor.matmul(scores[u % 4][:], m.w("flip"), bias[:, g * HG:(g + 1) * HG, :],
                                         start=False, stop=True)
                if token_masks is not None:
                    qm, km = token_masks
                    at = bass.ds(i * (2 * S) + u // NG * S, S)
                    t = nc.tensor.matmul(scores[u % 4][:], qm[:, at], bcast_mid(km[:, at], HG),
                                         start=False, stop=True)
                t.then_inc(m.scored.sem, 1)

            def turn(i, u):
                n = i * SC + (U0 + u)
                pe.wait_ge(m.exped.sem, m.exped.ended(n))
                pe.wait_ge(m.pt_copied.sem, m.pt_copied.free(n))
                for j in range(HG):
                    t = nc.tensor.transpose(PT[u % 2][:, j, :], shifted[u % 4][:, j, :], ident)
                t.then_inc(m.p_turned.sem, 1)

            def weigh(i, u):
                lane, g = u // NG, u % NG
                n = i * SC + (U0 + u)
                if g == 0:
                    pe.wait_ge(m.out_done.sem, m.out_done.free(i * 2 + (B0 + lane)))
                pe.wait_ge(m.pt_copied.sem, m.pt_copied.ended(n))
                for j in range(HG):
                    h = g * HG + j
                    t = nc.tensor.matmul(PO[:, lane, h * (DH + 1):(h + 1) * (DH + 1)], PTs[u % 2][:, j, :],
                                         V[:, bass.ds(i * 2 + lane, 1), h, :].squeeze(1), start=True, stop=True)
                t.then_inc(m.weighed.sem, 1)

            def body(i, limit):
                for u in range(SC):
                    if within(u + 3, limit):
                        score(i, u + 3)
                    if within(u + 1, limit):
                        turn(i, u + 1)
                    weigh(i, u)

            for u in range(3):
                score(0, u)
            turn(0, 0)
            passes(pe, body)

        @block.vector
        def _(dve):
            def shift(i, u):
                n = i * SC + (U0 + u)
                dve.wait_ge(m.scored.sem, m.scored.ended(n))
                m.dve_steps.done(dve, nc.vector.tensor_reduce(nmax[:, u % 2, :], scores[u % 4][:], AX.X, ALU.max))
                dve.wait_ge(m.p_turned.sem, m.p_turned.free(n))
                nc.vector.tensor_tensor(shifted[u % 4][:], scores[u % 4][:], bcast_last(nmax[:, u % 2, :], S),
                                        ALU.subtract).then_inc(m.shifted.sem, 1)

            def normalise(i, lane):
                n = i * SC + (U0 + NG * lane + NG - 1)
                dve.wait_ge(m.weighed.sem, m.weighed.ended(n))
                po = PO[:, lane, 0:H * (DH + 1)].rearrange("p (h e) -> p h e", h=H)
                m.dve_steps.done(dve, nc.vector.reciprocal(rsum[:, lane, :], po[:, :, DH]))
                nc.vector.tensor_tensor(
                    O[:, bass.ds(i * 2 + lane, 1), :].squeeze(1).rearrange("p (h d) -> p h d", h=H),
                    po[:, :, 0:DH], bcast_last(rsum[:, lane, :], DH), ALU.mult).then_inc(m.out_done.sem, 1)

            def body(i, limit):
                for u in range(SC):
                    if within(u + NG, limit):
                        shift(i, u + NG)
                    if u % NG == NG - 1:
                        normalise(i, u // NG)

            for u in range(NG):
                shift(0, u)
            with dve.Fori(0, LAST) as i:
                m.dve_steps.enter(i, SC + 2)
                body(i, None)
                m.dve_steps.leave(LAST)
            body(LAST, SC)

        @block.scalar
        def _(act):
            def exp(i, u):
                n = i * SC + (U0 + u)
                act.wait_ge(m.shifted.sem, m.shifted.ended(n))
                nc.scalar.activation(shifted[u % 4][:], shifted[u % 4][:], ACT.Exp,
                                     scale=scale).then_inc(m.exped.sem, 1)

            def copy(i, u):
                n = i * SC + (U0 + u)
                act.wait_ge(m.p_turned.sem, m.p_turned.ended(n))
                act.wait_ge(m.weighed.sem, m.weighed.free(n))
                nc.scalar.activation(PTs[u % 2][:], PT[u % 2][:], ACT.Copy).then_inc(m.pt_copied.sem, 1)

            def body(i, limit):
                for u in range(SC):
                    if within(u + 2, limit):
                        exp(i, u + 2)
                    copy(i, u)

            for u in range(2):
                exp(0, u)
            passes(act, body)


def out_project(nc, m, O, weight, bias_row=None, bias_times=1.0, target=None):
    Y = m.X if target is None else target
    n = m.n_tail
    m.n_tail += 1
    with ExitStack() as ctx:
        OT = ctx.enter_context(nc.sbuf_tensor(f"OT{n}", [D, T], F32))
        ps = ctx.enter_context(nc.psum_tensor(f"tail_t{n}", [D, T], F32))
        py = ctx.enter_context(nc.psum_tensor(f"tail_y{n}", [S, B, D], F32))
        block = ctx.enter_context(nc.Block())
        base_p, base_e = m.n_proj, m.n_evac
        m.n_proj += 4
        m.n_evac += 2
        halves = [slice(0, HALF), slice(HALF, T)]

        @block.tensor
        def _(pe):
            for b in range(B):
                t = nc.tensor.transpose(ps[:, b * S:(b + 1) * S], O[:, b, :], m.w("ident"))
                if b % 4 == 3:
                    t.then_inc(m.proj, 1)
            for b in range(B):
                if b % 4 == 0:
                    pe.wait_ge(m.evac, base_e + b // 4 + 1)
                t = nc.tensor.matmul(py[:, b, :], OT[:, b * S:(b + 1) * S], weight, start=True, stop=True)
                if b % 4 == 3:
                    t.then_inc(m.proj, 1)

        @block.scalar
        def _(act):
            for half in range(2):
                act.wait_ge(m.proj, base_p + half + 1)
                nc.scalar.activation(OT[:, halves[half]], ps[:, halves[half]], ACT.Copy).then_inc(m.evac, 1)

        @block.vector
        def _(dve):
            if bias_row is not None:
                m.dve_steps.done(dve, nc.vector.scalar_tensor_tensor(
                    out=Y[:], in0=bcast_mid(bias_row, B), scalar=bias_times, in1=Y[:], op0=ALU.mult, op1=ALU.add))
            for half in range(2):
                dve.wait_ge(m.proj, base_p + 3 + half)
                bs = slice(4 * half, 4 * half + 4)
                nc.vector.tensor_tensor(Y[:, bs, :], Y[:, bs, :], py[:, bs, :], ALU.add)


def add_products(nc, m, terms, extra=None, bias_row=None):
    with ExitStack() as ctx:
        py = ctx.enter_context(nc.psum_tensor(f"sum_y{m.n_proj}", [S, B, D], F32))
        block = ctx.enter_context(nc.Block())
        base = m.n_proj
        m.n_proj += 2

        @block.tensor
        def _(pe):
            for b in range(B):
                for k, (source, w) in enumerate(terms):
                    t = nc.tensor.matmul(py[:, b, :], source(b), w, start=(k == 0), stop=(k == len(terms) - 1))
                if b % 4 == 3:
                    t.then_inc(m.proj, 1)

        @block.vector
        def _(dve):
            if extra is not None:
                m.dve_steps.done(dve, nc.vector.tensor_tensor(m.X[:], m.X[:], extra, ALU.add))
            if bias_row is not None:
                m.dve_steps.done(dve, nc.vector.tensor_tensor(m.X[:], m.X[:], bcast_mid(bias_row, B), ALU.add))
            for half in range(2):
                dve.wait_ge(m.proj, base + half + 1)
                bs = slice(4 * half, 4 * half + 4)
                nc.vector.tensor_tensor(m.X[:, bs, :], m.X[:, bs, :], py[:, bs, :], ALU.add)


def mamba_stage(nc, m):
    norm_stage(nc, m, m.X, m.XN)
    norm_stage(nc, m, m.XN, m.O, m.w("ln_w"), m.w("ln_b"))
    with ExitStack() as outer:
        sb = lambda name, shape, dt=F32: outer.enter_context(nc.sbuf_tensor(name, shape, dt))
        u = sb("u", [128, IC, T])
        gate = sb("gate", [128, IC, T])
        delta = sb("delta", [128, IC, T])
        du = sb("du", [128, IC, T])
        A = sb("A", [128, IC, STATE])
        BC = [sb(f"BC{i}", [2 * STATE, T], BF16) for i in range(3)]
        y = sb("y", [128, IC, T])

        with ExitStack() as ctx:
            pre = lambda name, shape, dt=F32: ctx.enter_context(nc.sbuf_tensor(name, shape, dt))
            padded = [pre(f"padded{c}", [128, B, S + TAPS - 1]) for c in range(IC)]
            conv = pre("conv", [128, IC, T])
            BCf = pre("BCf", [2 * STATE, T])
            dt_low = pre("dt_low", [RANK, T])
            conv_w = m.w("conv_w").rearrange("p (c k) -> p c k", c=IC)
            with nc.Block() as block:
                @block.gpsimd
                def _(pool):
                    for c in range(IC):
                        nc.gpsimd.memset(padded[c][:, :, 0:TAPS - 1], 0.0)
            W_in = m.w("W_in")
            jobs = [((lambda half, c=c: padded[c][:, 4 * half:4 * half + 4, TAPS - 1:]),
                     [W_in[:, c * 128:(c + 1) * 128]], [m.XNT[:]], None) for c in range(IC)]
            jobs += [(gate[:, c, :], [W_in[:, INNER + c * 128:INNER + (c + 1) * 128]], [m.XNT[:]], None, ACT.Silu)
                     for c in range(IC)]
            project(nc, m, jobs)

            with nc.Block() as block:
                @block.vector
                def _(dve):
                    for k in range(TAPS):
                        for c in range(IC):
                            out = conv[:, c, :].rearrange("p (b s) -> p b s", b=B)
                            tap = padded[c][:, :, k:k + S]
                            if k == 0:
                                t = nc.vector.tensor_scalar(out, tap, conv_w[:, c, 0:1], m.w("conv_b")[:, c:c + 1],
                                                            ALU.mult, ALU.add)
                            else:
                                t = nc.vector.scalar_tensor_tensor(out=out, in0=tap, scalar=conv_w[:, c, k:k + 1],
                                                                   in1=out, op0=ALU.mult, op1=ALU.add)
                            v = m.dve_steps.inc(t)
                        dve.wait_ge(m.dve_steps.sem, v)
                v_conv = m.dve_steps.n

                @block.scalar
                def _(act):
                    act.wait_ge(m.dve_steps.sem, v_conv)
                    nc.scalar.activation(u[:], conv[:], ACT.Silu)

            W_x = m.w("W_xproj").rearrange("p (c n) -> p c n", c=IC)
            project(nc, m, [(dt_low[:], [W_x[:, c, 0:RANK] for c in range(IC)], [u[:, c, :] for c in range(IC)], None),
                            (BCf[:], [W_x[:, c, RANK:] for c in range(IC)], [u[:, c, :] for c in range(IC)], None)])
            W_dt = m.w("W_dt", slice(0, RANK))
            project(nc, m, [(delta[:, c, :], [W_dt[:, c * 128:(c + 1) * 128]], [dt_low[:]], m.w("b_dt")[:, c:c + 1])
                            for c in range(IC)])
            softplus_and_split(nc, m, delta, u, du, A, BC, BCf, ctx)
        scan_block(nc, m, outer, delta, du, A, BC, y)

        with nc.Block() as block:
            @block.vector
            def _(dve):
                for c in range(IC):
                    v = m.dve_steps.inc(nc.vector.scalar_tensor_tensor(
                        out=y[:, c, :], in0=u[:, c, :], scalar=m.w("Dskip")[:, c:c + 1], in1=y[:, c, :],
                        op0=ALU.mult, op1=ALU.add))
                dve.wait_ge(m.dve_steps.sem, v)
                nc.vector.tensor_tensor(y[:], y[:], gate[:], ALU.mult)
        W_out = m.w("W_out").rearrange("p (c n) -> p c n", c=IC)
        add_products(nc, m, [((lambda b, c=c: y[:, c, b * S:(b + 1) * S]), W_out[:, c, :]) for c in range(IC)],
                     extra=m.XN[:])


def softplus_and_split(nc, m, delta, u, du, A, BC, BCf, ctx):
    pre = lambda name, shape, dt=F32: ctx.enter_context(nc.sbuf_tensor(name, shape, dt))
    low, e, w, ln_w = (pre(name, [128, IC, T]) for name in ("low", "e", "w", "ln_w_"))
    rest = pre("rest", [2 * STATE, T])
    e_ready, w_ready, ln_ready = m.sem("e_ready"), m.sem("w_ready"), m.sem("ln_ready")
    low_ready = m.sem("low_ready")
    with nc.Block() as block:
        @block.vector
        def _(dve):
            steps = m.dve_steps
            nc.vector.scalar_tensor_tensor(out=low[:], in0=delta[:], scalar=-1.0, in1=delta[:], op0=ALU.mult,
                                           op1=ALU.min).then_inc(low_ready, 1)
            steps.done(dve, nc.vector.tensor_copy(BC[0][:], BCf[:]))
            steps.done(dve, nc.vector.tensor_tensor(rest[:], BCf[:], BC[0][:], ALU.subtract))
            steps.done(dve, nc.vector.tensor_copy(BC[1][:], rest[:]))
            steps.done(dve, nc.vector.tensor_tensor(rest[:], rest[:], BC[1][:], ALU.subtract))
            steps.done(dve, nc.vector.tensor_copy(BC[2][:], rest[:]))
            dve.wait_ge(e_ready, 1)
            nc.vector.tensor_scalar(w[:], e[:], 1.0, None, ALU.add).then_inc(w_ready, 1)
            dve.wait_ge(w_ready, 1)
            steps.done(dve, nc.vector.scalar_tensor_tensor(out=low[:], in0=w[:], scalar=-1.0, in1=e[:], op0=ALU.add,
                                                           op1=ALU.subtract))
            dve.wait_ge(ln_ready, 1)
            steps.done(dve, nc.vector.tensor_tensor(low[:], ln_w[:], low[:], ALU.subtract))
            steps.done(dve, nc.vector.scalar_tensor_tensor(out=delta[:], in0=delta[:], scalar=0.0, in1=low[:],
                                                           op0=ALU.max, op1=ALU.add))
            nc.vector.tensor_tensor(du[:], delta[:], u[:], ALU.mult)

        @block.scalar
        def _(act):
            steps = m.act_steps
            a = A[:].rearrange("p c n -> p (c n)")
            steps.done(act, nc.scalar.activation(a, m.w("A_log"), ACT.Exp))
            nc.scalar.activation(a, a, ACT.Copy, scale=-1.0)
            act.wait_ge(low_ready, 1)
            nc.scalar.activation(e[:], low[:], ACT.Exp).then_inc(e_ready, 1)
            act.wait_ge(w_ready, 1)
            nc.scalar.activation(ln_w[:], w[:], ACT.Ln).then_inc(ln_ready, 1)


def scan_block(nc, m, outer, delta, du, A, BC, y):
    sb = lambda name, shape, dt=F32: outer.enter_context(nc.sbuf_tensor(name, shape, dt))
    decay = [[sb(f"decay{c}{p}", [128, B, S]) for p in range(2)] for c in range(IC)]
    inp = [sb(f"inp{c}", [128, T]) for c in range(IC)]
    h = [[sb(f"h{c}{p}", [128, T]) for p in range(2)] for c in range(IC)]
    hC = [[sb(f"hC{c}{p}", [128, T]) for p in range(2)] for c in range(IC)]
    Cs = [sb(f"Cs{p}", [128, T]) for p in range(2)]
    ps_ctx = ExitStack()
    Bp = [ps_ctx.enter_context(nc.psum_tensor(f"Bp{p}", [128, T], F32)) for p in range(2)]
    Cp = ps_ctx.enter_context(nc.psum_tensor("Cp", [128, T], F32))
    Y1 = ps_ctx.enter_context(nc.psum_tensor("Y1", [128, T], F32))
    spread_b, spread_c = Ring(m.sem("spread_b"), 2), Ring(m.sem("spread_c"), 1)
    c_copied, decayed = Ring(m.sem("c_copied"), 2), Ring(m.sem("decayed"), 4)
    fed, scanned, weighed = Ring(m.sem("fed"), 4), Ring(m.sem("scanned"), 4), Ring(m.sem("c_weighed"), 4)
    summed0, summed1 = Ring(m.sem("summed0"), 2), Ring(m.sem("summed1"), 2)
    halves = [slice(0, HALF), slice(HALF, T)]
    with nc.Block() as block:
        @block.gpsimd
        def _(pool):
            for ring in (weighed,):
                pool.sem_inc(ring.sem, ring.start)
            for c in range(IC):
                for p in range(2):
                    nc.gpsimd.memset(decay[c][p][:], 0.0)
                nc.gpsimd.memset(hC[c][1][:], 0.0)
            nc.gpsimd.memset(y[:, 0, :], 0.0)

        @block.tensor
        def _(pe):
            for ring in (spread_b, spread_c):
                pe.sem_inc(ring.sem, ring.start)
            pe.sem_inc(summed1.sem, summed1.depth - 1)

        @block.scalar
        def _(act):
            for ring in (c_copied, decayed):
                act.sem_inc(ring.sem, ring.start)

        @block.vector
        def _(dve):
            for ring in (fed, scanned):
                dve.sem_inc(ring.sem, ring.start)
            dve.sem_inc(summed0.sem, summed0.depth - 1)

    with nc.Block() as block:
        @block.tensor
        def _(pe):
            def spread(out, row):
                for half in range(2):
                    for part in range(3):
                        t = nc.tensor.matmul(out[:, halves[half]], m.identb[:, bass.ds(row, 1)].to_broadcast([128, 128]),
                                             BC[part][:, halves[half]], start=(part == 0), stop=(part == 2))
                return t

            def add(p, start=False, stop=False):
                for half in range(2):
                    t = nc.tensor.matmul(Y1[:, halves[half]], m.w("ident"), hC[1][p][:, halves[half]],
                                         start=start, stop=stop, skip_group_check=True)
                return t

            add(1, start=True)
            with pe.Fori(0, STATE // 2) as i:
                for p in range(2):
                    n = i * 2 + p
                    pe.wait_ge(fed.sem, i * 4 + (2 * p + 2))
                    spread(Bp[p], n).then_inc(spread_b.sem, 1)
                    pe.wait_ge(c_copied.sem, n + 2)
                    spread(Cp, n + STATE).then_inc(spread_c.sem, 1)
                    pe.wait_ge(weighed.sem, i * 4 + (2 * p + weighed.depth))
                    add(1 - p).then_inc(summed1.sem, 1)
            pe.wait_ge(weighed.sem, 2 * STATE + weighed.depth)
            add(1, stop=True).then_inc(summed1.sem, 1)

        @block.scalar
        def _(act):
            with act.Fori(0, STATE // 2) as i:
                for p in range(2):
                    n = i * 2 + p
                    for c in range(IC):
                        use = i * 4 + (2 * p + c)
                        act.wait_ge(scanned.sem, scanned.free(use))
                        nc.scalar.activation(
                            decay[c][p][:, :, 1:S], delta[:, c, :].rearrange("p (b s) -> p b s", b=B)[:, :, 1:S],
                            ACT.Exp, scale=A[:, c, bass.ds(n, 1)]).then_inc(decayed.sem, 1)
                        if c == 0:
                            act.wait_ge(spread_c.sem, spread_c.ended(n))
                            act.wait_ge(weighed.sem, i * 4 + (2 * p + 2))
                            nc.scalar.activation(Cs[p][:], Cp[:], ACT.Copy).then_inc(c_copied.sem, 1)

        @block.vector
        def _(dve):
            with dve.Fori(0, STATE // 2) as i:
                m.dve_steps.enter(i, 0)
                for p in range(2):
                    n = i * 2 + p
                    dve.wait_ge(spread_b.sem, spread_b.ended(n))
                    for c in range(IC):
                        use = i * 4 + (2 * p + c)
                        dve.wait_ge(scanned.sem, scanned.ended(use) - 2)
                        nc.vector.tensor_tensor(inp[c][:], du[:, c, :], Bp[p][:], ALU.mult).then_inc(fed.sem, 1)
                    for c in range(IC):
                        use = i * 4 + (2 * p + c)
                        dve.wait_ge(fed.sem, fed.ended(use))
                        dve.wait_ge(decayed.sem, decayed.ended(use))
                        dve.wait_ge(weighed.sem, weighed.free(use))
                        nc.vector.tensor_tensor_scan(
                            h[c][p][:], decay[c][p][:].rearrange("p b s -> p (b s)"), inp[c][:], 0.0,
                            ALU.mult, ALU.add).then_inc(scanned.sem, 1)
                        if c == 0:
                            dve.wait_ge(weighed.sem, i * 4 + (2 * p - 1 + weighed.depth))
                            dve.wait_ge(summed0.sem, n + 1)
                            nc.vector.tensor_tensor(y[:, 0, :], y[:, 0, :], hC[0][1 - p][:],
                                                    ALU.add).then_inc(summed0.sem, 1)
                m.dve_steps.leave(STATE // 2)
            dve.wait_ge(weighed.sem, 2 * STATE - 1 + weighed.depth)
            dve.wait_ge(summed0.sem, STATE + 1)
            nc.vector.tensor_tensor(y[:, 0, :], y[:, 0, :], hC[0][1][:], ALU.add)
            dve.wait_ge(summed1.sem, STATE + 2)
            nc.vector.tensor_copy(y[:, 1, :], Y1[:])

        @block.gpsimd
        def _(pool):
            with pool.Fori(0, STATE // 2) as i:
                for p in range(2):
                    n = i * 2 + p
                    pool.wait_ge(c_copied.sem, c_copied.ended(n))
                    for c in range(IC):
                        use = i * 4 + (2 * p + c)
                        pool.wait_ge(scanned.sem, scanned.ended(use))
                        summed = (summed0, summed1)[c]
                        pool.wait_ge(summed.sem, summed.free(n))
                        nc.gpsimd.tensor_tensor(hC[c][p][:], h[c][p][:], Cs[p][:], ALU.mult).then_inc(weighed.sem, 1)
    ps_ctx.close()


def route(nc, m, E, weight, kind, comb, combT=None, rows=()):
    n = m.n_route
    m.n_route += 1
    EP = 16 if E > 8 else 8
    with ExitStack() as ctx:
        sb = lambda name, shape, dt=F32: ctx.enter_context(nc.sbuf_tensor(f"{name}_r{n}", shape, dt))
        val, eq = sb("val", [S, B, EP]), sb("eq", [S, B, EP])
        best, index = sb("best", [S, B, 8]), sb("index", [S, B, 8], U32)
        indexf, wt, tmp = sb("indexf", [S, B, 2]), sb("wt", [S, B, 2]), sb("tmp", [S, B])
        ps = ctx.enter_context(nc.psum_tensor(f"logits{n}", [S, B, EP], F32))
        psT = ctx.enter_context(nc.psum_tensor(f"combT_ps{n}", [16, T], F32))
        block = ctx.enter_context(nc.Block())
        base_p, base_e = m.n_proj, m.n_evac
        m.n_proj += 1 if combT is None else 3
        m.n_evac += 4
        v = {}

        @block.vector
        def _(dve):
            steps = m.dve_steps
            dve.wait_ge(m.proj, base_p + 1)
            if kind == "sigmoid":
                dve.wait_ge(m.evac, base_e + 1)
                steps.done(dve, nc.vector.tensor_scalar(val[:], val[:], 1.0, None, ALU.add))
                steps.done(dve, nc.vector.reciprocal(val[:], val[:]))
            elif kind == "softmax_all":
                steps.done(dve, nc.vector.memset(val[:], -1.0))
                steps.done(dve, nc.vector.tensor_reduce(tmp[:], ps[:, :, 0:E], AX.X, ALU.max))
                v["shifted"] = steps.inc(nc.vector.tensor_tensor(val[:, :, 0:E], ps[:, :, 0:E], bcast_last(tmp[:], E),
                                                                 ALU.subtract))
                dve.wait_ge(m.evac, base_e + 1)
                steps.done(dve, nc.vector.tensor_reduce(tmp[:], val[:, :, 0:E], AX.X, ALU.add))
                steps.done(dve, nc.vector.reciprocal(tmp[:], tmp[:]))
                steps.done(dve, nc.vector.tensor_tensor(val[:, :, 0:E], val[:, :, 0:E], bcast_last(tmp[:], E),
                                                        ALU.mult))
            else:
                steps.done(dve, nc.vector.tensor_copy(val[:], ps[:]))
                for row in rows:
                    steps.done(dve, nc.vector.tensor_tensor(val[:], val[:], bcast_mid(row, B), ALU.add))
            for b in range(B):
                k = steps.inc(nc.vector.max(best[:, b, :], val[:, b, :]))
            dve.wait_ge(steps.sem, k)
            for b in range(B):
                k = steps.inc(nc.vector.max_index(index[:, b, :], best[:, b, :], val[:, b, :]))
            dve.wait_ge(steps.sem, k)
            steps.done(dve, nc.vector.tensor_copy(indexf[:], index[:, :, 0:2]))
            if kind in ("sigmoid", "softmax_all"):
                eps, times = (1e-20, 2.5) if kind == "sigmoid" else (1e-9, 1.0)
                steps.done(dve, nc.vector.scalar_tensor_tensor(out=tmp[:], in0=best[:, :, 0], scalar=eps,
                                                               in1=best[:, :, 1], op0=ALU.add, op1=ALU.add))
                steps.done(dve, nc.vector.reciprocal(tmp[:], tmp[:]))
                for k in range(2):
                    steps.done(dve, nc.vector.scalar_tensor_tensor(
                        out=wt[:, :, k], in0=best[:, :, k], scalar=times, in1=tmp[:], op0=ALU.mult, op1=ALU.mult))
            else:
                v["second"] = steps.inc(nc.vector.tensor_tensor(tmp[:], best[:, :, 1], best[:, :, 0], ALU.subtract))
                dve.wait_ge(m.evac, base_e + 1)
                steps.done(dve, nc.vector.tensor_scalar(wt[:, :, 0], tmp[:], 1.0, None, ALU.add))
                steps.done(dve, nc.vector.reciprocal(wt[:, :, 0], wt[:, :, 0]))
                steps.done(dve, nc.vector.tensor_tensor(wt[:, :, 1], wt[:, :, 0], tmp[:], ALU.mult))
            for k in range(2):
                out = comb if k == 0 else eq[:]
                steps.done(dve, nc.vector.tensor_tensor(out, bcast_mid(m.w("iota16")[:, 0:EP], B),
                                                        bcast_last(indexf[:, :, k], EP), ALU.is_equal))
                steps.done(dve, nc.vector.tensor_tensor(out, out, bcast_last(wt[:, :, k], EP), ALU.mult))
            steps.done(dve, nc.vector.tensor_tensor(comb, comb, eq[:], ALU.add))
            v["comb"] = steps.n
            if combT is not None:
                dve.wait_ge(m.proj, base_p + 2)
                steps.inc(nc.vector.tensor_copy(combT, psT[0:EP, :]))
            if kind == "softmax_all":
                steps.done(dve, nc.vector.memset(comb[:, :, E:E + 1], 1.0))

        @block.tensor
        def _(pe):
            for b in range(B):
                t = nc.tensor.matmul(ps[:, b, 0:E], m.XNT[:, b * S:(b + 1) * S], weight, start=True, stop=True)
            t.then_inc(m.proj, 1)
            if combT is not None:
                pe.wait_ge(m.dve_steps.sem, v["comb"])
                for b in range(B):
                    t = nc.tensor.transpose(psT[0:EP, b * S:(b + 1) * S], comb[:, b, :], m.w("ident"))
                t.then_inc(m.proj, 2)

        @block.scalar
        def _(act):
            if kind == "sigmoid":
                act.wait_ge(m.proj, base_p + 1)
                t = nc.scalar.activation(val[:], ps[:], ACT.Exp, scale=-1.0)
            elif kind == "softmax_all":
                act.wait_ge(m.dve_steps.sem, v["shifted"])
                t = nc.scalar.activation(val[:, :, 0:E], val[:, :, 0:E], ACT.Exp)
            else:
                act.wait_ge(m.dve_steps.sem, v["second"])
                t = nc.scalar.activation(tmp[:], tmp[:], ACT.Exp)
            t.then_inc(m.evac, 4)


def experts(nc, m, E, FC, weights, func, comb, gated=False):
    E0, S0, U0, H0 = m.n_expert, 2 * m.n_expert, m.n_unit, m.n_hunit
    m.n_expert += E
    m.n_unit += 2 * E * FC
    m.n_hunit += 2 * E * FC if gated else 0
    call = m.n_moe
    m.n_moe += 1
    F = FC * 128
    down = 2 * F if gated else F
    with ExitStack() as ctx:
        sb = lambda name, shape, dt=F32: ctx.enter_context(nc.sbuf_tensor(f"{name}_e{call}", shape, dt))
        W = [sb(f"W{i}", [128, down + F + (0 if gated else FC)]) for i in range(2)]
        hid = [sb(f"hid{i}", [128, FC, HALF]) for i in range(2)]
        silu = [sb(f"silu{i}", [128, HALF]) for i in range(2)]
        G = [ctx.enter_context(nc.psum_tensor(f"G{call}_{i}", [128, HALF], F32)) for i in range(2)]
        U = [ctx.enter_context(nc.psum_tensor(f"U{call}_{i}", [128, HALF], F32)) for i in range(2)] if gated else G
        Y = [ctx.enter_context(nc.psum_tensor(f"Y{call}_{i}", [S, B // 2, D], F32)) for i in range(2)]
        block = ctx.enter_context(nc.Block())
        unit = lambda i, s, fc: i * (4 * FC) + (s * FC + fc)
        order = [("up", 0), ("up", 1), ("down", 0), ("up", 2), ("down", 1), ("up", 3), ("down", 2), ("down", 3)]

        @block.sync
        def _(sp):
            with sp.Fori(0, E // 2) as i:
                for e in range(2):
                    sp.wait_ge(m.y_done.sem, i * 4 + m.y_done.ended(S0 + 2 * e - 3))
                    sp.dma_start(W[e][:], weights[bass.ds(i * 2 + e, 1)].squeeze(0)).then_inc(m.w_loaded[e], 16)

        @block.tensor
        def _(pe):
            with pe.Fori(0, E // 2) as i:
                def up(s):
                    e, half = s // 2, s % 2
                    if half == 0:
                        pe.wait_ge(m.w_loaded[e], i * 16 + 16 * (E0 // 2 + 1))
                    for fc in range(FC):
                        u = unit(i, s, fc)
                        pe.wait_ge(m.act_done.sem, m.act_done.free(u + U0))
                        at = slice(fc * 128, (fc + 1) * 128)
                        cols = slice(half * HALF, (half + 1) * HALF)
                        t = nc.tensor.matmul(G[fc % 2][:], W[e][:, at], m.XNT[:, cols], start=True, stop=True)
                        if gated:
                            pe.wait_ge(m.h_done.sem, m.h_done.free(u + H0))
                            at = slice(F + fc * 128, F + (fc + 1) * 128)
                            t = nc.tensor.matmul(U[fc % 2][:], W[e][:, at], m.XNT[:, cols], start=True, stop=True)
                        t.then_inc(m.up_done.sem, 1)

                def to_down(s):
                    e = s // 2
                    last = unit(i, s, FC - 1)
                    if gated:
                        pe.wait_ge(m.h_done.sem, m.h_done.ended(last + H0))
                    else:
                        pe.wait_ge(m.act_done.sem, m.act_done.ended(last + U0))
                    pe.wait_ge(m.added.sem, m.added.free(i * 16 + (4 * (S0 + s) + 3)))
                    for b in range(B // 2):
                        for fc in range(FC):
                            t = nc.tensor.matmul(Y[s % 2][:, b, :], hid[s % 2][:, fc, b * S:(b + 1) * S],
                                                 W[e][:, down + fc * 128:down + (fc + 1) * 128],
                                                 start=(fc == 0), stop=(fc == FC - 1))
                    t.then_inc(m.y_done.sem, 1)

                for what, s in order:
                    (up if what == "up" else to_down)(s)

        @block.scalar
        def _(act):
            with act.Fori(0, E // 2) as i:
                for s in range(4):
                    for fc in range(FC):
                        u = unit(i, s, fc)
                        act.wait_ge(m.up_done.sem, m.up_done.ended(u + U0))
                        if gated:
                            act.wait_ge(m.h_done.sem, m.h_done.free(u + H0))
                            t = nc.scalar.activation(silu[fc % 2][:], G[fc % 2][:], func)
                        else:
                            if fc == 0:
                                act.wait_ge(m.y_done.sem, m.y_done.free(i * 4 + (S0 + s)))
                            t = nc.scalar.activation(hid[s % 2][:, fc, :], G[fc % 2][:], func,
                                                     bias=W[s // 2][:, down + F + fc:down + F + fc + 1])
                        t.then_inc(m.act_done.sem, 1)

        @block.vector
        def _(dve):
            with dve.Fori(0, E // 2) as i:
                def gate(s):
                    for fc in range(FC):
                        u = unit(i, s, fc)
                        if fc == 0:
                            dve.wait_ge(m.y_done.sem, m.y_done.free(i * 4 + (S0 + s)))
                        dve.wait_ge(m.act_done.sem, m.act_done.ended(u + U0))
                        nc.vector.tensor_tensor(hid[s % 2][:, fc, :], silu[fc % 2][:], U[fc % 2][:],
                                                ALU.mult).then_inc(m.h_done.sem, 1)

                def add(s):
                    n = i * 16 + 4 * (S0 + s)
                    dve.wait_ge(m.y_done.sem, m.y_done.ended(i * 4 + (S0 + s)))
                    dve.wait_ge(m.added.sem, m.added.ended(n - 1))
                    for b in range(B // 2):
                        x = m.X[:, (s % 2) * (B // 2) + b, :]
                        at = i * 2 + ((s % 2) * (B // 2) + b) * comb.shape[2] + s // 2
                        nc.vector.scalar_tensor_tensor(
                            out=x, in0=Y[s % 2][:, b, :], scalar=comb.rearrange("p b e -> p (b e)")[:, bass.ds(at, 1)],
                            in1=x, op0=ALU.mult, op1=ALU.add).then_inc(m.added.sem, 1)

                for what, s in order:
                    if what == "down":
                        add(s)
                    elif gated:
                        gate(s)


def ffn0_stage(nc, m):
    norm_stage(nc, m, m.X, m.XN)
    C, EC = 5, 4
    with ExitStack() as ctx:
        sb = lambda name, shape, dt=F32: ctx.enter_context(nc.sbuf_tensor(f"{name}_f0", shape, dt))
        comb, combT = sb("comb", [S, B, 8]), sb("combT", [8, T])
        hid, up = sb("hid", [128, C, T]), sb("up", [128, C, T])
        spread = sb("spread", [128, EC, T])
        route(nc, m, 8, m.w("L0f_router"), "sigmoid", comb[:], combT[:])
        wg, wu, wd = (m.w(f"L0f_{k}") for k in "gud")
        at = lambda c: slice(c * 128, (c + 1) * 128)
        jobs = [(hid[:, c, :], [wg[:, at(c)]], [m.XNT[:]], None, ACT.Silu) for c in range(C)]
        jobs += [(up[:, c, :], [wu[:, at(c)]], [m.XNT[:]], None) for c in range(C)]
        jobs += [(spread[:, c, :], [m.w("L0f_sel", slice(0, 8))[:, at(c)]], [combT[:]], None) for c in range(EC)]
        project(nc, m, jobs)
        with nc.Block() as block:
            @block.vector
            def _(dve):
                m.dve_steps.done(dve, nc.vector.tensor_tensor(hid[:], hid[:], up[:], ALU.mult))
                nc.vector.tensor_tensor(hid[:, 0:EC, :], hid[:, 0:EC, :], spread[:], ALU.mult)
        add_products(nc, m, [((lambda b, c=c: hid[:, c, b * S:(b + 1) * S]), wd[:, at(c)]) for c in range(C)])


def expert_stage(nc, m, layer, E, FC, kind, func, weights, rows=(), b2=None, gated=False):
    EP = 16 if E > 8 else 8
    with ExitStack() as ctx:
        sb = lambda name, shape, dt=F32: ctx.enter_context(nc.sbuf_tensor(f"{name}_{layer}", shape, dt))
        comb, combT = sb("comb", [S, B, EP]), sb("combT", [EP, T])
        route(nc, m, E, m.w(f"{layer}_router"), kind, comb[:], combT[:] if b2 is not None else None, rows)
        if b2 is not None:
            add_products(nc, m, [((lambda b: combT[:, b * S:(b + 1) * S]), b2)])
        experts(nc, m, 8 if gated else E, FC, weights, func, comb[:], gated)


def cross_attention0(nc, m):
    norm_stage(nc, m, m.X, m.XN)
    with ExitStack() as ctx:
        sb = lambda name, shape, dt=F32: ctx.enter_context(nc.sbuf_tensor(f"{name}_x0", shape, dt))
        QT, KT, QR, KR = (sb(name, [D, T]) for name in ("QT", "KT", "QR", "KR"))
        V = sb("V", [S, B, H, DH + 1])
        mask8, maskf = sb("mask8", [128, T], U8), sb("maskf", [128, T])
        qm, km = sb("qm", [128, T], BF16), sb("km", [128, T], BF16)
        mask_loaded = m.sem("mask_loaded")
        project(nc, m, [(QT[:], [m.w("L0x_q")], [m.XNT[:]], None), (QR[:], [m.w("L0x_qs")], [m.XNT[:]], None),
                        (KT[:], [m.w("L0x_k")], [m.CT[:]], None), (KR[:], [m.w("L0x_ks")], [m.CT[:]], None)])
        rope(nc, m, [(QT[:], QR[:], m.w("rope0c"), m.w("rope0s")), (KT[:], KR[:], m.w("rope0c"), m.w("rope0s"))])
        with nc.Block() as block:
            @block.sync
            def _(sp):
                sp.dma_start(mask8[:], m.dram["mask"].to_broadcast([128, T])).then_inc(mask_loaded, 16)

            @block.vector
            def _(dve):
                steps = m.dve_steps
                steps.inc(nc.vector.memset(qm[:], 0.0))
                steps.done(dve, nc.vector.memset(km[:], 0.0))
                dve.wait_ge(mask_loaded, 16)
                steps.done(dve, nc.vector.tensor_copy(maskf[:], mask8[:]))
                nc.vector.tensor_copy(qm[0:1, :], maskf[0:1, :])
                nc.vector.memset(qm[32:33, :], 1.0)
                nc.vector.tensor_scalar(km[0:1, :], maskf[0:1, :], BIG, None, ALU.mult)
                nc.vector.memset(km[32:33, :], -BIG)
                nc.vector.tensor_tensor(QT[:], QT[:], maskf[:], ALU.mult)
                nc.vector.tensor_tensor(KT[:], KT[:], maskf[:], ALU.mult)
        values(nc, m, V, m.CT[:], m.w("L0x_v"))
        attend(nc, m, QT, KT, V, m.O, token_masks=(qm, km))
    out_project(nc, m, m.O, m.w("L0x_o"))


def attention1(nc, m):
    norm_stage(nc, m, m.X, m.XN)
    with ExitStack() as ctx:
        sb = lambda name, shape, dt=F32: ctx.enter_context(nc.sbuf_tensor(f"{name}_a1", shape, dt))
        QT, KT = sb("QT", [D, T]), sb("KT", [D, T])
        V = sb("V", [S, B, H, DH + 1])
        rel, table = sb("rel", [128, 2, D]), sb("table", [128, 2, H])
        bias = sb("bias", [S, H, S])
        rel_loaded, summed, stored, loaded = (m.sem(n) for n in ("rel_loaded", "rel_summed", "rel_stored",
                                                                "bias_loaded"))
        tableT = sb("tableT", [H, 2 * S])
        turn_ctx = ExitStack()
        ps = turn_ctx.enter_context(nc.psum_tensor("table_ps", [H, 2 * S], F32))
        base = m.n_proj
        m.n_proj += 1
        with nc.Block() as block:
            tab = m.dram["rel_table"]

            @block.sync
            def _(sp):
                sp.dma_start(rel[:], m.dram["rel_pos"]).then_inc(rel_loaded, 16)
                sp.wait_ge(summed, 2)
                sp.dma_start(tab, tableT[:]).then_inc(stored, 16)
                sp.wait_ge(stored, 16)
                sp.dma_start(bias[:], bass.AP(tab.tensor, tab.offset,
                                              [[1, S], [2 * S, H], [1, S]])).then_inc(loaded, 16)

            @block.tensor
            def _(pe):
                pe.wait_ge(summed, 1)
                for c in range(2):
                    t = nc.tensor.transpose(ps[:, c * 128:(c + 1) * 128], table[:, c, :], m.w("ident"))
                t.then_inc(m.proj, 1)

            @block.vector
            def _(dve):
                dve.wait_ge(rel_loaded, 16)
                nc.vector.tensor_reduce(table[:], rel[:].rearrange("p c (h d) -> p c h d", h=H), AX.X,
                                        ALU.add).then_inc(summed, 1)
                dve.wait_ge(m.proj, base + 1)
                nc.vector.tensor_copy(tableT[:], ps[:]).then_inc(summed, 1)
                dve.wait_ge(loaded, 16)
                nc.vector.scalar_tensor_tensor(out=bias[:], in0=bias[:], scalar=float(DH) ** 0.5,
                                               in1=bcast_mid(m.w("causal_flip"), H), op0=ALU.mult, op1=ALU.add)
        turn_ctx.close()
        project(nc, m, [(QT[:], [m.w("L1a_q")], [m.XNT[:]], m.w("L1a_bq")),
                        (KT[:], [m.w("L1a_k")], [m.XNT[:]], m.w("L1a_bk"))])
        values(nc, m, V, m.XNT[:], m.w("L1a_v"), m.row("L1a_bv"))
        attend(nc, m, QT, KT, V, m.O, bias=bias)
    out_project(nc, m, m.O, m.w("L1a_o"), m.row("L1a_bo"))


def mix_stage1(nc, m):
    norm_stage(nc, m, m.X, m.XN)
    with ExitStack() as ctx:
        mean = ctx.enter_context(nc.sbuf_tensor("ctx_mean", [D, B], F32))
        with nc.Block() as block:
            @block.vector
            def _(dve):
                m.dve_steps.done(dve, nc.vector.tensor_reduce(
                    mean[:], m.CT[:].rearrange("p (b s) -> p b s", b=B), AX.X, ALU.add))
                nc.vector.tensor_scalar(mean[:], mean[:], 1.0 / S, None, ALU.mult)
        add_products(nc, m, [((lambda b: m.XNT[:, b * S:(b + 1) * S]), m.w("L1x_w1")),
                             ((lambda b: mean[:, b:b + 1].to_broadcast([D, S])), m.w("L1x_w2"))],
                     bias_row=m.row("L1x_b"))


def ffn1_stage(nc, m):
    norm_stage(nc, m, m.X, m.XN)
    expert_stage(nc, m, "L1f", 16, 2, "softmax_two", ACT.Relu, m.dram["L1f_w"],
                 rows=(m.row("L1f_bg"), m.row("L1f_bias")), b2=m.w("L1f_b2", slice(0, 16)))


def attention2(nc, m):
    norm_stage(nc, m, m.X, m.XN)
    with ExitStack() as ctx:
        sb = lambda name, shape, dt=F32: ctx.enter_context(nc.sbuf_tensor(f"{name}_a2", shape, dt))
        QT, KT, QR, KR = (sb(name, [D, T]) for name in ("QT", "KT", "QR", "KR"))
        V = sb("V", [S, B, H, DH + 1])
        project(nc, m, [(QT[:], [m.w("L2a_q")], [m.XNT[:]], None), (QR[:], [m.w("L2a_qs")], [m.XNT[:]], None),
                        (KT[:], [m.w("L2a_k")], [m.XNT[:]], None), (KR[:], [m.w("L2a_ks")], [m.XNT[:]], None)])
        rope(nc, m, [(QT[:], QR[:], m.w("rope2c"), m.w("rope2s")), (KT[:], KR[:], m.w("rope2c"), m.w("rope2s"))])
        values(nc, m, V, m.XNT[:], m.w("L2a_v"))
        attend(nc, m, QT, KT, V, m.O, mask=m.causal4[:])
    out_project(nc, m, m.O, m.w("L2a_o"))


def bidirectional2(nc, m):
    norm_stage(nc, m, m.X, m.XN)
    with ExitStack() as outer:
        sb = lambda name, shape, dt=F32: outer.enter_context(nc.sbuf_tensor(f"{name}_x2", shape, dt))
        hw, P, PTs = sb("hw", [D, T]), sb("P", [S, B, S]), sb("PTs", [S, T])
        F2, F3, F4 = (sb(name, [D, T]) for name in ("F2", "F3", "F4"))
        top, total, best = sb("top", [S, B]), sb("total", [S, B]), sb("best", [S, B])
        batt, btop, btotal = sb("batt", [B, S]), sb("btop", [B, 1]), sb("btotal", [B, 1])
        battT, hc = sb("battT", [S, B]), sb("hc", [D, B])
        steps = m.dve_steps
        halves = [slice(0, HALF), slice(HALF, T)]
        with ExitStack() as ctx:
            sim = ctx.enter_context(nc.psum_tensor("sim", [S, B, S], F32))
            small = ctx.enter_context(nc.psum_tensor("small_x2", [S, 256], F32))
            base_p, base_e = m.n_proj, m.n_evac
            m.n_proj += 3
            m.n_evac += 2
            v = {}
            with nc.Block() as block:
                @block.vector
                def _(dve):
                    v["hw"] = steps.inc(nc.vector.tensor_scalar(hw[:], m.XNT[:], m.w("L2x_w3"), m.w("L2x_w2"),
                                                                ALU.mult, ALU.add))
                    dve.wait_ge(m.proj, base_p + 1)
                    steps.done(dve, nc.vector.tensor_reduce(top[:], sim[:], AX.X, ALU.max))
                    v["shift"] = steps.inc(nc.vector.tensor_tensor(P[:], sim[:], bcast_last(top[:], S), ALU.subtract))
                    steps.done(dve, nc.vector.tensor_tensor(best[:], top[:], small[:, 0:B], ALU.add))
                    v["best"] = steps.inc(nc.vector.tensor_scalar(best[:], best[:], m.row("L2x_bsim"), None, ALU.add))
                    dve.wait_ge(m.proj, base_p + 2)
                    steps.done(dve, nc.vector.tensor_reduce(btop[:], small[0:B, 128:256], AX.X, ALU.max))
                    v["bshift"] = steps.inc(nc.vector.tensor_scalar(batt[:], small[0:B, 128:256], btop[:], None,
                                                                    ALU.subtract))
                    dve.wait_ge(m.evac, base_e + 2)
                    steps.done(dve, nc.vector.tensor_reduce(total[:], P[:], AX.X, ALU.add))
                    steps.done(dve, nc.vector.reciprocal(total[:], total[:]))
                    steps.done(dve, nc.vector.tensor_tensor(P[:], P[:], bcast_last(total[:], S), ALU.mult))
                    steps.done(dve, nc.vector.tensor_reduce(btotal[:], batt[:], AX.X, ALU.add))
                    steps.done(dve, nc.vector.reciprocal(btotal[:], btotal[:]))
                    nc.vector.tensor_scalar(batt[:], batt[:], btotal[:], None, ALU.mult)

                @block.tensor
                def _(pe):
                    for b in range(B):
                        nc.tensor.matmul(small[:, b:b + 1], m.XNT[:, b * S:(b + 1) * S], m.w("L2x_w1"),
                                         start=True, stop=True)
                    pe.wait_ge(steps.sem, v["hw"])
                    for b in range(B):
                        t = nc.tensor.matmul(sim[:, b, :], hw[:, b * S:(b + 1) * S], m.CT[:, b * S:(b + 1) * S],
                                             start=True, stop=True)
                    t.then_inc(m.proj, 1)
                    pe.wait_ge(steps.sem, v["best"])
                    nc.tensor.transpose(small[0:B, 128:256], best[:], m.w("ident")).then_inc(m.proj, 2)

                @block.scalar
                def _(act):
                    act.wait_ge(steps.sem, v["shift"])
                    nc.scalar.activation(P[:], P[:], ACT.Exp).then_inc(m.evac, 1)
                    act.wait_ge(steps.sem, v["bshift"])
                    nc.scalar.activation(batt[:], batt[:], ACT.Exp).then_inc(m.evac, 1)
        with ExitStack() as ctx:
            pt = ctx.enter_context(nc.psum_tensor("pt_x2", [S, T], F32))
            hat = ctx.enter_context(nc.psum_tensor("hat", [D, T], F32))
            small = ctx.enter_context(nc.psum_tensor("small2", [S, 256], F32))
            base_p, base_e = m.n_proj, m.n_evac
            m.n_proj += 6
            m.n_evac += 5
            with nc.Block() as block:
                @block.tensor
                def _(pe):
                    nc.tensor.transpose(small[:, 0:B], batt[:], m.w("ident", slice(0, B))[:, 0:B]).then_inc(m.proj, 1)
                    for b in range(B):
                        t = nc.tensor.transpose(pt[:, b * S:(b + 1) * S], P[:, b, :], m.w("ident"))
                        if b % 4 == 3:
                            t.then_inc(m.proj, 1)
                    pe.wait_ge(m.evac, base_e + 1)
                    for b in range(B):
                        t = nc.tensor.matmul(small[:, 128 + b:129 + b], m.XN[:, b, :], battT[:, b:b + 1],
                                             start=True, stop=True)
                    t.then_inc(m.proj, 1)
                    for b in range(B):
                        if b % 4 == 0:
                            pe.wait_ge(m.evac, base_e + 2 + b // 4)
                        t = nc.tensor.matmul(hat[:, b * S:(b + 1) * S], m.CTOK[:, b, :], PTs[:, b * S:(b + 1) * S],
                                             start=True, stop=True)
                        if b % 4 == 3:
                            t.then_inc(m.proj, 1)

                @block.scalar
                def _(act):
                    act.wait_ge(m.proj, base_p + 1)
                    nc.scalar.activation(battT[:], small[:, 0:B], ACT.Copy).then_inc(m.evac, 1)
                    for half in range(2):
                        act.wait_ge(m.proj, base_p + 2 + half)
                        nc.scalar.activation(PTs[:, halves[half]], pt[:, halves[half]], ACT.Copy).then_inc(m.evac, 1)
                    for half in range(2):
                        act.wait_ge(m.proj, base_p + 5 + half)
                        nc.scalar.activation(F2[:, halves[half]], hat[:, halves[half]], ACT.Copy).then_inc(m.evac, 1)

                @block.vector
                def _(dve):
                    dve.wait_ge(m.proj, base_p + 4)
                    steps.done(dve, nc.vector.tensor_copy(hc[:], small[:, 128:128 + B]))
                    nc.vector.tensor_tensor(F4[:].rearrange("p (b s) -> p b s", b=B),
                                            m.XNT[:].rearrange("p (b s) -> p b s", b=B), bcast_last(hc[:], S), ALU.mult)
                    for half in range(2):
                        dve.wait_ge(m.evac, base_e + 4 + half)
                        nc.vector.tensor_tensor(F3[:, halves[half]], m.XNT[:, halves[half]], F2[:, halves[half]],
                                                ALU.mult)
        w = m.w("L2x_wqv")
        add_products(nc, m, [((lambda b, f=f: f[:, b * S:(b + 1) * S]), w[:, k * D:(k + 1) * D])
                             for k, f in enumerate((m.XNT, F2, F3, F4))], bias_row=m.row("L2x_b"))


def block2(nc, m):
    norm_stage(nc, m, m.X, m.XN)
    norm_stage(nc, m, m.XN, m.O, m.w("L2n1_w"), m.w("L2n1_b"))
    with ExitStack() as ctx:
        sb = lambda name, shape, dt=F32: ctx.enter_context(nc.sbuf_tensor(f"{name}_b2", shape, dt))
        QT, KT = sb("QT", [D, T]), sb("KT", [D, T])
        V = sb("V", [S, B, H, DH + 1])
        project(nc, m, [(QT[:], [m.w("L2f_q")], [m.XNT[:]], m.w("L2f_bq")),
                        (KT[:], [m.w("L2f_k")], [m.XNT[:]], m.w("L2f_bk"))])
        values(nc, m, V, m.XNT[:], m.w("L2f_v"), m.row("L2f_bv"))
        attend(nc, m, QT, KT, V, m.O, mask=m.causal4[:])
    out_project(nc, m, m.O, m.w("L2f_o"), m.row("L2f_bo"), target=m.XN)
    norm_stage(nc, m, m.XN, m.O, m.w("L2n2_w"), m.w("L2n2_b"))
    with nc.Block() as block:
        @block.vector
        def _(dve):
            nc.vector.tensor_tensor(m.X[:], m.X[:], m.XN[:], ALU.add)
    expert_stage(nc, m, "L2f", 8, 4, "softmax_two", ACT.Gelu, m.dram["L2f_w"],
                 b2=m.w("L2f_b2", slice(0, 8)))


def attention3(nc, m):
    norm_stage(nc, m, m.X, m.XN)
    with ExitStack() as ctx:
        sb = lambda name, shape, dt=F32: ctx.enter_context(nc.sbuf_tensor(f"{name}_a3", shape, dt))
        QT, KT, K2T = sb("QT", [D, T]), sb("KT", [D, T]), sb("K2T", [D, T])
        V, O2 = sb("V", [S, B, H, DH + 1]), sb("O2", [S, B, D])
        project(nc, m, [(QT[:], [m.w("L3a_q")], [m.XNT[:]], m.w("L3a_bq")),
                        (KT[:], [m.w("L3a_k")], [m.XNT[:]], m.w("L3a_bk")),
                        (K2T[:], [m.w("L3a_k2")], [m.XNT[:]], m.w("L3a_bk2"))])
        with nc.Block() as block:
            @block.vector
            def _(dve):
                m.dve_steps.done(dve, nc.vector.memset(V[:], 1.0))
                nc.vector.tensor_copy(V[:, :, :, 0:DH], m.XN[:].rearrange("p b (h d) -> p b h d", h=H))
        attend(nc, m, QT, KT, V, m.O, mask=m.causal4[:])
        with ExitStack() as inner:
            later = inner.enter_context(nc.psum_tensor("later", [S, B, D], F32))
            base = m.n_proj
            m.n_proj += 1
            with nc.Block() as block:
                @block.tensor
                def _(pe):
                    for b in range(B):
                        t = nc.tensor.transpose(later[0:S - 1, b, :], m.XNT[:, b * S + 1:(b + 1) * S], m.w("ident"))
                    t.then_inc(m.proj, 1)

                @block.vector
                def _(dve):
                    dve.wait_ge(m.proj, base + 1)
                    v4 = lambda a: a.rearrange("p b (h d) -> p b h d", h=H)
                    for b in range(B):
                        heads = lambda a: a[0:S - 1, b, :].rearrange("p (h d) -> p h d", h=H)
                        nc.vector.tensor_tensor(V[0:S - 1, b, :, 0:DH], heads(later), heads(m.O), ALU.subtract)
        attend(nc, m, QT, K2T, V, O2, mask=m.strict4[:])
        with nc.Block() as block:
            @block.vector
            def _(dve):
                nc.vector.scalar_tensor_tensor(out=m.O[:], in0=O2[:], scalar=m.w("row1"), in1=m.O[:], op0=ALU.mult,
                                               op1=ALU.add)
    out_project(nc, m, m.O, m.w("L3a_o"), m.row("L3a_bo"), bias_times=2.0)


def autocorrelation3(nc, m):
    norm_stage(nc, m, m.X, m.XN)
    steps = m.dve_steps
    TOP = 4
    with ExitStack() as outer:
        sb = lambda name, shape, dt=F32: outer.enter_context(nc.sbuf_tensor(f"{name}_x3", shape, dt))
        tok = [sb(f"tok{k}", [S, B, D]) for k in range(3)]
        c = [sb(f"cos{k}", [FREQ, T]) for k in range(3)]
        s = [sb(f"sin{k}", [FREQ, T]) for k in range(3)]
        re, im, tmp = sb("re", [FREQ, T]), sb("im", [FREQ, T]), sb("tmp", [FREQ, T])
        res, ims = sb("res", [FREQ, B * H]), sb("ims", [FREQ, B * H])
        corr, best, index = sb("corr", [128, S]), sb("best", [128, 8]), sb("index", [128, 8], U32)
        indexf, wt, one = sb("indexf", [128, TOP]), sb("wt", [128, TOP]), sb("one", [128, 1])
        wvec, wtmp, wT = sb("wvec", [128, S]), sb("wtmp", [128, S]), sb("wT", [S, 128])
        wc, ws = sb("wc", [FREQ, 128]), sb("ws", [FREQ, 128])
        sources = (m.XNT[:], m.CT[:], m.CT[:])
        for k, name in enumerate("qkv"):
            token_linear(nc, m, tok[k], sources[k], m.w(f"L3x_{name}"), m.row(f"L3x_b{name}"))
        flat = [t[:].rearrange("p b d -> p (b d)") for t in tok]
        project(nc, m, [(x[k][:], [m.w(w)], [flat[k]], None) for k in range(3) for x, w in ((c, "dft_c"), (s, "dft_s"))])
        ps_ctx = ExitStack()
        pc = ps_ctx.enter_context(nc.psum_tensor("corr_ps", [128, S], F32))
        pw = ps_ctx.enter_context(nc.psum_tensor("w_ps", [128, 3 * 128], F32))
        base_p, base_e = m.n_proj, m.n_evac
        m.n_proj += 3
        m.n_evac += 2
        v = {}
        with nc.Block() as block:
            @block.vector
            def _(dve):
                tt = lambda out, a, b, op: steps.done(dve, nc.vector.tensor_tensor(out, a, b, op))
                tt(re[:], c[0][:], c[1][:], ALU.mult)
                tt(tmp[:], s[0][:], s[1][:], ALU.mult)
                tt(re[:], re[:], tmp[:], ALU.add)
                tt(im[:], s[0][:], c[1][:], ALU.mult)
                tt(tmp[:], c[0][:], s[1][:], ALU.mult)
                tt(im[:], im[:], tmp[:], ALU.subtract)
                steps.done(dve, nc.vector.tensor_reduce(res[:], re[:].rearrange("p (g d) -> p g d", d=DH), AX.X, ALU.add))
                v["sums"] = steps.inc(nc.vector.tensor_reduce(ims[:], im[:].rearrange("p (g d) -> p g d", d=DH), AX.X,
                                                              ALU.add))
                dve.wait_ge(m.proj, base_p + 1)
                steps.done(dve, nc.vector.tensor_copy(corr[:], pc[:]))
                steps.done(dve, nc.vector.max(best[:], corr[:]))
                steps.done(dve, nc.vector.max_index(index[:], best[:], corr[:]))
                steps.done(dve, nc.vector.tensor_copy(indexf[:], index[:, 0:TOP]))
                v["shift"] = steps.inc(nc.vector.tensor_scalar(wt[:], best[:, 0:TOP], best[:, 0:1], None, ALU.subtract))
                dve.wait_ge(m.evac, base_e + 1)
                steps.done(dve, nc.vector.tensor_reduce(one[:], wt[:], AX.X, ALU.add))
                steps.done(dve, nc.vector.reciprocal(one[:], one[:]))
                steps.done(dve, nc.vector.tensor_scalar(wt[:], wt[:], one[:], None, ALU.mult))
                for k in range(TOP):
                    out = wvec if k == 0 else wtmp
                    steps.done(dve, nc.vector.tensor_scalar(out[:], m.w("iota128"), indexf[:, k:k + 1], wt[:, k:k + 1],
                                                            ALU.is_equal, ALU.mult))
                    if k:
                        tt(wvec[:], wvec[:], wtmp[:], ALU.add)
                v["wvec"] = steps.n
                dve.wait_ge(m.proj, base_p + 2)
                v["wT"] = steps.inc(nc.vector.tensor_copy(wT[:], pw[:, 0:128]))
                dve.wait_ge(m.proj, base_p + 3)
                steps.inc(nc.vector.tensor_copy(wc[:], pw[0:FREQ, 128:256]))
                steps.done(dve, nc.vector.tensor_copy(ws[:], pw[0:FREQ, 256:384]))
                wide = lambda a: bcast_last(a[:], DH)
                v3 = lambda a: a[:].rearrange("p (g d) -> p g d", d=DH)
                tt(v3(re), v3(c[2]), wide(wc), ALU.mult)
                tt(v3(tmp), v3(s[2]), wide(ws), ALU.mult)
                tt(re[:], re[:], tmp[:], ALU.subtract)
                tt(v3(im), v3(s[2]), wide(wc), ALU.mult)
                tt(v3(tmp), v3(c[2]), wide(ws), ALU.mult)
                tt(im[:], im[:], tmp[:], ALU.add)

            @block.tensor
            def _(pe):
                freq = slice(0, FREQ)
                pe.wait_ge(steps.sem, v["sums"])
                nc.tensor.matmul(pc[:], res[:], m.w("invh_c", freq), start=True, stop=False)
                nc.tensor.matmul(pc[:], ims[:], m.w("invh_s", freq), start=False, stop=True).then_inc(m.proj, 1)
                pe.wait_ge(steps.sem, v["wvec"])
                nc.tensor.transpose(pw[:, 0:128], wvec[:], m.w("ident")).then_inc(m.proj, 1)
                pe.wait_ge(steps.sem, v["wT"])
                nc.tensor.matmul(pw[0:FREQ, 128:256], m.w("dft_c"), wT[:], start=True, stop=True)
                nc.tensor.matmul(pw[0:FREQ, 256:384], m.w("dft_s"), wT[:], start=True, stop=True).then_inc(m.proj, 1)

            @block.scalar
            def _(act):
                act.wait_ge(steps.sem, v["shift"])
                nc.scalar.activation(wt[:], wt[:], ACT.Exp).then_inc(m.evac, 2)
        ps_ctx.close()
        freq = slice(0, FREQ)
        project(nc, m, [(m.O[:].rearrange("p b d -> p (b d)"), [m.w("inv_c", freq), m.w("inv_s", freq)],
                         [re[:], im[:]], None)])
    out_project(nc, m, m.O, m.w("L3x_o"), m.row("L3x_bo"))


def token_linear(nc, m, out, source, weight, bias_row):
    with ExitStack() as ctx:
        ps = ctx.enter_context(nc.psum_tensor(f"lin_ps{m.n_proj}", [S, B, D], F32))
        block = ctx.enter_context(nc.Block())
        base = m.n_proj
        m.n_proj += 2

        @block.tensor
        def _(pe):
            for b in range(B):
                t = nc.tensor.matmul(ps[:, b, :], source[:, b * S:(b + 1) * S], weight, start=True, stop=True)
                if b % 4 == 3:
                    t.then_inc(m.proj, 1)

        @block.vector
        def _(dve):
            for half in range(2):
                dve.wait_ge(m.proj, base + half + 1)
                bs = slice(4 * half, 4 * half + 4)
                nc.vector.tensor_tensor(out[:, bs, :], ps[:, bs, :], bcast_mid(bias_row, B // 2), ALU.add)


def ffn3_stage(nc, m):
    norm_stage(nc, m, m.X, m.XN)
    expert_stage(nc, m, "L3f", 7, 4, "softmax_all", ACT.Silu, m.dram["L3f_w"], gated=True)


def build(nc, dram, stages):
    with ExitStack() as ctx:
        m = Model(nc, ctx, dram)
        start_stage(nc, m)
        todo = [lambda: mamba_stage(nc, m)] + [lambda f=f: f(nc, m) for f in STAGES]
        for k in range(stages):
            if k == 1:
                late_constants(nc, m)
            todo[k]()
        with nc.Block() as block:
            @block.sync
            def _(sp):
                if stages <= 1:
                    sp.wait_ge(m.loaded_rest, 64)
                sp.dma_start(dram["out"], m.X[:]).then_inc(m.stored, 16)
                sp.wait_ge(m.stored, 16)


STAGES = [cross_attention0, ffn0_stage, attention1, mix_stage1, ffn1_stage, attention2, bidirectional2, block2, attention3,
          autocorrelation3, ffn3_stage]
N_STAGES = 12


def pack(table, total, arrays, rows=128):
    out = np.zeros((rows, total), np.float32)
    for name, (at, n) in table.items():
        a = np.asarray(arrays[name]).reshape(-1, n)
        out[:a.shape[0], at:at + n] = a
    return out


def host_arrays(i):
    def chunks(a, width):
        return a.reshape(-1, 128, width).transpose(1, 0, 2).reshape(128, -1)

    a = {}
    a["ident"] = np.eye(128, dtype=np.float32)
    a["ln_w"], a["ln_b"] = (i[f"L0_attn_{n}"].reshape(128, 1) for n in ("ln_w", "ln_b"))
    a["W_in"] = i["L0_attn_W_in"]
    a["conv_w"] = chunks(i["L0_attn_conv_w"].reshape(INNER, TAPS), TAPS)
    a["conv_b"] = chunks(i["L0_attn_conv_b"].reshape(INNER, 1), 1)
    a["W_xproj"] = chunks(i["L0_attn_W_xproj"], RANK + 2 * STATE)
    a["W_dt"] = i["L0_attn_W_dt"]
    a["b_dt"] = chunks(i["L0_attn_b_dt"].reshape(INNER, 1), 1)
    a["A_log"] = chunks(i["L0_attn_A_log"], STATE)
    a["Dskip"] = chunks(i["L0_attn_D"].reshape(INNER, 1), 1)
    a["W_out"] = chunks(i["L0_attn_W_out"], D)

    p, t = np.arange(128), np.arange(S)
    a["head_mask"] = (p[:, None] // DH == np.arange(H)).astype(np.float32)
    a["causal"] = np.where(t[None, :] > t[:, None], NEG, 0.0).astype(np.float32)
    a["flip"], a["causal_flip"] = a["ident"][::-1], a["causal"][::-1]
    a["strict"] = np.where(t[None, :] >= t[:, None], NEG, 0.0).astype(np.float32)
    a["row1"] = (t[:, None] > 0).astype(np.float32)
    a["neghalf"] = np.full((128, B), -0.5, np.float32)
    a["iota16"] = np.tile(np.arange(16, dtype=np.float32), (128, 1))
    a["iota128"] = np.tile(np.arange(128, dtype=np.float32), (128, 1))
    w0 = (1.0 / 10000.0 ** (np.arange(1, DH + 1, 2, dtype=np.float32) / DH)).astype(np.float32)
    ang0 = np.arange(1, S + 1, dtype=np.float32)[:, None] * w0
    d = p % DH
    a["rope0c"] = np.cos(ang0).T[d // 2]
    a["rope0s"] = np.sin(ang0).T[d // 2] * np.where(d % 2, 1, -1)[:, None]
    w2 = (1.0 / 10000.0 ** (np.arange(DH // 2, dtype=np.float32) / (DH // 2))).astype(np.float32)
    ang2 = np.arange(S, dtype=np.float32)[:, None] * w2
    a["rope2c"] = np.cos(ang2).T[d % 4]
    a["rope2s"] = np.sin(ang2).T[d % 4] * np.where(d < 4, -1, 1)[:, None]
    f = np.arange(FREQ)
    theta = 2 * np.pi * (t[:, None] * f % S) / S
    a["dft_c"], a["dft_s"] = np.cos(theta), np.sin(theta)
    both = np.where((f == 0) | (f == S // 2), 1.0, 2.0)[:, None] / S
    a["inv_c"], a["inv_s"] = np.cos(theta).T * both, np.sin(theta).T * both
    a["invh_c"], a["invh_s"] = a["inv_c"] / DH, a["inv_s"] / DH
    a["L0f_sel"] = (np.arange(512) // 64 == np.arange(8)[:, None]).astype(np.float32)

    pairs = p ^ 1
    halves = p // DH * DH + (d + DH // 2) % DH
    wkv = i["L0_xattn_W_kv"]
    a["L0x_q"], a["L0x_k"], a["L0x_v"], a["L0x_o"] = i["L0_xattn_W_q"], wkv[:, :D], wkv[:, D:], i["L0_xattn_W_c"]
    a["L0x_qs"], a["L0x_ks"] = a["L0x_q"][:, pairs], a["L0x_k"][:, pairs]
    a["L0f_router"] = i["L0_ffn_gate_weight"].T
    a["L0f_g"] = np.concatenate([i["L0_ffn_w_gate"].reshape(512, D), i["L0_ffn_ws_gate"]]).T
    a["L0f_u"] = np.concatenate([i["L0_ffn_w_up"].reshape(512, D), i["L0_ffn_ws_up"]]).T
    a["L0f_d"] = chunks(np.concatenate([i["L0_ffn_w_down"].transpose(0, 2, 1).reshape(512, D),
                                        i["L0_ffn_ws_down"].T]), D)
    qkv, qb = i["L1_attn_qkv_w"], i["L1_attn_qkv_b"]
    a["L1a_q"], a["L1a_k"], a["L1a_v"], a["L1a_o"] = qkv[:D].T, qkv[D:2 * D].T, qkv[2 * D:].T, i["L1_attn_proj_w"].T
    a["L1a_bq"], a["L1a_bk"], a["L1a_bv"] = qb[:D, None], qb[D:2 * D, None], qb[2 * D:]
    a["L1a_bo"] = i["L1_attn_proj_b"]
    a["L1x_w1"], a["L1x_w2"], a["L1x_b"] = i["L1_xattn_W"][:, :D].T, i["L1_xattn_W"][:, D:].T, i["L1_xattn_b"]
    a["L1f_router"], a["L1f_bg"], a["L1f_bias"] = i["L1_ffn_Wg"], i["L1_ffn_bg"], i["L1_ffn_bias"]
    a["L1f_b2"] = i["L1_ffn_b2"]
    kv = p // DH % HG * DH + d
    a["L2a_q"], a["L2a_k"], a["L2a_v"], a["L2a_o"] = (
        i["L2_attn_wq"], i["L2_attn_wk"][:, kv], i["L2_attn_wv"][:, kv], i["L2_attn_wo"])
    a["L2a_qs"], a["L2a_ks"] = a["L2a_q"][:, halves], a["L2a_k"][:, halves]
    a["L2x_w1"], a["L2x_w2"], a["L2x_w3"] = i["L2_xattn_w_sim"].reshape(3, D, 1)
    a["L2x_bsim"], a["L2x_b"], a["L2x_wqv"] = i["L2_xattn_b_sim"], i["L2_xattn_b_qv"], chunks(i["L2_xattn_W_qv"], D)
    for k in (1, 2):
        a[f"L2n{k}_w"], a[f"L2n{k}_b"] = i[f"L2_ffn_ln{k}_w"][:, None], i[f"L2_ffn_ln{k}_b"][:, None]
    w, b = i["L2_ffn_Wqkv"], i["L2_ffn_bqkv"]
    a["L2f_q"], a["L2f_k"], a["L2f_v"], a["L2f_o"] = w[:, :D], w[:, D:2 * D], w[:, 2 * D:], i["L2_ffn_Wo"]
    a["L2f_bq"], a["L2f_bk"], a["L2f_bv"], a["L2f_bo"] = b[:D, None], b[D:2 * D, None], b[2 * D:], i["L2_ffn_bo"]
    a["L2f_router"] = i["L2_ffn_gate_W"]
    a["L2f_b2"] = i["L2_ffn_fc2_b"]
    w, b = i["L3_attn_W_attn"], i["L3_attn_b_attn"]
    a["L3a_q"], a["L3a_k"], a["L3a_bq"], a["L3a_bk"] = w[:, :D], w[:, D:], b[:D, None], b[D:, None]
    a["L3a_k2"], a["L3a_bk2"] = i["L3_attn_W_k2"], i["L3_attn_b_k2"][:, None]
    a["L3a_o"], a["L3a_bo"] = i["L3_attn_W_proj"], i["L3_attn_b_proj"]
    for n in "qkvo":
        a[f"L3x_{n}"], a[f"L3x_b{n}"] = i[f"L3_xattn_W{n}"].T, i[f"L3_xattn_b{n}"]
    a["L3f_router"] = i["L3_ffn_router_w"].T
    return a


def big_arrays(i):
    def by_chunks(w):
        e, f, n = w.shape
        return w.reshape(e, f // 128, 128, n).transpose(0, 2, 1, 3).reshape(e, 128, -1)

    rel = np.zeros((2 * S, D), np.float32)
    rel[:2 * S - 1] = i["L1_attn_rel_pos_emb"][::-1]
    out = {
        "mask": i["mask_BxS2_bf1"].reshape(1, T).view(np.uint8),
        "rel_pos": rel.reshape(2, 128, D).transpose(1, 0, 2),
        "L1f_w": np.concatenate([i["L1_ffn_W1"], by_chunks(i["L1_ffn_W2"]), by_chunks(i["L1_ffn_b1"][:, :, None])], axis=2),
        "L2f_w": np.concatenate([i["L2_ffn_fc1_w"].transpose(0, 2, 1),
                                 by_chunks(i["L2_ffn_fc2_w"].transpose(0, 2, 1)),
                                 by_chunks(i["L2_ffn_fc1_b"][:, :, None])], axis=2),
    }
    gate, up, down = (np.concatenate([i[f"L3_ffn_routed_{n}"], i[f"L3_ffn_shared_{n}"][None]]).transpose(0, 2, 1)
                      for n in ("gate", "up", "down"))
    out["L3f_w"] = np.concatenate([gate, up, by_chunks(down)], axis=2)
    return {k: np.ascontiguousarray(v) for k, v in out.items()}


def kernel(**inputs):
    import concourse.bacc as bacc
    from concourse.bass_utils import run_bass_kernel_spmd

    i = {k: np.asarray(v) for k, v in inputs.items()}
    a = host_arrays(i)
    arrays = {
        "x": np.ascontiguousarray(i["x"].transpose(1, 0, 2)),
        "ctx_feat": np.ascontiguousarray(i["ctx_1024"].transpose(2, 0, 1)).reshape(D, T),
        "ctx_tok": np.ascontiguousarray(i["ctx_1024"].transpose(1, 0, 2)),
        "mamba": pack(MAMBA_AT, MAMBA_N, a),
        "small": pack(SMALL_AT, SMALL_N, a),
        "rows": pack(ROWS_AT, ROWS_N, a, rows=1),
        **big_arrays(i),
    }
    nc = bacc.Bacc("TRN2", target_bir_lowering=False, num_devices=1)
    dram = {name: nc.dram_tensor(name, list(v.shape), mybir.dt.from_np(v.dtype), kind="ExternalInput").ap()
            for name, v in arrays.items()}
    dram["rel_table"] = nc.dram_tensor("rel_table", [H, 2 * S], F32, kind="Internal").ap()
    dram["out"] = nc.dram_tensor("out", [S, B, D], F32, kind="ExternalOutput").ap()
    build(nc, dram, N_STAGES)
    result = run_bass_kernel_spmd(nc, [arrays], core_ids=[0])
    return np.ascontiguousarray(np.asarray(result.results[0]["out"]).transpose(1, 0, 2))
```

```python
from contextlib import ExitStack

import numpy as np

import concourse.bass as bass
from concourse import mybir

F32 = mybir.dt.float32
BF16 = mybir.dt.bfloat16
U8 = mybir.dt.uint8
U32 = mybir.dt.uint32
ACT = mybir.ActivationFunctionType
ALU = mybir.AluOpType
AX = mybir.AxisListType

B, S, D = 8, 128, 128
T = B * S
HALF = 512
H, DH = 16, 8
HG = 4
NG = H // HG
EPS = 1e-5
NEG = -1.0e30
BIG = float(2 ** 30)
INNER, STATE, RANK, TAPS = 256, 64, 8, 4
IC = INNER // 128
FREQ = S // 2 + 1


class Steps:

    def __init__(self, sem):
        self.sem, self.n, self.i, self.k = sem, 0, None, 0

    def inc(self, instruction):
        instruction.then_inc(self.sem, 1)
        if self.i is None:
            self.n += 1
            return self.n
        self.k += 1
        return self.i * self.per + (self.n + self.k)

    def done(self, engine, instruction):
        engine.wait_ge(self.sem, self.inc(instruction))

    def enter(self, i, per):
        self.i, self.per, self.k = i, per, 0

    def leave(self, passes):
        assert self.k == self.per, (self.k, self.per)
        self.i = None
        self.n += passes * self.per


class Ring:

    def __init__(self, sem, depth, spare=0):
        self.sem, self.depth, self.spare = sem, depth, spare
        self.start = depth + spare

    def ended(self, n):
        return n + (self.start + 1)

    def free(self, n):
        return n + (self.spare + 1)


def layout(name_shapes):
    table, at = {}, 0
    for name, n in name_shapes:
        table[name] = (at, n)
        at += n
    return table, at


MAMBA = [("ident", 128), ("ln_w", 1), ("ln_b", 1), ("W_in", 2 * INNER), ("conv_w", IC * TAPS), ("conv_b", IC),
         ("W_xproj", IC * (RANK + 2 * STATE)), ("W_dt", INNER), ("b_dt", IC), ("A_log", IC * STATE), ("Dskip", IC),
         ("W_out", IC * D)]
SMALL = [("head_mask", H), ("causal", S), ("strict", S), ("flip", S), ("causal_flip", S), ("row1", 1), ("iota16", 16), ("iota128", 128),
         ("rope0c", S), ("rope0s", S), ("rope2c", S), ("rope2s", S),
         ("L0x_q", D), ("L0x_qs", D), ("L0x_k", D), ("L0x_ks", D), ("L0x_v", D), ("L0x_o", D),
         ("L0f_router", 8), ("L0f_g", 640), ("L0f_u", 640), ("L0f_d", 640), ("L0f_sel", 512),
         ("L1a_q", D), ("L1a_k", D), ("L1a_v", D), ("L1a_o", D), ("L1a_bq", 1), ("L1a_bk", 1),
         ("L1x_w1", D), ("L1x_w2", D),
         ("L1f_router", 16), ("L1f_b2", D),
         ("L2a_q", D), ("L2a_qs", D), ("L2a_k", D), ("L2a_ks", D), ("L2a_v", D), ("L2a_o", D),
         ("L2x_w1", 1), ("L2x_w2", 1), ("L2x_w3", 1), ("L2x_wqv", 4 * D),
         ("L2n1_w", 1), ("L2n1_b", 1), ("L2n2_w", 1), ("L2n2_b", 1),
         ("L2f_q", D), ("L2f_k", D), ("L2f_v", D), ("L2f_o", D), ("L2f_bq", 1), ("L2f_bk", 1),
         ("L2f_router", 8), ("L2f_b2", D),
         ("L3a_q", D), ("L3a_k", D), ("L3a_k2", D), ("L3a_o", D), ("L3a_bq", 1), ("L3a_bk", 1), ("L3a_bk2", 1),
         ("L3x_q", D), ("L3x_k", D), ("L3x_v", D), ("L3x_o", D),
         ("dft_c", FREQ), ("dft_s", FREQ), ("inv_c", S), ("inv_s", S), ("invh_c", S), ("invh_s", S),
         ("L3f_router", 7)]
ROWS = [("L1a_bv", D), ("L1a_bo", D), ("L1x_b", D), ("L1f_bg", 16), ("L1f_bias", 16), ("L2x_b", D), ("L2x_bsim", 1),
        ("L2f_bv", D), ("L2f_bo", D), ("L3a_bo", D),
        ("L3x_bq", D), ("L3x_bk", D), ("L3x_bv", D), ("L3x_bo", D)]
MAMBA_AT, MAMBA_N = layout(MAMBA)
SMALL_AT, SMALL_N = layout(SMALL)
ROWS_AT, ROWS_N = layout(ROWS)


class Model:

    def __init__(self, nc, ctx, dram):
        self.nc, self.dram = nc, dram
        self.n_norm = self.n_attn = self.n_tail = self.n_moe = self.n_route = 0

        def sb(name, shape, dt=F32):
            return ctx.enter_context(nc.sbuf_tensor(name, shape, dt))

        def sem(name):
            return ctx.enter_context(nc.semaphore(name))

        self.X = sb("X", [S, B, D])
        self.XN = sb("XN", [S, B, D])
        self.XNT = sb("XNT", [D, T])
        self.CT = sb("CT", [D, T])
        self.CTOK = sb("CTOK", [S, B, D])
        self.O = sb("O", [S, B, D])
        self.mamba_pack = sb("mamba_pack", [128, MAMBA_N])
        self.small_pack = sb("small_pack", [128, SMALL_N])
        self.row_pack = sb("row_pack", [128, ROWS_N])
        self.neghalf = sb("neghalf", [S, B])
        self.identb = sb("identb", [128, 128], BF16)
        self.select2 = sb("select2", [128, STATE], BF16)
        self.causal = lambda g: bcast_mid(self.w("causal"), HG)
        self.strict = lambda g: bcast_mid(self.w("strict"), HG)
        self.rel = sb("rel", [128, 2, D])
        self.pos_bias = sb("pos_bias", [S, H, S])
        self.mask8 = sb("mask8", [128, T], U8)
        self.masked_cos, self.masked_sin = sb("masked_cos", [D, B, S]), sb("masked_sin", [D, B, S])
        self.q_mask, self.k_mask = sb("q_mask", [128, T], BF16), sb("k_mask", [128, T], BF16)
        self.bias_loaded, self.bias_scaled = sem("bias_loaded"), sem("bias_scaled")
        self.loaded_x, self.loaded_mamba, self.loaded_rest = sem("loaded_x"), sem("loaded_mamba"), sem("loaded_rest")
        self.stored = sem("stored")
        self.pe_steps, self.act_steps = Steps(sem("pe_steps")), Steps(sem("act_steps"))
        self.dve_steps, self.pool_steps = Steps(sem("dve_steps")), Steps(sem("pool_steps"))
        self.stats_ready, self.rstd_ready = sem("stats_ready"), sem("rstd_ready")
        self.normed, self.turned = sem("normed"), sem("turned")
        self.kq = Ring(sem("kq_copied"), 2)
        self.scored = Ring(sem("scored"), 8)
        self.shifted = Ring(sem("shifted"), 4)
        self.exped = Ring(sem("exped"), 4)
        self.p_turned = Ring(sem("p_turned"), 4)
        self.pt_copied = Ring(sem("pt_copied"), 2)
        self.weighed = Ring(sem("weighed"), 2)
        self.out_done = Ring(sem("out_done"), 2)
        self.proj, self.evac = sem("proj"), sem("evac")
        self.n_proj = self.n_evac = self.n_values = 0
        self.value_done = sem("value_done")
        self.w_loaded = [sem(f"w_loaded{e}") for e in range(2)]
        self.up_done = Ring(sem("up_done"), 2)
        self.act_done = Ring(sem("act_done"), 2)
        self.h_done = Ring(sem("h_done"), 2)
        self.y_done = Ring(sem("y_done"), 2, spare=1)
        self.added = Ring(sem("added"), 8)
        self.n_expert = self.n_unit = self.n_hunit = self.n_b2 = self.n_turn = 0
        self.logits_done, self.route_exped = sem("logits_done"), sem("route_exped")
        self.comb_turned, self.comb_copied, self.b2_done = sem("comb_turned"), sem("comb_copied"), sem("b2_done")
        self.rings = {"pool": [self.kq], "tensor": [self.scored, self.p_turned, self.weighed, self.up_done, self.y_done],
                      "vector": [self.shifted, self.out_done, self.h_done, self.added],
                      "scalar": [self.exped, self.pt_copied, self.act_done]}
        self.sem = sem

    def w(self, name, rows=slice(0, 128)):
        for table, pack in ((MAMBA_AT, self.mamba_pack), (SMALL_AT, self.small_pack)):
            if name in table:
                at, n = table[name]
                return pack[rows, at:at + n]
        raise KeyError(name)

    def row(self, name):
        at, n = ROWS_AT[name]
        return self.row_pack[:, at:at + n]


def bcast_mid(ap, n):
    return ap.unsqueeze(1).to_broadcast([ap.shape[0], n, ap.shape[1]])


def bcast_last(ap, n):
    return ap.unsqueeze(2).to_broadcast([ap.shape[0], ap.shape[1], n])


def start_stage(nc, m):
    d = m.dram
    with nc.Block() as block:
        @block.sync
        def _(sp):
            sp.dma_start(m.X[:], d["x"]).then_inc(m.loaded_x, 16)
            sp.dma_start(m.mamba_pack[:], d["mamba"]).then_inc(m.loaded_mamba, 16)
            sp.dma_start(m.small_pack[:], d["small"]).then_inc(m.loaded_rest, 16)
            sp.dma_start(m.row_pack[:], d["rows"].to_broadcast([128, ROWS_N])).then_inc(m.loaded_rest, 16)
            sp.dma_start(m.CT[:], d["ctx_feat"]).then_inc(m.loaded_rest, 16)
            sp.dma_start(m.CTOK[:], d["ctx_tok"]).then_inc(m.loaded_rest, 16)
            sp.dma_start(m.rel[:], d["rel_pos"]).then_inc(m.loaded_rest, 16)
            sp.dma_start(m.mask8[:], d["mask"].to_broadcast([128, T])).then_inc(m.loaded_rest, 16)

        @block.gpsimd
        def _(pool):
            for ring in m.rings["pool"]:
                pool.sem_inc(ring.sem, ring.start)
            nc.gpsimd.memset(m.neghalf[:], -0.5)

        @block.tensor
        def _(pe):
            for ring in m.rings["tensor"]:
                pe.sem_inc(ring.sem, ring.start)

        @block.scalar
        def _(act):
            for ring in m.rings["scalar"]:
                act.sem_inc(ring.sem, ring.start)

        @block.vector
        def _(dve):
            for ring in m.rings["vector"]:
                dve.sem_inc(ring.sem, ring.start)
            dve.wait_ge(m.loaded_x, 16)
            dve.wait_ge(m.loaded_mamba, 16)
            nc.vector.tensor_copy(m.identb[:], m.w("ident"))
            nc.vector.tensor_tensor(m.select2[:], m.w("ident")[:, 0:STATE], m.w("ident")[:, STATE:], ALU.add)


def norm_stage(nc, m, src, dst, weight=None, bias=None):
    with ExitStack() as ctx:
        norm = Norm(nc, m, ctx, src, dst, weight, bias)
        norm.emit(ctx.enter_context(nc.Block()))


class Norm:

    def __init__(self, nc, m, ctx, src, dst, weight=None, bias=None):
        n = m.n_norm
        m.n_norm += 1
        self.nc, self.m, self.n, self.src, self.dst, self.weight, self.bias = nc, m, n, src, dst, weight, bias
        self.stats = ctx.enter_context(nc.sbuf_tensor(f"stats{n}", [S, B, 6], F32))
        self.mv = ctx.enter_context(nc.sbuf_tensor(f"mv{n}", [S, B, 2], F32))
        self.ve = ctx.enter_context(nc.sbuf_tensor(f"ve{n}", [S, B], F32))
        self.rstd = ctx.enter_context(nc.sbuf_tensor(f"rstd{n}", [S, B], F32))
        self.ps = ctx.enter_context(nc.psum_tensor(f"norm_ps{n}", [D, T], F32))

    def emit(self, block, ready=(None, None)):
        nc, m, n, src, dst, ps = self.nc, self.m, self.n, self.src, self.dst, self.ps
        stats, mv, ve, rstd, weight, bias = self.stats, self.mv, self.ve, self.rstd, self.weight, self.bias
        HB = B // 2

        def copy_turned(engine, half):
            out, in_ = m.XNT[:, half * HALF:(half + 1) * HALF], ps[:, half * HALF:(half + 1) * HALF]
            if engine is nc.vector:
                if weight is None:
                    nc.vector.tensor_copy(out, in_)
                else:
                    nc.vector.tensor_scalar(out, in_, weight, bias, ALU.mult, ALU.add)
            elif weight is None:
                nc.scalar.activation(out, in_, ACT.Copy)
            else:
                nc.scalar.activation(out, in_, ACT.Identity, bias=bias, scale=weight)

        @block.vector
        def _(dve):
            for half in range(2):
                batches = range(half * HB, (half + 1) * HB)
                if ready[half] is not None:
                    dve.wait_ge(*ready[half])
                for b in batches:
                    v = m.dve_steps.inc(nc.vector.bn_stats(stats[:, b, :], src[:, b, :]))
                dve.wait_ge(m.dve_steps.sem, v)
                for b in batches:
                    v = m.dve_steps.inc(nc.vector.bn_aggr(mv[:, b, :], stats[:, b, :]))
                dve.wait_ge(m.dve_steps.sem, v)
                bs = slice(half * HB, (half + 1) * HB)
                nc.vector.tensor_scalar(ve[:, bs], mv[:, bs, 1], EPS, None, ALU.add).then_inc(m.stats_ready, 1)
            for b in range(B):
                if b % HB == 0:
                    dve.wait_ge(m.rstd_ready, 2 * n + b // HB + 1)
                nc.vector.tensor_scalar(dst[:, b, :], src[:, b, :], mv[:, b, 0:1], rstd[:, b:b + 1],
                                        ALU.subtract, ALU.mult).then_inc(m.normed, 1)
            dve.wait_ge(m.turned, 2 * n + 1)
            copy_turned(nc.vector, 0)

        @block.gpsimd
        def _(pool):
            for half in range(2):
                bs = slice(half * HB, (half + 1) * HB)
                pool.wait_ge(m.stats_ready, 2 * n + half + 1)
                nc.gpsimd.tensor_tensor(rstd[:, bs], ve[:, bs], m.neghalf[:, bs], ALU.pow).then_inc(m.rstd_ready, 1)

        @block.tensor
        def _(pe):
            for b in range(B):
                pe.wait_ge(m.normed, n * B + b + 1)
                t = nc.tensor.transpose(ps[:, b * S:(b + 1) * S], dst[:, b, :], m.w("ident"))
                if b % 4 == 3:
                    t.then_inc(m.turned, 1)

        @block.scalar
        def _(act):
            act.wait_ge(m.turned, 2 * n + 2)
            copy_turned(nc.scalar, 1)


def project(nc, m, jobs):
    with ExitStack() as ctx:
        ps = [ctx.enter_context(nc.psum_tensor(f"proj_ps{m.n_proj}_{i}", [128, HALF], F32)) for i in range(4)]
        block = ctx.enter_context(nc.Block())
        base_p, base_e = m.n_proj, m.n_evac
        units = [(j, half) for j in range(len(jobs)) for half in range(T // HALF)]
        m.n_proj += len(units)
        m.n_evac += len(units)
        cols = lambda half: slice(half * HALF, (half + 1) * HALF)

        @block.tensor
        def _(pe):
            for u, (j, half) in enumerate(units):
                weights, sources = jobs[j][1:3]
                if u >= 4:
                    pe.wait_ge(m.evac, base_e + u - 3)
                for i, (w, s) in enumerate(zip(weights, sources)):
                    t = nc.tensor.matmul(ps[u % 4][0:w.shape[1], :], w, s[:, cols(half)], start=(i == 0),
                                         stop=(i == len(weights) - 1))
                t.then_inc(m.proj, 1)

        @block.scalar
        def _(act):
            for u, (j, half) in enumerate(units):
                out, weights, sources, bias, func = (*jobs[j], None)[:5]
                act.wait_ge(m.proj, base_p + u + 1)
                in_ = ps[u % 4][0:weights[0].shape[1], :]
                out = out(half) if callable(out) else out[:, cols(half)]
                if len(out.shape) == 3:
                    in_ = in_.rearrange("p (b s) -> p b s", b=out.shape[1])
                if bias is None:
                    c = nc.scalar.activation(out, in_, func or ACT.Copy)
                else:
                    c = nc.scalar.activation(out, in_, func or ACT.Identity, bias=bias)
                c.then_inc(m.evac, 1)


def attention_inputs(nc, m, parts, V, v_source=None, v_weight=None, v_bias=None, turn=None):
    call = m.n_proj
    slots = 2 if turn else 4
    units = [(j, half) for j in range(len(parts)) for half in range(2)]
    with ExitStack() as ctx:
        ps = [[ctx.enter_context(nc.psum_tensor(f"in_ps{call}_{i}_{k}", [128, HALF], F32))
               for k in range(2 if turn else 1)] for i in range(slots)]
        pv = ctx.enter_context(nc.psum_tensor(f"val_ps{call}", [S, B, D], F32))
        if turn:
            swapped = [ctx.enter_context(nc.sbuf_tensor(f"swapped{call}_{u}", [128, B // 2, S], F32))
                       for u in range(len(units))]
        block = ctx.enter_context(nc.Block())
        base_p, base_e, base_v = m.n_proj, m.n_evac, m.n_values
        m.n_proj += len(units)
        m.n_evac += len(units)
        m.n_values += 2 if v_source is not None else 0
        cols = lambda half: slice(half * HALF, (half + 1) * HALF)
        heads = lambda a: a.rearrange("p b (h d) -> p b h d", h=H)

        @block.tensor
        def _(pe):
            def product(u):
                out, source, *weights = parts[units[u][0]]
                if u >= slots:
                    pe.wait_ge(m.evac, base_e + u - slots + 1)
                for k, w in enumerate(weights[:2 if turn else 1]):
                    t = nc.tensor.matmul(ps[u % slots][k][:], w, source[:, cols(units[u][1])], start=True, stop=True)
                t.then_inc(m.proj, 1)

            for u in range(slots):
                product(u)
            if v_source is not None:
                for b in range(B):
                    t = nc.tensor.matmul(pv[:, b, :], v_source[:, b * S:(b + 1) * S], v_weight, start=True, stop=True)
                    if b % 4 == 3:
                        t.then_inc(m.value_done, 1)
            for u in range(slots, len(units)):
                product(u)

        def copy_values(half, with_bias):
            bs = slice(4 * half, 4 * half + 4)
            out, in_ = V[:, bs, :, 0:DH], heads(pv[:, bs, :])
            if with_bias:
                bias = v_bias.rearrange("p (h d) -> p h d", h=H).unsqueeze(1).to_broadcast([S, B // 2, H, DH])
                nc.vector.tensor_tensor(out, in_, bias, ALU.add)
            else:
                nc.scalar.activation(out, in_, ACT.Copy)

        @block.vector
        def _(dve):
            if turn:
                for u, (j, half) in enumerate(units):
                    out = parts[j][0][:, cols(half)].rearrange("p (b s) -> p b s", b=B // 2)
                    product = [t[:].rearrange("p (b s) -> p b s", b=B // 2) for t in ps[u % slots]]
                    dve.wait_ge(m.proj, base_p + u + 1)
                    nc.vector.tensor_tensor(out, product[0], turn[0](half), ALU.mult)
                    nc.vector.tensor_tensor(swapped[u][:], product[1], turn[1](half), ALU.mult).then_inc(m.evac, 1)
            if v_source is None:
                nc.vector.tensor_copy(V[:, :, :, 0:DH], heads(m.XN[:]))
            elif v_bias is not None:
                for half in range(2):
                    dve.wait_ge(m.value_done, base_v + half + 1)
                    copy_values(half, True)

        @block.gpsimd
        def _(pool):
            nc.gpsimd.memset(V[:, :, :, DH:DH + 1], 1.0)
            if turn:
                for u, (j, half) in enumerate(units):
                    pool.wait_ge(m.evac, base_e + u + 1)
                    out = parts[j][0][:, cols(half)].rearrange("p (b s) -> p b s", b=B // 2)
                    nc.gpsimd.tensor_tensor(out, out, swapped[u][:], ALU.add)

        @block.scalar
        def _(act):
            if not turn:
                for u, (j, half) in enumerate(units):
                    out, bias = parts[j][0][:, cols(half)], parts[j][3]
                    act.wait_ge(m.proj, base_p + u + 1)
                    nc.scalar.activation(out, ps[u % slots][0][:], ACT.Identity, bias=bias).then_inc(m.evac, 1)
            if v_source is not None and v_bias is None:
                for half in range(2):
                    act.wait_ge(m.value_done, base_v + half + 1)
                    copy_values(half, False)


def attend(nc, m, QT, KT, V, O, bias=None, token_masks=None):
    call = m.n_attn
    m.n_attn += 1
    U0, B0 = call * B * NG, call * B
    scale = float(DH) ** -0.5
    with ExitStack() as ctx:
        sb = lambda name, shape, dt=F32: ctx.enter_context(nc.sbuf_tensor(f"{name}_a{call}", shape, dt))
        Qs = [sb(f"Qs{i}", [D, S]) for i in range(2)]
        KH = [sb(f"KH{i}", [D, H, S]) for i in range(2)]
        shifted = [sb(f"shifted{i}", [S, HG, S]) for i in range(4)]
        PTs = [sb(f"PTs{i}", [S, HG, S]) for i in range(2)]
        nmax = sb("nmax", [S, 2, HG])
        rsum = sb("rsum", [S, 2, H])
        scores = [ctx.enter_context(nc.psum_tensor(f"scores{call}_{i}", [S, HG, S], F32)) for i in range(4)]
        PT = [ctx.enter_context(nc.psum_tensor(f"PT{call}_{i}", [S, HG, S], F32)) for i in range(2)]
        PO = ctx.enter_context(nc.psum_tensor(f"PO{call}", [S, 2, HALF], F32))
        block = ctx.enter_context(nc.Block())
        ident = m.w("ident")
        SC = 2 * NG
        LAST = B // 2 - 1

        def passes(engine, body):
            with engine.Fori(0, LAST) as i:
                body(i, None)
            body(LAST, SC)

        def within(u, limit):
            return limit is None or u < limit

        @block.gpsimd
        def _(pool):
            with pool.Fori(0, B // 2) as i:
                for lane in range(2):
                    pool.wait_ge(m.scored.sem, i * SC + (U0 + NG * lane + NG))
                    at = bass.ds(i * (2 * S) + lane * S, S)
                    nc.gpsimd.tensor_copy(Qs[lane][:], QT[:, at]).then_inc(m.kq.sem, 1)
                    for g in range(NG):
                        heads = slice(g * HG, (g + 1) * HG)
                        nc.gpsimd.tensor_tensor(KH[lane][:, heads, :], bcast_mid(KT[:, at], HG),
                                                bcast_last(m.w("head_mask")[:, heads], S),
                                                ALU.mult).then_inc(m.kq.sem, 1)

        @block.tensor
        def _(pe):
            def score(i, u):
                lane, g = u // NG % 2, u % NG
                n = i * SC + (U0 + u)
                pe.wait_ge(m.kq.sem, i * (2 * (NG + 1)) + ((B0 + u // NG) * (NG + 1) + g + 2 + m.kq.depth))
                pe.wait_ge(m.shifted.sem, m.shifted.free(n))
                t = nc.tensor.matmul(scores[u % 4][:], Qs[lane][:], KH[lane][:, g * HG:(g + 1) * HG, :],
                                     start=True, stop=token_masks is None)
                if token_masks is not None:
                    qm, km = token_masks
                    at = bass.ds(i * (2 * S) + u // NG * S, S)
                    t = nc.tensor.matmul(scores[u % 4][:], qm[:, at], bcast_mid(km[:, at], HG),
                                         start=False, stop=True)
                t.then_inc(m.scored.sem, 1)

            def turn(i, u):
                n = i * SC + (U0 + u)
                pe.wait_ge(m.exped.sem, m.exped.ended(n))
                pe.wait_ge(m.pt_copied.sem, m.pt_copied.free(n))
                for j in range(HG):
                    t = nc.tensor.transpose(PT[u % 2][:, j, :], shifted[u % 4][:, j, :], ident)
                t.then_inc(m.p_turned.sem, 1)

            def weigh(i, u):
                lane, g = u // NG, u % NG
                n = i * SC + (U0 + u)
                if g == 0:
                    pe.wait_ge(m.out_done.sem, m.out_done.free(i * 2 + (B0 + lane)))
                pe.wait_ge(m.pt_copied.sem, m.pt_copied.ended(n))
                for j in range(HG):
                    h = g * HG + j
                    t = nc.tensor.matmul(PO[:, lane, h * (DH + 1):(h + 1) * (DH + 1)], PTs[u % 2][:, j, :],
                                         V[:, bass.ds(i * 2 + lane, 1), h, :].squeeze(1), start=True, stop=True)
                t.then_inc(m.weighed.sem, 1)

            def body(i, limit):
                for u in range(SC):
                    if within(u + 3, limit):
                        score(i, u + 3)
                    if within(u + 1, limit):
                        turn(i, u + 1)
                    weigh(i, u)

            for u in range(3):
                score(0, u)
            turn(0, 0)
            passes(pe, body)

        @block.vector
        def _(dve):
            def shift(i, u):
                n = i * SC + (U0 + u)
                dve.wait_ge(m.scored.sem, m.scored.ended(n))
                dve.wait_ge(m.p_turned.sem, m.p_turned.free(n))
                x = scores[u % 4][:]
                if bias is not None:
                    x = shifted[u % 4][:]
                    m.dve_steps.done(dve, nc.vector.tensor_tensor(x, scores[u % 4][:], bias(u % NG), ALU.add))
                m.dve_steps.done(dve, nc.vector.tensor_reduce(nmax[:, u % 2, :], x, AX.X, ALU.max))
                nc.vector.tensor_tensor(shifted[u % 4][:], x, bcast_last(nmax[:, u % 2, :], S),
                                        ALU.subtract).then_inc(m.shifted.sem, 1)

            def normalise(i, lane):
                n = i * SC + (U0 + NG * lane + NG - 1)
                dve.wait_ge(m.weighed.sem, m.weighed.ended(n))
                po = PO[:, lane, 0:H * (DH + 1)].rearrange("p (h e) -> p h e", h=H)
                m.dve_steps.done(dve, nc.vector.reciprocal(rsum[:, lane, :], po[:, :, DH]))
                nc.vector.tensor_tensor(
                    O[:, bass.ds(i * 2 + lane, 1), :].squeeze(1).rearrange("p (h d) -> p h d", h=H),
                    po[:, :, 0:DH], bcast_last(rsum[:, lane, :], DH), ALU.mult).then_inc(m.out_done.sem, 1)

            def body(i, limit):
                for u in range(SC):
                    if within(u + NG, limit):
                        shift(i, u + NG)
                    if u % NG == NG - 1:
                        normalise(i, u // NG)

            for u in range(NG):
                shift(0, u)
            with dve.Fori(0, LAST) as i:
                m.dve_steps.enter(i, (1 if bias is None else 2) * SC + 2)
                body(i, None)
                m.dve_steps.leave(LAST)
            body(LAST, SC)

        @block.scalar
        def _(act):
            def exp(i, u):
                n = i * SC + (U0 + u)
                act.wait_ge(m.shifted.sem, m.shifted.ended(n))
                nc.scalar.activation(shifted[u % 4][:], shifted[u % 4][:], ACT.Exp,
                                     scale=scale).then_inc(m.exped.sem, 1)

            def copy(i, u):
                n = i * SC + (U0 + u)
                act.wait_ge(m.p_turned.sem, m.p_turned.ended(n))
                act.wait_ge(m.weighed.sem, m.weighed.free(n))
                nc.scalar.activation(PTs[u % 2][:], PT[u % 2][:], ACT.Copy).then_inc(m.pt_copied.sem, 1)

            def body(i, limit):
                for u in range(SC):
                    copy(i, u)
                    if within(u + 2, limit):
                        exp(i, u + 2)

            for u in range(2):
                exp(0, u)
            passes(act, body)


def out_project(nc, m, O, weight, bias_row=None, bias_times=1.0, target=None, norm=None):
    Y = m.X if target is None else target
    n = m.n_tail
    m.n_tail += 1
    with ExitStack() as ctx:
        OT = ctx.enter_context(nc.sbuf_tensor(f"OT{n}", [D, T], F32))
        ps = ctx.enter_context(nc.psum_tensor(f"tail_t{n}", [D, T], F32))
        py = ctx.enter_context(nc.psum_tensor(f"tail_y{n}", [S, B, D], F32))
        norm = Norm(nc, m, ctx, *(norm or (m.X, m.XN)))
        block = ctx.enter_context(nc.Block())
        ready = []
        base_p, base_e = m.n_proj, m.n_evac
        m.n_proj += 4
        m.n_evac += 2
        halves = [slice(0, HALF), slice(HALF, T)]

        @block.tensor
        def _(pe):
            for b in range(B):
                t = nc.tensor.transpose(ps[:, b * S:(b + 1) * S], O[:, b, :], m.w("ident"))
                if b % 4 == 3:
                    t.then_inc(m.proj, 1)
            for b in range(B):
                if b % 4 == 0:
                    pe.wait_ge(m.evac, base_e + b // 4 + 1)
                t = nc.tensor.matmul(py[:, b, :], OT[:, b * S:(b + 1) * S], weight, start=True, stop=True)
                if b % 4 == 3:
                    t.then_inc(m.proj, 1)

        @block.scalar
        def _(act):
            for half in range(2):
                act.wait_ge(m.proj, base_p + half + 1)
                nc.scalar.activation(OT[:, halves[half]], ps[:, halves[half]], ACT.Copy).then_inc(m.evac, 1)

        @block.vector
        def _(dve):
            if bias_row is not None:
                m.dve_steps.done(dve, nc.vector.scalar_tensor_tensor(
                    out=Y[:], in0=bcast_mid(bias_row, B), scalar=bias_times, in1=Y[:], op0=ALU.mult, op1=ALU.add))
            for half in range(2):
                dve.wait_ge(m.proj, base_p + 3 + half)
                bs = slice(4 * half, 4 * half + 4)
                ready.append((m.dve_steps.sem, m.dve_steps.inc(
                    nc.vector.tensor_tensor(Y[:, bs, :], Y[:, bs, :], py[:, bs, :], ALU.add))))

        norm.emit(block, ready)


class EarlyWork:

    def __init__(self, nc, m, ctx):
        self.nc, self.m = nc, m
        self.table = ctx.enter_context(nc.sbuf_tensor("table", [128, 2, H], F32))
        self.tableT = ctx.enter_context(nc.sbuf_tensor("tableT", [H, 2 * S], F32))
        self.mask = m.O[:].rearrange("p b d -> p (b d)")
        self.ps = ctx.enter_context(nc.psum_tensor("table_ps", [H, 2 * S], F32))

    def emit(self, block):
        nc, m, table, tableT, mask, ps = self.nc, self.m, self.table, self.tableT, self.mask, self.ps
        summed, turned, copied, stored = (m.sem(n) for n in ("table_summed", "table_turned", "table_copied",
                                                             "table_stored"))
        widened, cleared = m.sem("mask_widened"), m.sem("masks_cleared")
        tab = m.dram["rel_table"]

        @block.sync
        def _(sp):
            sp.wait_ge(copied, 1)
            sp.dma_start(tab, tableT[:]).then_inc(stored, 16)
            sp.wait_ge(stored, 16)
            sp.dma_start(m.pos_bias[:], bass.AP(tab.tensor, tab.offset, [[1, S], [2 * S, H], [1, S]])
                         ).then_inc(m.bias_loaded, 16)

        @block.vector
        def _(dve):
            m.dve_steps.inc(nc.vector.memset(m.q_mask[:], 0.0))
            m.dve_steps.done(dve, nc.vector.memset(m.k_mask[:], 0.0))
            nc.vector.memset(m.q_mask[32:33, :], 1.0)
            nc.vector.memset(m.k_mask[32:33, :], -BIG).then_inc(cleared, 1)
            dve.wait_ge(m.loaded_rest, 96)
            nc.vector.tensor_reduce(table[:], m.rel[:].rearrange("p c (h d) -> p c h d", h=H), AX.X,
                                    ALU.add).then_inc(summed, 1)

        @block.tensor
        def _(pe):
            pe.wait_ge(summed, 1)
            for c in range(2):
                t = nc.tensor.transpose(ps[:, c * 128:(c + 1) * 128], table[:, c, :], m.w("ident"))
            t.then_inc(turned, 1)

        @block.scalar
        def _(act):
            act.wait_ge(turned, 1)
            nc.scalar.activation(tableT[:], ps[:], ACT.Copy).then_inc(copied, 1)
            act.wait_ge(m.loaded_rest, 96)
            nc.scalar.activation(mask, m.mask8[:], ACT.Copy).then_inc(widened, 1)
            act.wait_ge(cleared, 1)
            act.wait_ge(widened, 1)
            nc.scalar.activation(m.q_mask[0:1, :], mask[0:1, :], ACT.Copy)
            nc.scalar.activation(m.k_mask[0:1, :], mask[0:1, :], ACT.Copy, scale=BIG)

        @block.gpsimd
        def _(pool):
            pool.wait_ge(widened, 1)
            view = mask.rearrange("p (b s) -> p b s", b=B)
            for out, name in ((m.masked_cos, "rope0c"), (m.masked_sin, "rope0s")):
                nc.gpsimd.tensor_tensor(out[:], view, bcast_mid(m.w(name), B), ALU.mult)


def add_products(nc, m, terms, extra=None, bias_row=None, norm=True, early=False):
    with ExitStack() as ctx:
        py = ctx.enter_context(nc.psum_tensor(f"sum_y{m.n_proj}", [S, B, D], F32))
        norm = Norm(nc, m, ctx, m.X, m.XN) if norm else None
        early = EarlyWork(nc, m, ctx) if early else None
        block = ctx.enter_context(nc.Block())
        ready = []
        if early is not None:
            early.emit(block)
        base = m.n_proj
        m.n_proj += 2

        @block.tensor
        def _(pe):
            for b in range(B):
                for k, (source, w) in enumerate(terms):
                    t = nc.tensor.matmul(py[:, b, :], source(b), w, start=(k == 0), stop=(k == len(terms) - 1))
                if b % 4 == 3:
                    t.then_inc(m.proj, 1)

        @block.vector
        def _(dve):
            if extra is not None:
                m.dve_steps.done(dve, nc.vector.tensor_tensor(m.X[:], m.X[:], extra, ALU.add))
            if bias_row is not None:
                m.dve_steps.done(dve, nc.vector.tensor_tensor(m.X[:], m.X[:], bcast_mid(bias_row, B), ALU.add))
            for half in range(2):
                dve.wait_ge(m.proj, base + half + 1)
                bs = slice(4 * half, 4 * half + 4)
                ready.append((m.dve_steps.sem, m.dve_steps.inc(
                    nc.vector.tensor_tensor(m.X[:, bs, :], m.X[:, bs, :], py[:, bs, :], ALU.add))))

        if norm is not None:
            norm.emit(block, ready)


def mamba_stage(nc, m):
    norm_stage(nc, m, m.X, m.XN)
    norm_stage(nc, m, m.XN, m.O, m.w("ln_w"), m.w("ln_b"))
    with ExitStack() as outer:
        sb = lambda name, shape, dt=F32: outer.enter_context(nc.sbuf_tensor(name, shape, dt))
        u = sb("u", [128, IC, T])
        gate = sb("gate", [128, IC, T])
        delta = sb("delta", [128, IC, T])
        du = sb("du", [128, IC, T])
        A = sb("A", [128, IC, STATE])
        BC = [sb(f"BC{i}", [2 * STATE, T], BF16) for i in range(3)]
        y = sb("y", [128, IC, T])

        with ExitStack() as ctx:
            pre = lambda name, shape, dt=F32: ctx.enter_context(nc.sbuf_tensor(name, shape, dt))
            padded = [pre(f"padded{c}", [128, B, S + TAPS - 1]) for c in range(IC)]
            conv = pre("conv", [128, IC, T])
            BCf = pre("BCf", [2 * STATE, T])
            dt_low = pre("dt_low", [RANK, T])
            conv_w = m.w("conv_w").rearrange("p (c k) -> p c k", c=IC)
            with nc.Block() as block:
                @block.gpsimd
                def _(pool):
                    for c in range(IC):
                        nc.gpsimd.memset(padded[c][:, :, 0:TAPS - 1], 0.0)
            W_in = m.w("W_in")
            jobs = [((lambda half, c=c: padded[c][:, 4 * half:4 * half + 4, TAPS - 1:]),
                     [W_in[:, c * 128:(c + 1) * 128]], [m.XNT[:]], None) for c in range(IC)]
            jobs += [(gate[:, c, :], [W_in[:, INNER + c * 128:INNER + (c + 1) * 128]], [m.XNT[:]], None, ACT.Silu)
                     for c in range(IC)]
            project(nc, m, jobs)

            with nc.Block() as block:
                @block.vector
                def _(dve):
                    for k in range(TAPS):
                        for c in range(IC):
                            out = conv[:, c, :].rearrange("p (b s) -> p b s", b=B)
                            tap = padded[c][:, :, k:k + S]
                            if k == 0:
                                t = nc.vector.tensor_scalar(out, tap, conv_w[:, c, 0:1], m.w("conv_b")[:, c:c + 1],
                                                            ALU.mult, ALU.add)
                            else:
                                t = nc.vector.scalar_tensor_tensor(out=out, in0=tap, scalar=conv_w[:, c, k:k + 1],
                                                                   in1=out, op0=ALU.mult, op1=ALU.add)
                            v = m.dve_steps.inc(t)
                        dve.wait_ge(m.dve_steps.sem, v)
                v_conv = m.dve_steps.n

                @block.scalar
                def _(act):
                    act.wait_ge(m.dve_steps.sem, v_conv)
                    nc.scalar.activation(u[:], conv[:], ACT.Silu)

            W_x = m.w("W_xproj").rearrange("p (c n) -> p c n", c=IC)
            project(nc, m, [(dt_low[:], [W_x[:, c, 0:RANK] for c in range(IC)], [u[:, c, :] for c in range(IC)], None),
                            (BCf[:], [W_x[:, c, RANK:] for c in range(IC)], [u[:, c, :] for c in range(IC)], None)])
            W_dt = m.w("W_dt", slice(0, RANK))
            project(nc, m, [(delta[:, c, :], [W_dt[:, c * 128:(c + 1) * 128]], [dt_low[:]], m.w("b_dt")[:, c:c + 1])
                            for c in range(IC)])
            softplus_and_split(nc, m, delta, u, du, A, BC, BCf, ctx)
        scan_block(nc, m, outer, delta, du, A, BC, y)

        with nc.Block() as block:
            @block.vector
            def _(dve):
                for c in range(IC):
                    v = m.dve_steps.inc(nc.vector.scalar_tensor_tensor(
                        out=y[:, c, :], in0=u[:, c, :], scalar=m.w("Dskip")[:, c:c + 1], in1=y[:, c, :],
                        op0=ALU.mult, op1=ALU.add))
                dve.wait_ge(m.dve_steps.sem, v)
                nc.vector.tensor_tensor(y[:], y[:], gate[:], ALU.mult)
        W_out = m.w("W_out").rearrange("p (c n) -> p c n", c=IC)
        add_products(nc, m, [((lambda b, c=c: y[:, c, b * S:(b + 1) * S]), W_out[:, c, :]) for c in range(IC)],
                     extra=m.XN[:], early=True)


def softplus_and_split(nc, m, delta, u, du, A, BC, BCf, ctx):
    pre = lambda name, shape, dt=F32: ctx.enter_context(nc.sbuf_tensor(name, shape, dt))
    low, e, w, ln_w = (pre(name, [128, IC, T]) for name in ("low", "e", "w", "ln_w_"))
    rest, mid = pre("rest", [2 * STATE, T]), pre("mid", [2 * STATE, T], BF16)
    e_ready, w_ready, ln_ready, low_ready = (m.sem(n) for n in ("e_ready", "w_ready", "ln_ready", "low_ready"))
    high_ready, rest_ready, mid_ready = (m.sem(n) for n in ("high_ready", "rest_ready", "mid_ready"))
    is_b, is_c = slice(0, STATE), slice(STATE, 2 * STATE)
    with nc.Block() as block:
        @block.vector
        def _(dve):
            steps = m.dve_steps
            both = range(IC)
            for c in both:
                nc.vector.scalar_tensor_tensor(out=low[:, c, :], in0=delta[:, c, :], scalar=-1.0, in1=delta[:, c, :],
                                               op0=ALU.mult, op1=ALU.min).then_inc(low_ready, 1)
            for c in both:
                dve.wait_ge(e_ready, c + 1)
                nc.vector.tensor_scalar(w[:, c, :], e[:, c, :], 1.0, None, ALU.add).then_inc(w_ready, 1)
            for c in both:
                dve.wait_ge(w_ready, c + 1)
                v = steps.inc(nc.vector.scalar_tensor_tensor(out=low[:, c, :], in0=w[:, c, :], scalar=-1.0,
                                                             in1=e[:, c, :], op0=ALU.add, op1=ALU.subtract))
            for c in both:
                dve.wait_ge(steps.sem, v - 1 + c)
                dve.wait_ge(ln_ready, c + 1)
                steps.inc(nc.vector.tensor_tensor(low[:, c, :], ln_w[:, c, :], low[:, c, :], ALU.subtract))
            for c in both:
                dve.wait_ge(steps.sem, v + 1 + c)
                steps.inc(nc.vector.scalar_tensor_tensor(out=delta[:, c, :], in0=delta[:, c, :], scalar=0.0,
                                                         in1=low[:, c, :], op0=ALU.max, op1=ALU.add))
            for c in both:
                dve.wait_ge(steps.sem, v + 3 + c)
                nc.vector.tensor_tensor(du[:, c, :], delta[:, c, :], u[:, c, :], ALU.mult)

        @block.scalar
        def _(act):
            steps = m.act_steps
            for rows, out in ((is_b, BC[0]), (is_c, BC[1])):
                nc.scalar.activation(out[rows, :], BCf[rows, :], ACT.Copy).then_inc(high_ready, 1)
            a = A[:].rearrange("p c n -> p (c n)")
            steps.done(act, nc.scalar.activation(a, m.w("A_log"), ACT.Exp))
            nc.scalar.activation(a, a, ACT.Copy, scale=-1.0)
            for c in range(IC):
                act.wait_ge(low_ready, c + 1)
                nc.scalar.activation(e[:, c, :], low[:, c, :], ACT.Exp).then_inc(e_ready, 1)
            for c in range(IC):
                act.wait_ge(w_ready, c + 1)
                nc.scalar.activation(ln_w[:, c, :], w[:, c, :], ACT.Ln).then_inc(ln_ready, 1)
            act.wait_ge(rest_ready, 2)
            nc.scalar.activation(mid[:], rest[:], ACT.Copy).then_inc(mid_ready, 1)
            act.wait_ge(mid_ready, 1)
            nc.scalar.activation(BC[0][is_c, :], mid[is_b, :], ACT.Copy)
            nc.scalar.activation(BC[1][is_b, :], mid[is_c, :], ACT.Copy)

        @block.gpsimd
        def _(pool):
            for k, (rows, high) in enumerate(((is_b, BC[0]), (is_c, BC[1]))):
                pool.wait_ge(high_ready, k + 1)
                nc.gpsimd.tensor_tensor(rest[rows, :], BCf[rows, :], high[rows, :], ALU.subtract).then_inc(rest_ready, 1)
            pool.wait_ge(mid_ready, 1)
            nc.gpsimd.tensor_tensor(BC[2][:], rest[:], mid[:], ALU.subtract)


def scan_block(nc, m, outer, delta, du, A, BC, y):
    sb = lambda name, shape, dt=F32: outer.enter_context(nc.sbuf_tensor(name, shape, dt))
    decay = [[sb(f"decay{c}{p}", [128, B, S]) for p in range(2)] for c in range(IC)]
    inp = [sb(f"inp{c}", [128, T]) for c in range(IC)]
    h = [[sb(f"h{c}{p}", [128, T]) for p in range(2)] for c in range(IC)]
    hC = [[sb(f"hC{c}{p}", [128, T]) for p in range(2)] for c in range(IC)]
    Cs = [sb(f"Cs{p}", [128, T]) for p in range(2)]
    ps_ctx = ExitStack()
    Bp = ps_ctx.enter_context(nc.psum_tensor("Bp", [128, T], F32))
    Cp = ps_ctx.enter_context(nc.psum_tensor("Cp", [128, T], F32))
    Y = [ps_ctx.enter_context(nc.psum_tensor(f"Y{c}", [128, T], F32)) for c in range(IC)]
    PASS = 4
    spread_b, spread_c = Ring(m.sem("spread_b"), 1), Ring(m.sem("spread_c"), 1)
    c_copied, decayed = Ring(m.sem("c_copied"), 2), Ring(m.sem("decayed"), 4)
    fed, scanned, weighed = Ring(m.sem("fed"), 4), Ring(m.sem("scanned"), 4), Ring(m.sem("c_weighed"), 4)
    first_summed, others_summed, summed1 = m.sem("first_summed"), m.sem("others_summed"), m.sem("summed1")
    halves = [slice(0, HALF), slice(HALF, T)]
    with nc.Block() as block:
        @block.gpsimd
        def _(pool):
            for ring in (weighed,):
                pool.sem_inc(ring.sem, ring.start)
            for c in range(IC):
                for p in range(2):
                    nc.gpsimd.memset(decay[c][p][:], 0.0)
                    nc.gpsimd.memset(hC[c][p][:], 0.0)
            nc.gpsimd.memset(y[:, 0, :], 0.0)

        @block.tensor
        def _(pe):
            for ring in (spread_b, spread_c):
                pe.sem_inc(ring.sem, ring.start)

        @block.scalar
        def _(act):
            for ring in (c_copied, decayed):
                act.sem_inc(ring.sem, ring.start)

        @block.vector
        def _(dve):
            for ring in (fed, scanned):
                dve.sem_inc(ring.sem, ring.start)
            dve.sem_inc(first_summed, 1)

    with nc.Block() as block:
        @block.tensor
        def _(pe):
            def spread(out, n, c):
                for half in range(2):
                    for part, row in ((m.select2[:, bass.ds(n, 1)], BC[c]),
                                      (m.identb[:, bass.ds(n + c * STATE, 1)], BC[2])):
                        t = nc.tensor.matmul(out[:, halves[half]], part.to_broadcast([128, 128]),
                                             row[:, halves[half]], start=(row is BC[c]), stop=(row is BC[2]))
                return t

            def add(c, p, start=False, stop=False):
                for half in range(2):
                    t = nc.tensor.matmul(Y[c][:, halves[half]], m.w("ident"), hC[c][p][:, halves[half]],
                                         start=start, stop=stop, skip_group_check=True)
                return t

            for c in range(IC):
                add(c, 1, start=True)
            with pe.Fori(0, STATE // PASS) as i:
                for k in range(PASS):
                    n, p = i * PASS + k, k % 2
                    if k != 2:
                        pe.wait_ge(weighed.sem, i * (2 * PASS) + (2 * k + 1))
                        add(0, p).then_inc(others_summed, 1)
                    pe.wait_ge(fed.sem, i * (2 * PASS) + (2 * k + 4))
                    spread(Bp, n, 0).then_inc(spread_b.sem, 1)
                    pe.wait_ge(c_copied.sem, n + 2)
                    spread(Cp, n, 1).then_inc(spread_c.sem, 1)
                    pe.wait_ge(weighed.sem, i * (2 * PASS) + (2 * k + 2))
                    add(1, p).then_inc(summed1, 1)
            pe.wait_ge(weighed.sem, 2 * STATE + weighed.depth)
            for c in range(IC):
                add(c, 0)
                t = add(c, 1, stop=True)
            t.then_inc(summed1, 1)

        @block.scalar
        def _(act):
            with act.Fori(0, STATE // PASS) as i:
                for k in range(PASS):
                    n, p = i * PASS + k, k % 2
                    for c in range(IC):
                        use = i * (2 * PASS) + (2 * k + c)
                        act.wait_ge(scanned.sem, scanned.free(use))
                        nc.scalar.activation(
                            decay[c][p][:, :, 1:S], delta[:, c, :].rearrange("p (b s) -> p b s", b=B)[:, :, 1:S],
                            ACT.Exp, scale=A[:, c, bass.ds(n, 1)]).then_inc(decayed.sem, 1)
                        if c == 0:
                            act.wait_ge(spread_c.sem, spread_c.ended(n))
                            act.wait_ge(weighed.sem, i * (2 * PASS) + (2 * k + 2))
                            nc.scalar.activation(Cs[p][:], Cp[:], ACT.Copy).then_inc(c_copied.sem, 1)

        @block.vector
        def _(dve):
            with dve.Fori(0, STATE // PASS) as i:
                for k in range(PASS):
                    n, p = i * PASS + k, k % 2
                    dve.wait_ge(spread_b.sem, spread_b.ended(n))
                    for c in range(IC):
                        use = i * (2 * PASS) + (2 * k + c)
                        dve.wait_ge(scanned.sem, scanned.ended(use) - 2)
                        nc.vector.tensor_tensor(inp[c][:], du[:, c, :], Bp[:], ALU.mult).then_inc(fed.sem, 1)
                    for c in range(IC):
                        use = i * (2 * PASS) + (2 * k + c)
                        dve.wait_ge(fed.sem, fed.ended(use))
                        dve.wait_ge(decayed.sem, decayed.ended(use))
                        dve.wait_ge(weighed.sem, weighed.free(use))
                        nc.vector.tensor_tensor_scan(
                            h[c][p][:], decay[c][p][:].rearrange("p b s -> p (b s)"), inp[c][:], 0.0,
                            ALU.mult, ALU.add).then_inc(scanned.sem, 1)
                    if k == 1:
                        dve.wait_ge(weighed.sem, i * (2 * PASS) + (2 * k - 1 + weighed.depth))
                        dve.wait_ge(first_summed, i + 1)
                        nc.vector.tensor_tensor(y[:, 0, :], y[:, 0, :], hC[0][0][:], ALU.add).then_inc(first_summed, 1)
            dve.wait_ge(first_summed, STATE // PASS + 1)
            dve.wait_ge(summed1, STATE + 1)
            nc.vector.tensor_tensor(y[:, 0, :], y[:, 0, :], Y[0][:], ALU.add)
            nc.vector.tensor_copy(y[:, 1, :], Y[1][:])

        @block.gpsimd
        def _(pool):
            with pool.Fori(0, STATE // PASS) as i:
                for k in range(PASS):
                    n, p = i * PASS + k, k % 2
                    pool.wait_ge(c_copied.sem, c_copied.ended(n))
                    for c in range(IC):
                        use = i * (2 * PASS) + (2 * k + c)
                        pool.wait_ge(scanned.sem, scanned.ended(use))
                        if c == 1:
                            pool.wait_ge(summed1, n + 1)
                        elif k == 2:
                            pool.wait_ge(first_summed, i + 2)
                        else:
                            pool.wait_ge(others_summed, i * (PASS - 1) + (k + 1 - k // 2))
                        nc.gpsimd.tensor_tensor(hC[c][p][:], h[c][p][:], Cs[p][:], ALU.mult).then_inc(weighed.sem, 1)
    ps_ctx.close()


class Route:

    def __init__(self, nc, m, ctx, E, weight, kind, comb, rows=()):
        self.nc, self.m, self.E, self.weight, self.kind, self.comb, self.rows = nc, m, E, weight, kind, comb, rows
        self.n = n = m.n_route
        m.n_route += 1
        self.EP = EP = 16 if E > 8 else 8
        sb = lambda name, shape, dt=F32: ctx.enter_context(nc.sbuf_tensor(f"{name}_r{n}", shape, dt))
        self.val, self.eq = sb("val", [S, B, EP]), sb("eq", [S, B, EP])
        self.best, self.index = sb("best", [S, B, 8]), sb("index", [S, B, 8], U32)
        self.indexf, self.wt, self.tmp = sb("indexf", [S, B, 2]), sb("wt", [S, B, 2]), sb("tmp", [S, B])
        self.ps = ctx.enter_context(nc.psum_tensor(f"logits{n}", [S, B, EP], F32))

    def emit(self, block):
        nc, m, n, E, EP, kind, comb = self.nc, self.m, self.n, self.E, self.EP, self.kind, self.comb
        val, eq, best, index, indexf = self.val, self.eq, self.best, self.index, self.indexf
        wt, tmp, ps = self.wt, self.tmp, self.ps
        v = {}

        @block.vector
        def _(dve):
            steps = m.dve_steps
            dve.wait_ge(m.logits_done, n + 1)
            if kind == "sigmoid":
                dve.wait_ge(m.route_exped, n + 1)
                steps.done(dve, nc.vector.tensor_scalar(val[:], val[:], 1.0, None, ALU.add))
                steps.done(dve, nc.vector.reciprocal(val[:], val[:]))
            elif kind == "softmax_all":
                steps.done(dve, nc.vector.memset(val[:], -1.0))
                steps.done(dve, nc.vector.tensor_reduce(tmp[:], ps[:, :, 0:E], AX.X, ALU.max))
                v["shifted"] = steps.inc(nc.vector.tensor_tensor(val[:, :, 0:E], ps[:, :, 0:E], bcast_last(tmp[:], E),
                                                                 ALU.subtract))
                dve.wait_ge(m.route_exped, n + 1)
                steps.done(dve, nc.vector.tensor_reduce(tmp[:], val[:, :, 0:E], AX.X, ALU.add))
                steps.done(dve, nc.vector.reciprocal(tmp[:], tmp[:]))
                steps.done(dve, nc.vector.tensor_tensor(val[:, :, 0:E], val[:, :, 0:E], bcast_last(tmp[:], E),
                                                        ALU.mult))
            else:
                steps.done(dve, nc.vector.tensor_copy(val[:], ps[:]))
                for row in self.rows:
                    steps.done(dve, nc.vector.tensor_tensor(val[:], val[:], bcast_mid(row, B), ALU.add))
            for b in range(B):
                k = steps.inc(nc.vector.max(best[:, b, :], val[:, b, :]))
            dve.wait_ge(steps.sem, k)
            if kind == "softmax_two":
                v["second"] = steps.inc(nc.vector.tensor_tensor(tmp[:], best[:, :, 1], best[:, :, 0], ALU.subtract))
            for b in range(B):
                k = steps.inc(nc.vector.max_index(index[:, b, :], best[:, b, :], val[:, b, :]))
            dve.wait_ge(steps.sem, k)
            steps.done(dve, nc.vector.tensor_copy(indexf[:], index[:, :, 0:2]))
            if kind in ("sigmoid", "softmax_all"):
                eps, times = (1e-20, 2.5) if kind == "sigmoid" else (1e-9, 1.0)
                steps.done(dve, nc.vector.scalar_tensor_tensor(out=tmp[:], in0=best[:, :, 0], scalar=eps,
                                                               in1=best[:, :, 1], op0=ALU.add, op1=ALU.add))
                steps.done(dve, nc.vector.reciprocal(tmp[:], tmp[:]))
                for k in range(2):
                    steps.done(dve, nc.vector.scalar_tensor_tensor(
                        out=wt[:, :, k], in0=best[:, :, k], scalar=times, in1=tmp[:], op0=ALU.mult, op1=ALU.mult))
            else:
                dve.wait_ge(m.route_exped, n + 1)
                steps.done(dve, nc.vector.tensor_scalar(wt[:, :, 0], tmp[:], 1.0, None, ALU.add))
                steps.done(dve, nc.vector.reciprocal(wt[:, :, 0], wt[:, :, 0]))
                steps.done(dve, nc.vector.tensor_tensor(wt[:, :, 1], wt[:, :, 0], tmp[:], ALU.mult))
            for k in range(2):
                out = comb if k == 0 else eq[:]
                steps.done(dve, nc.vector.tensor_tensor(out, bcast_mid(m.w("iota16")[:, 0:EP], B),
                                                        bcast_last(indexf[:, :, k], EP), ALU.is_equal))
                steps.done(dve, nc.vector.tensor_tensor(out, out, bcast_last(wt[:, :, k], EP), ALU.mult))
            steps.done(dve, nc.vector.tensor_tensor(comb, comb, eq[:], ALU.add))
            if kind == "softmax_all":
                steps.done(dve, nc.vector.memset(comb[:, :, E:E + 1], 1.0))
        self.comb_value = m.dve_steps.n

        @block.tensor
        def _(pe):
            for b in range(B):
                t = nc.tensor.matmul(ps[:, b, 0:E], m.XNT[:, b * S:(b + 1) * S], self.weight, start=True, stop=True)
            t.then_inc(m.logits_done, 1)

        @block.scalar
        def _(act):
            if kind == "sigmoid":
                act.wait_ge(m.logits_done, n + 1)
                t = nc.scalar.activation(val[:], ps[:], ACT.Exp, scale=-1.0)
            elif kind == "softmax_all":
                act.wait_ge(m.dve_steps.sem, v["shifted"])
                t = nc.scalar.activation(val[:, :, 0:E], val[:, :, 0:E], ACT.Exp)
            else:
                act.wait_ge(m.dve_steps.sem, v["second"])
                t = nc.scalar.activation(tmp[:], tmp[:], ACT.Exp)
            t.then_inc(m.route_exped, 1)


def expert_stage(nc, m, layer, routed, FC, kind, func, weights, rows=(), b2=None, gated=False, last=False):
    E = 8 if gated else routed
    EP = 16 if E > 8 else 8
    E0, S0, U0, H0 = m.n_expert, 2 * m.n_expert, m.n_unit, m.n_hunit
    m.n_expert += E
    m.n_unit += 2 * E * FC
    m.n_hunit += 2 * E * FC if gated else 0
    call = m.n_moe
    m.n_moe += 1
    F = FC * 128
    down = 2 * F if gated else F
    with ExitStack() as ctx:
        sb = lambda name, shape, dt=F32: ctx.enter_context(nc.sbuf_tensor(f"{name}_e{call}", shape, dt))
        comb = sb("comb", [S, B, EP])
        route = Route(nc, m, ctx, routed, m.w(f"{layer}_router"), kind, comb[:], rows)
        W = [sb(f"W{i}", [128, down + F + (0 if gated else FC)]) for i in range(2)]
        hid = [sb(f"hid{i}", [128, FC, HALF]) for i in range(2)]
        silu = [sb(f"silu{i}", [128, HALF]) for i in range(2)]
        G = [ctx.enter_context(nc.psum_tensor(f"G{call}_{i}", [128, HALF], F32)) for i in range(2)]
        U = [ctx.enter_context(nc.psum_tensor(f"U{call}_{i}", [128, HALF], F32)) for i in range(2)] if gated else G
        Y = [ctx.enter_context(nc.psum_tensor(f"Y{call}_{i}", [S, B // 2, D], F32)) for i in range(2)]
        norm = None if last else Norm(nc, m, ctx, m.X, m.XN)
        block = ctx.enter_context(nc.Block())
        route.emit(block)
        unit = lambda i, s, fc: i * (4 * FC) + (s * FC + fc)
        order = [("up", 0), ("up", 1), ("down", 0), ("up", 2), ("down", 1), ("up", 3), ("down", 2), ("down", 3)]

        @block.sync
        def _(sp):
            with sp.Fori(0, E // 2) as i:
                for e in range(2):
                    sp.wait_ge(m.y_done.sem, i * 4 + m.y_done.ended(S0 + 2 * e - 3))
                    sp.dma_start(W[e][:], weights[bass.ds(i * 2 + e, 1)].squeeze(0)).then_inc(m.w_loaded[e], 16)

        @block.tensor
        def _(pe):
            with pe.Fori(0, E // 2) as i:
                def up(s):
                    e, half = s // 2, s % 2
                    if half == 0:
                        pe.wait_ge(m.w_loaded[e], i * 16 + 16 * (E0 // 2 + 1))
                    for fc in range(FC):
                        u = unit(i, s, fc)
                        pe.wait_ge(m.act_done.sem, m.act_done.free(u + U0))
                        at = slice(fc * 128, (fc + 1) * 128)
                        cols = slice(half * HALF, (half + 1) * HALF)
                        t = nc.tensor.matmul(G[fc % 2][:], W[e][:, at], m.XNT[:, cols], start=True, stop=True)
                        if gated:
                            pe.wait_ge(m.h_done.sem, m.h_done.free(u + H0))
                            at = slice(F + fc * 128, F + (fc + 1) * 128)
                            t = nc.tensor.matmul(U[fc % 2][:], W[e][:, at], m.XNT[:, cols], start=True, stop=True)
                        t.then_inc(m.up_done.sem, 1)

                def to_down(s):
                    e = s // 2
                    last = unit(i, s, FC - 1)
                    if gated:
                        pe.wait_ge(m.h_done.sem, m.h_done.ended(last + H0))
                    else:
                        pe.wait_ge(m.act_done.sem, m.act_done.ended(last + U0))
                    pe.wait_ge(m.added.sem, m.added.free(i * 16 + (4 * (S0 + s) + 3)))
                    for b in range(B // 2):
                        for fc in range(FC):
                            t = nc.tensor.matmul(Y[s % 2][:, b, :], hid[s % 2][:, fc, b * S:(b + 1) * S],
                                                 W[e][:, down + fc * 128:down + (fc + 1) * 128],
                                                 start=(fc == 0), stop=(fc == FC - 1))
                    t.then_inc(m.y_done.sem, 1)

                for what, s in order:
                    (up if what == "up" else to_down)(s)

        @block.scalar
        def _(act):
            with act.Fori(0, E // 2) as i:
                for s in range(4):
                    for fc in range(FC):
                        u = unit(i, s, fc)
                        act.wait_ge(m.up_done.sem, m.up_done.ended(u + U0))
                        if gated:
                            act.wait_ge(m.h_done.sem, m.h_done.free(u + H0))
                            t = nc.scalar.activation(silu[fc % 2][:], G[fc % 2][:], func)
                        else:
                            if fc == 0:
                                act.wait_ge(m.y_done.sem, m.y_done.free(i * 4 + (S0 + s)))
                            t = nc.scalar.activation(hid[s % 2][:, fc, :], G[fc % 2][:], func,
                                                     bias=W[s // 2][:, down + F + fc:down + F + fc + 1])
                        t.then_inc(m.act_done.sem, 1)

        @block.vector
        def _(dve):
            with dve.Fori(0, E // 2) as i:
                def gate(s):
                    for fc in range(FC):
                        u = unit(i, s, fc)
                        if fc == 0:
                            dve.wait_ge(m.y_done.sem, m.y_done.free(i * 4 + (S0 + s)))
                        dve.wait_ge(m.act_done.sem, m.act_done.ended(u + U0))
                        nc.vector.tensor_tensor(hid[s % 2][:, fc, :], silu[fc % 2][:], U[fc % 2][:],
                                                ALU.mult).then_inc(m.h_done.sem, 1)

                def add(s):
                    n = i * 16 + 4 * (S0 + s)
                    dve.wait_ge(m.y_done.sem, m.y_done.ended(i * 4 + (S0 + s)))
                    dve.wait_ge(m.added.sem, m.added.ended(n - 1))
                    for b in range(B // 2):
                        x = m.X[:, (s % 2) * (B // 2) + b, :]
                        at = i * 2 + ((s % 2) * (B // 2) + b) * EP + s // 2
                        nc.vector.scalar_tensor_tensor(
                            out=x, in0=Y[s % 2][:, b, :], scalar=comb[:].rearrange("p b e -> p (b e)")[:, bass.ds(at, 1)],
                            in1=x, op0=ALU.mult, op1=ALU.add).then_inc(m.added.sem, 1)

                for what, s in order:
                    if what == "down":
                        add(s)
                    elif gated:
                        gate(s)

        done = m.added.ended(8 * (E0 + E) - 1)
        ready = ((m.added.sem, done - 4), (m.added.sem, done))
        if b2 is not None:
            combT = sb("combT", [EP, T])
            k, k2 = m.n_turn, m.n_b2
            m.n_turn += 2
            m.n_b2 += 2
            ready = []

            @block.tensor
            def _(pe):
                pe.wait_ge(m.dve_steps.sem, route.comb_value)
                for b in range(B):
                    t = nc.tensor.transpose(norm.ps[0:EP, b * S:(b + 1) * S], comb[:, b, :], m.w("ident"))
                    if b % 4 == 3:
                        t.then_inc(m.comb_turned, 1)
                pe.wait_ge(m.act_done.sem, m.act_done.ended(2 * E * FC - 1 + U0))
                for b in range(B):
                    if b % 4 == 0:
                        pe.wait_ge(m.comb_copied, k + b // 4 + 1)
                    t = nc.tensor.matmul(G[b // 4][:, b % 4 * D:(b % 4 + 1) * D], combT[:, b * S:(b + 1) * S], b2,
                                         start=True, stop=True)
                    if b % 4 == 3:
                        t.then_inc(m.b2_done, 1)

            @block.scalar
            def _(act):
                for half in range(2):
                    act.wait_ge(m.comb_turned, k + half + 1)
                    cols = slice(half * HALF, (half + 1) * HALF)
                    nc.scalar.activation(combT[:, cols], norm.ps[0:EP, cols], ACT.Copy).then_inc(m.comb_copied, 1)

            @block.vector
            def _(dve):
                dve.wait_ge(m.added.sem, done)
                for half in range(2):
                    dve.wait_ge(m.b2_done, k2 + half + 1)
                    x = m.X[:, half * (B // 2):(half + 1) * (B // 2), :]
                    term = G[half][:].rearrange("p (b d) -> p b d", b=B // 2)
                    ready.append((m.dve_steps.sem, m.dve_steps.inc(nc.vector.tensor_tensor(x, x, term, ALU.add))))
        if norm is not None:
            norm.emit(block, ready)


def ffn0_stage(nc, m):
    C, EC = 5, 4
    units = [(c, half) for c in range(C) for half in range(2)]
    spreads = [(c, half) for c in range(EC) for half in range(2)]
    cols = lambda half: slice(half * HALF, (half + 1) * HALF)
    with ExitStack() as ctx:
        sb = lambda name, shape, dt=F32: ctx.enter_context(nc.sbuf_tensor(f"{name}_f0", shape, dt))
        comb, combT = sb("comb", [S, B, 8]), sb("combT", [128, T])
        hid, up = sb("hid", [128, C, T]), sb("up", [128, C, T])
        wg, wu, wd = (m.w(f"L0f_{k}") for k in "gud")
        at = lambda c: slice(c * 128, (c + 1) * 128)
        hid_ready, spread_done, spread_used = (m.sem(n) for n in ("f0_hidden", "f0_spread", "f0_spread_used"))
        with ExitStack() as inner:
            psum = lambda name: [inner.enter_context(nc.psum_tensor(f"{name}_f0_{i}", [128, HALF], F32))
                                 for i in range(2)]
            G, U, P = psum("G"), psum("U"), psum("P")
            route = Route(nc, m, inner, 8, m.w("L0f_router"), "sigmoid", comb[:])
            block = inner.enter_context(nc.Block())
            base_p, base_e = m.n_proj, m.n_evac
            m.n_proj += len(units)
            m.n_evac += len(units)
            k = m.n_turn
            m.n_turn += 2
            route.emit(block)

            @block.tensor
            def _(pe):
                for u, (c, half) in enumerate(units):
                    if u >= 2:
                        pe.wait_ge(m.evac, base_e + u - 1)
                    for ps, w in ((G, wg), (U, wu)):
                        t = nc.tensor.matmul(ps[u % 2][:], w[:, at(c)], m.XNT[:, cols(half)], start=True, stop=True)
                    t.then_inc(m.proj, 1)
                    if u == 5:
                        pe.wait_ge(m.dve_steps.sem, route.comb_value)
                        for b in range(B):
                            t = nc.tensor.transpose(P[b // 4][0:8, b % 4 * S:(b % 4 + 1) * S], comb[:, b, :],
                                                    m.w("ident"))
                            if b % 4 == 3:
                                t.then_inc(m.comb_turned, 1)
                pe.wait_ge(m.comb_copied, k + 2)
                for u, (c, half) in enumerate(spreads):
                    if u >= 2:
                        pe.wait_ge(spread_used, u - 1)
                    nc.tensor.matmul(P[u % 2][:], m.w("L0f_sel")[:, at(c)], combT[:, cols(half)], start=True,
                                     stop=True).then_inc(spread_done, 1)

            @block.scalar
            def _(act):
                for u, (c, half) in enumerate(units):
                    act.wait_ge(m.proj, base_p + u + 1)
                    nc.scalar.activation(hid[:, c, cols(half)], G[u % 2][:], ACT.Silu)
                    nc.scalar.activation(up[:, c, cols(half)], U[u % 2][:], ACT.Copy).then_inc(m.evac, 1)

            @block.gpsimd
            def _(pool):
                for u, (c, half) in enumerate(units):
                    pool.wait_ge(m.evac, base_e + u + 1)
                    x = hid[:, c, cols(half)]
                    nc.gpsimd.tensor_tensor(x, x, up[:, c, cols(half)], ALU.mult).then_inc(hid_ready, 1)

            @block.vector
            def _(dve):
                m.dve_steps.done(dve, nc.vector.memset(combT[:], 0.0))
                for half in range(2):
                    dve.wait_ge(m.comb_turned, k + half + 1)
                    nc.vector.tensor_copy(combT[0:8, cols(half)], P[half][0:8, :]).then_inc(m.comb_copied, 1)
                for u, (c, half) in enumerate(spreads):
                    dve.wait_ge(spread_done, u + 1)
                    dve.wait_ge(hid_ready, u + 1)
                    x = hid[:, c, cols(half)]
                    nc.vector.tensor_tensor(x, x, P[u % 2][:], ALU.mult).then_inc(spread_used, 1)
        add_products(nc, m, [((lambda b, c=c: hid[:, c, b * S:(b + 1) * S]), wd[:, at(c)]) for c in range(C)])


def cross_attention0(nc, m):
    with ExitStack() as ctx:
        sb = lambda name, shape, dt=F32: ctx.enter_context(nc.sbuf_tensor(f"{name}_x0", shape, dt))
        QT, KT = sb("QT", [D, T]), sb("KT", [D, T])
        V = sb("V", [S, B, H, DH + 1])
        four = lambda a: (lambda half: a[:, half * (B // 2):(half + 1) * (B // 2), :])
        attention_inputs(nc, m, [(QT, m.XNT, m.w("L0x_q"), m.w("L0x_qs")), (KT, m.CT, m.w("L0x_k"), m.w("L0x_ks"))],
                         V, m.CT, m.w("L0x_v"), turn=(four(m.masked_cos), four(m.masked_sin)))
        attend(nc, m, QT, KT, V, m.O, token_masks=(m.q_mask, m.k_mask))
    out_project(nc, m, m.O, m.w("L0x_o"))


def attention1(nc, m):
    with ExitStack() as ctx:
        sb = lambda name, shape, dt=F32: ctx.enter_context(nc.sbuf_tensor(f"{name}_a1", shape, dt))
        QT, KT = sb("QT", [D, T]), sb("KT", [D, T])
        V = sb("V", [S, B, H, DH + 1])
        BN = HALF // S
        bias = sb("bias", [S, H, S])
        ps_ctx = ExitStack()
        ps = [ps_ctx.enter_context(nc.psum_tensor(f"bias_ps{g}", [S, HALF], F32)) for g in range(NG)]
        base = m.n_proj
        m.n_proj += NG
        with nc.Block() as block:
            @block.vector
            def _(dve):
                dve.wait_ge(m.bias_loaded, 16)
                nc.vector.scalar_tensor_tensor(out=m.pos_bias[:], in0=m.pos_bias[:], scalar=float(DH) ** 0.5,
                                               in1=bcast_mid(m.w("causal_flip"), H), op0=ALU.mult,
                                               op1=ALU.add).then_inc(m.bias_scaled, 1)

            @block.tensor
            def _(pe):
                pe.wait_ge(m.bias_scaled, 1)
                for g in range(NG):
                    nc.tensor.matmul(ps[g][:], m.w("flip"), m.pos_bias[:, g * BN:(g + 1) * BN, :], start=True,
                                     stop=True).then_inc(m.proj, 1)

            @block.scalar
            def _(act):
                for g in range(NG):
                    act.wait_ge(m.proj, base + g + 1)
                    nc.scalar.activation(bias[:, g * BN:(g + 1) * BN, :], ps[g][:].rearrange("p (h k) -> p h k", h=BN),
                                         ACT.Copy)
        ps_ctx.close()
        attention_inputs(nc, m, [(QT, m.XNT, m.w("L1a_q"), m.w("L1a_bq")), (KT, m.XNT, m.w("L1a_k"), m.w("L1a_bk"))],
                         V, m.XNT, m.w("L1a_v"), m.row("L1a_bv"))
        attend(nc, m, QT, KT, V, m.O, bias=lambda g: bias[:, g * HG:(g + 1) * HG, :])
    out_project(nc, m, m.O, m.w("L1a_o"), m.row("L1a_bo"))


def mix_stage1(nc, m):
    with ExitStack() as ctx:
        mean = ctx.enter_context(nc.sbuf_tensor("ctx_mean", [D, B], F32))
        with nc.Block() as block:
            @block.vector
            def _(dve):
                m.dve_steps.done(dve, nc.vector.tensor_reduce(
                    mean[:], m.CT[:].rearrange("p (b s) -> p b s", b=B), AX.X, ALU.add))
                nc.vector.tensor_scalar(mean[:], mean[:], 1.0 / S, None, ALU.mult)
        add_products(nc, m, [((lambda b: m.XNT[:, b * S:(b + 1) * S]), m.w("L1x_w1")),
                             ((lambda b: mean[:, b:b + 1].to_broadcast([D, S])), m.w("L1x_w2"))],
                     bias_row=m.row("L1x_b"))


def ffn1_stage(nc, m):
    expert_stage(nc, m, "L1f", 16, 2, "softmax_two", ACT.Relu, m.dram["L1f_w"],
                 rows=(m.row("L1f_bg"), m.row("L1f_bias")), b2=m.w("L1f_b2", slice(0, 16)))


def attention2(nc, m):
    with ExitStack() as ctx:
        sb = lambda name, shape, dt=F32: ctx.enter_context(nc.sbuf_tensor(f"{name}_a2", shape, dt))
        QT, KT = sb("QT", [D, T]), sb("KT", [D, T])
        V = sb("V", [S, B, H, DH + 1])
        attention_inputs(nc, m, [(QT, m.XNT, m.w("L2a_q"), m.w("L2a_qs")), (KT, m.XNT, m.w("L2a_k"), m.w("L2a_ks"))],
                         V, m.XNT, m.w("L2a_v"),
                         turn=[lambda half, t=t: bcast_mid(m.w(t), B // 2) for t in ("rope2c", "rope2s")])
        attend(nc, m, QT, KT, V, m.O, bias=m.causal)
    out_project(nc, m, m.O, m.w("L2a_o"))


def bidirectional2(nc, m):
    with ExitStack() as outer:
        sb = lambda name, shape, dt=F32: outer.enter_context(nc.sbuf_tensor(f"{name}_x2", shape, dt))
        hw, P, PTs = sb("hw", [D, T]), sb("P", [S, B, S]), sb("PTs", [S, T])
        F2, F3, F4 = (sb(name, [D, T]) for name in ("F2", "F3", "F4"))
        top, total, best = sb("top", [S, B]), sb("total", [S, B]), sb("best", [S, B])
        batt, btop, btotal = sb("batt", [B, S]), sb("btop", [B, 1]), sb("btotal", [B, 1])
        battT, hc = sb("battT", [S, B]), sb("hc", [D, B])
        steps = m.dve_steps
        halves = [slice(0, HALF), slice(HALF, T)]
        with ExitStack() as ctx:
            sim = ctx.enter_context(nc.psum_tensor("sim", [S, B, S], F32))
            small = ctx.enter_context(nc.psum_tensor("small_x2", [S, 256], F32))
            base_p, base_e = m.n_proj, m.n_evac
            m.n_proj += 3
            m.n_evac += 2
            v = {}
            with nc.Block() as block:
                @block.vector
                def _(dve):
                    v["hw"] = steps.inc(nc.vector.tensor_scalar(hw[:], m.XNT[:], m.w("L2x_w3"), m.w("L2x_w2"),
                                                                ALU.mult, ALU.add))
                    dve.wait_ge(m.proj, base_p + 1)
                    steps.done(dve, nc.vector.tensor_reduce(top[:], sim[:], AX.X, ALU.max))
                    v["shift"] = steps.inc(nc.vector.tensor_tensor(P[:], sim[:], bcast_last(top[:], S), ALU.subtract))
                    steps.done(dve, nc.vector.tensor_tensor(best[:], top[:], small[:, 0:B], ALU.add))
                    v["best"] = steps.inc(nc.vector.tensor_scalar(best[:], best[:], m.row("L2x_bsim"), None, ALU.add))
                    dve.wait_ge(m.proj, base_p + 2)
                    steps.done(dve, nc.vector.tensor_reduce(btop[:], small[0:B, 128:256], AX.X, ALU.max))
                    v["bshift"] = steps.inc(nc.vector.tensor_scalar(batt[:], small[0:B, 128:256], btop[:], None,
                                                                    ALU.subtract))
                    dve.wait_ge(m.evac, base_e + 2)
                    steps.done(dve, nc.vector.tensor_reduce(total[:], P[:], AX.X, ALU.add))
                    steps.done(dve, nc.vector.reciprocal(total[:], total[:]))
                    steps.done(dve, nc.vector.tensor_tensor(P[:], P[:], bcast_last(total[:], S), ALU.mult))
                    steps.done(dve, nc.vector.tensor_reduce(btotal[:], batt[:], AX.X, ALU.add))
                    steps.done(dve, nc.vector.reciprocal(btotal[:], btotal[:]))
                    nc.vector.tensor_scalar(batt[:], batt[:], btotal[:], None, ALU.mult)

                @block.tensor
                def _(pe):
                    for b in range(B):
                        nc.tensor.matmul(small[:, b:b + 1], m.XNT[:, b * S:(b + 1) * S], m.w("L2x_w1"),
                                         start=True, stop=True)
                    pe.wait_ge(steps.sem, v["hw"])
                    for b in range(B):
                        t = nc.tensor.matmul(sim[:, b, :], hw[:, b * S:(b + 1) * S], m.CT[:, b * S:(b + 1) * S],
                                             start=True, stop=True)
                    t.then_inc(m.proj, 1)
                    pe.wait_ge(steps.sem, v["best"])
                    nc.tensor.transpose(small[0:B, 128:256], best[:], m.w("ident")).then_inc(m.proj, 2)

                @block.scalar
                def _(act):
                    act.wait_ge(steps.sem, v["shift"])
                    nc.scalar.activation(P[:], P[:], ACT.Exp).then_inc(m.evac, 1)
                    act.wait_ge(steps.sem, v["bshift"])
                    nc.scalar.activation(batt[:], batt[:], ACT.Exp).then_inc(m.evac, 1)
        with ExitStack() as ctx:
            pt = ctx.enter_context(nc.psum_tensor("pt_x2", [S, T], F32))
            hat = ctx.enter_context(nc.psum_tensor("hat", [D, T], F32))
            small = ctx.enter_context(nc.psum_tensor("small2", [S, 256], F32))
            base_p, base_e = m.n_proj, m.n_evac
            m.n_proj += 6
            m.n_evac += 5
            with nc.Block() as block:
                @block.tensor
                def _(pe):
                    nc.tensor.transpose(small[:, 0:B], batt[:], m.w("ident", slice(0, B))[:, 0:B]).then_inc(m.proj, 1)
                    for b in range(B):
                        t = nc.tensor.transpose(pt[:, b * S:(b + 1) * S], P[:, b, :], m.w("ident"))
                        if b % 4 == 3:
                            t.then_inc(m.proj, 1)
                    pe.wait_ge(m.evac, base_e + 1)
                    for b in range(B):
                        t = nc.tensor.matmul(small[:, 128 + b:129 + b], m.XN[:, b, :], battT[:, b:b + 1],
                                             start=True, stop=True)
                    t.then_inc(m.proj, 1)
                    for b in range(B):
                        if b % 4 == 0:
                            pe.wait_ge(m.evac, base_e + 2 + b // 4)
                        t = nc.tensor.matmul(hat[:, b * S:(b + 1) * S], m.CTOK[:, b, :], PTs[:, b * S:(b + 1) * S],
                                             start=True, stop=True)
                        if b % 4 == 3:
                            t.then_inc(m.proj, 1)

                @block.scalar
                def _(act):
                    act.wait_ge(m.proj, base_p + 1)
                    nc.scalar.activation(battT[:], small[:, 0:B], ACT.Copy).then_inc(m.evac, 1)
                    for half in range(2):
                        act.wait_ge(m.proj, base_p + 2 + half)
                        nc.scalar.activation(PTs[:, halves[half]], pt[:, halves[half]], ACT.Copy).then_inc(m.evac, 1)
                    for half in range(2):
                        act.wait_ge(m.proj, base_p + 5 + half)
                        nc.scalar.activation(F2[:, halves[half]], hat[:, halves[half]], ACT.Copy).then_inc(m.evac, 1)

                @block.vector
                def _(dve):
                    dve.wait_ge(m.proj, base_p + 4)
                    steps.done(dve, nc.vector.tensor_copy(hc[:], small[:, 128:128 + B]))
                    nc.vector.tensor_tensor(F4[:].rearrange("p (b s) -> p b s", b=B),
                                            m.XNT[:].rearrange("p (b s) -> p b s", b=B), bcast_last(hc[:], S), ALU.mult)
                    for half in range(2):
                        dve.wait_ge(m.evac, base_e + 4 + half)
                        nc.vector.tensor_tensor(F3[:, halves[half]], m.XNT[:, halves[half]], F2[:, halves[half]],
                                                ALU.mult)
        w = m.w("L2x_wqv")
        add_products(nc, m, [((lambda b, f=f: f[:, b * S:(b + 1) * S]), w[:, k * D:(k + 1) * D])
                             for k, f in enumerate((m.XNT, F2, F3, F4))], bias_row=m.row("L2x_b"))


def block2(nc, m):
    norm_stage(nc, m, m.XN, m.O, m.w("L2n1_w"), m.w("L2n1_b"))
    with ExitStack() as ctx:
        sb = lambda name, shape, dt=F32: ctx.enter_context(nc.sbuf_tensor(f"{name}_b2", shape, dt))
        QT, KT = sb("QT", [D, T]), sb("KT", [D, T])
        V = sb("V", [S, B, H, DH + 1])
        attention_inputs(nc, m, [(QT, m.XNT, m.w("L2f_q"), m.w("L2f_bq")), (KT, m.XNT, m.w("L2f_k"), m.w("L2f_bk"))],
                         V, m.XNT, m.w("L2f_v"), m.row("L2f_bv"))
        attend(nc, m, QT, KT, V, m.O, bias=m.causal)
    out_project(nc, m, m.O, m.w("L2f_o"), m.row("L2f_bo"), target=m.XN,
                norm=(m.XN, m.O, m.w("L2n2_w"), m.w("L2n2_b")))
    with nc.Block() as block:
        @block.vector
        def _(dve):
            nc.vector.tensor_tensor(m.X[:], m.X[:], m.XN[:], ALU.add)
    expert_stage(nc, m, "L2f", 8, 4, "softmax_two", ACT.Gelu, m.dram["L2f_w"],
                 b2=m.w("L2f_b2", slice(0, 8)))


def attention3(nc, m):
    with ExitStack() as ctx:
        sb = lambda name, shape, dt=F32: ctx.enter_context(nc.sbuf_tensor(f"{name}_a3", shape, dt))
        QT, KT, K2T = sb("QT", [D, T]), sb("KT", [D, T]), sb("K2T", [D, T])
        V, O2 = sb("V", [S, B, H, DH + 1]), sb("O2", [S, B, D])
        attention_inputs(nc, m, [(QT, m.XNT, m.w("L3a_q"), m.w("L3a_bq")), (KT, m.XNT, m.w("L3a_k"), m.w("L3a_bk")),
                                 (K2T, m.XNT, m.w("L3a_k2"), m.w("L3a_bk2"))], V)
        attend(nc, m, QT, KT, V, m.O, bias=m.causal)
        with ExitStack() as inner:
            later = inner.enter_context(nc.psum_tensor("later", [S, B, D], F32))
            base = m.n_proj
            m.n_proj += 1
            with nc.Block() as block:
                @block.tensor
                def _(pe):
                    for b in range(B):
                        t = nc.tensor.transpose(later[0:S - 1, b, :], m.XNT[:, b * S + 1:(b + 1) * S], m.w("ident"))
                    t.then_inc(m.proj, 1)

                @block.vector
                def _(dve):
                    dve.wait_ge(m.proj, base + 1)
                    v4 = lambda a: a.rearrange("p b (h d) -> p b h d", h=H)
                    for b in range(B):
                        heads = lambda a: a[0:S - 1, b, :].rearrange("p (h d) -> p h d", h=H)
                        nc.vector.tensor_tensor(V[0:S - 1, b, :, 0:DH], heads(later), heads(m.O), ALU.subtract)
        attend(nc, m, QT, K2T, V, O2, bias=m.strict)
        with nc.Block() as block:
            @block.vector
            def _(dve):
                nc.vector.scalar_tensor_tensor(out=m.O[:], in0=O2[:], scalar=m.w("row1"), in1=m.O[:], op0=ALU.mult,
                                               op1=ALU.add)
    out_project(nc, m, m.O, m.w("L3a_o"), m.row("L3a_bo"), bias_times=2.0)


def autocorrelation3(nc, m):
    steps = m.dve_steps
    TOP = 4
    with ExitStack() as outer:
        sb = lambda name, shape, dt=F32: outer.enter_context(nc.sbuf_tensor(f"{name}_x3", shape, dt))
        tok = [sb(f"tok{k}", [S, B, D]) for k in range(3)]
        c = [sb(f"cos{k}", [FREQ, T]) for k in range(3)]
        s = [sb(f"sin{k}", [FREQ, T]) for k in range(3)]
        re, im, tmp = sb("re", [FREQ, T]), sb("im", [FREQ, T]), sb("tmp", [FREQ, T])
        res, ims = sb("res", [FREQ, B * H]), sb("ims", [FREQ, B * H])
        corr, best, index = sb("corr", [128, S]), sb("best", [128, 8]), sb("index", [128, 8], U32)
        indexf, wt, one = sb("indexf", [128, TOP]), sb("wt", [128, TOP]), sb("one", [128, 1])
        wvec, wtmp, wT = sb("wvec", [128, S]), sb("wtmp", [128, S]), sb("wT", [S, 128])
        wc, ws = sb("wc", [FREQ, 128]), sb("ws", [FREQ, 128])
        sources = (m.XNT[:], m.CT[:], m.CT[:])
        for k, name in enumerate("qkv"):
            token_linear(nc, m, tok[k], sources[k], m.w(f"L3x_{name}"), m.row(f"L3x_b{name}"))
        flat = [t[:].rearrange("p b d -> p (b d)") for t in tok]
        project(nc, m, [(x[k][:], [m.w(w)], [flat[k]], None) for k in range(3) for x, w in ((c, "dft_c"), (s, "dft_s"))])
        ps_ctx = ExitStack()
        pc = ps_ctx.enter_context(nc.psum_tensor("corr_ps", [128, S], F32))
        pw = ps_ctx.enter_context(nc.psum_tensor("w_ps", [128, 3 * 128], F32))
        base_p, base_e = m.n_proj, m.n_evac
        m.n_proj += 3
        m.n_evac += 2
        v = {}
        with nc.Block() as block:
            @block.vector
            def _(dve):
                tt = lambda out, a, b, op: steps.done(dve, nc.vector.tensor_tensor(out, a, b, op))
                tt(re[:], c[0][:], c[1][:], ALU.mult)
                tt(tmp[:], s[0][:], s[1][:], ALU.mult)
                tt(re[:], re[:], tmp[:], ALU.add)
                tt(im[:], s[0][:], c[1][:], ALU.mult)
                tt(tmp[:], c[0][:], s[1][:], ALU.mult)
                tt(im[:], im[:], tmp[:], ALU.subtract)
                steps.done(dve, nc.vector.tensor_reduce(res[:], re[:].rearrange("p (g d) -> p g d", d=DH), AX.X, ALU.add))
                v["sums"] = steps.inc(nc.vector.tensor_reduce(ims[:], im[:].rearrange("p (g d) -> p g d", d=DH), AX.X,
                                                              ALU.add))
                dve.wait_ge(m.proj, base_p + 1)
                steps.done(dve, nc.vector.tensor_copy(corr[:], pc[:]))
                steps.done(dve, nc.vector.max(best[:], corr[:]))
                steps.done(dve, nc.vector.max_index(index[:], best[:], corr[:]))
                steps.done(dve, nc.vector.tensor_copy(indexf[:], index[:, 0:TOP]))
                v["shift"] = steps.inc(nc.vector.tensor_scalar(wt[:], best[:, 0:TOP], best[:, 0:1], None, ALU.subtract))
                dve.wait_ge(m.evac, base_e + 1)
                steps.done(dve, nc.vector.tensor_reduce(one[:], wt[:], AX.X, ALU.add))
                steps.done(dve, nc.vector.reciprocal(one[:], one[:]))
                steps.done(dve, nc.vector.tensor_scalar(wt[:], wt[:], one[:], None, ALU.mult))
                for k in range(TOP):
                    out = wvec if k == 0 else wtmp
                    steps.done(dve, nc.vector.tensor_scalar(out[:], m.w("iota128"), indexf[:, k:k + 1], wt[:, k:k + 1],
                                                            ALU.is_equal, ALU.mult))
                    if k:
                        tt(wvec[:], wvec[:], wtmp[:], ALU.add)
                v["wvec"] = steps.n
                dve.wait_ge(m.proj, base_p + 2)
                v["wT"] = steps.inc(nc.vector.tensor_copy(wT[:], pw[:, 0:128]))
                dve.wait_ge(m.proj, base_p + 3)
                steps.inc(nc.vector.tensor_copy(wc[:], pw[0:FREQ, 128:256]))
                steps.done(dve, nc.vector.tensor_copy(ws[:], pw[0:FREQ, 256:384]))
                wide = lambda a: bcast_last(a[:], DH)
                v3 = lambda a: a[:].rearrange("p (g d) -> p g d", d=DH)
                tt(v3(re), v3(c[2]), wide(wc), ALU.mult)
                tt(v3(tmp), v3(s[2]), wide(ws), ALU.mult)
                tt(re[:], re[:], tmp[:], ALU.subtract)
                tt(v3(im), v3(s[2]), wide(wc), ALU.mult)
                tt(v3(tmp), v3(c[2]), wide(ws), ALU.mult)
                tt(im[:], im[:], tmp[:], ALU.add)

            @block.tensor
            def _(pe):
                freq = slice(0, FREQ)
                pe.wait_ge(steps.sem, v["sums"])
                nc.tensor.matmul(pc[:], res[:], m.w("invh_c", freq), start=True, stop=False)
                nc.tensor.matmul(pc[:], ims[:], m.w("invh_s", freq), start=False, stop=True).then_inc(m.proj, 1)
                pe.wait_ge(steps.sem, v["wvec"])
                nc.tensor.transpose(pw[:, 0:128], wvec[:], m.w("ident")).then_inc(m.proj, 1)
                pe.wait_ge(steps.sem, v["wT"])
                nc.tensor.matmul(pw[0:FREQ, 128:256], m.w("dft_c"), wT[:], start=True, stop=True)
                nc.tensor.matmul(pw[0:FREQ, 256:384], m.w("dft_s"), wT[:], start=True, stop=True).then_inc(m.proj, 1)

            @block.scalar
            def _(act):
                act.wait_ge(steps.sem, v["shift"])
                nc.scalar.activation(wt[:], wt[:], ACT.Exp).then_inc(m.evac, 2)
        ps_ctx.close()
        freq = slice(0, FREQ)
        project(nc, m, [(m.O[:].rearrange("p b d -> p (b d)"), [m.w("inv_c", freq), m.w("inv_s", freq)],
                         [re[:], im[:]], None)])
    out_project(nc, m, m.O, m.w("L3x_o"), m.row("L3x_bo"))


def token_linear(nc, m, out, source, weight, bias_row):
    with ExitStack() as ctx:
        ps = ctx.enter_context(nc.psum_tensor(f"lin_ps{m.n_proj}", [S, B, D], F32))
        block = ctx.enter_context(nc.Block())
        base = m.n_proj
        m.n_proj += 2

        @block.tensor
        def _(pe):
            for b in range(B):
                t = nc.tensor.matmul(ps[:, b, :], source[:, b * S:(b + 1) * S], weight, start=True, stop=True)
                if b % 4 == 3:
                    t.then_inc(m.proj, 1)

        @block.vector
        def _(dve):
            for half in range(2):
                dve.wait_ge(m.proj, base + half + 1)
                bs = slice(4 * half, 4 * half + 4)
                nc.vector.tensor_tensor(out[:, bs, :], ps[:, bs, :], bcast_mid(bias_row, B // 2), ALU.add)


def ffn3_stage(nc, m):
    expert_stage(nc, m, "L3f", 7, 4, "softmax_all", ACT.Silu, m.dram["L3f_w"], gated=True, last=True)


def build(nc, dram, stages):
    with ExitStack() as ctx:
        m = Model(nc, ctx, dram)
        start_stage(nc, m)
        todo = [lambda: mamba_stage(nc, m)] + [lambda f=f: f(nc, m) for f in STAGES]
        for k in range(stages):
            todo[k]()
        with nc.Block() as block:
            @block.sync
            def _(sp):
                if stages < 3:
                    sp.wait_ge(m.bias_loaded, 16)
                sp.dma_start(dram["out"], m.X[:]).then_inc(m.stored, 16)
                sp.wait_ge(m.stored, 16)


STAGES = [cross_attention0, ffn0_stage, attention1, mix_stage1, ffn1_stage, attention2, bidirectional2, block2, attention3,
          autocorrelation3, ffn3_stage]
N_STAGES = 12


def pack(table, total, arrays, rows=128):
    out = np.zeros((rows, total), np.float32)
    for name, (at, n) in table.items():
        a = np.asarray(arrays[name]).reshape(-1, n)
        out[:a.shape[0], at:at + n] = a
    return out


def host_arrays(i):
    def chunks(a, width):
        return a.reshape(-1, 128, width).transpose(1, 0, 2).reshape(128, -1)

    a = {}
    a["ident"] = np.eye(128, dtype=np.float32)
    a["ln_w"], a["ln_b"] = (i[f"L0_attn_{n}"].reshape(128, 1) for n in ("ln_w", "ln_b"))
    a["W_in"] = i["L0_attn_W_in"]
    a["conv_w"] = chunks(i["L0_attn_conv_w"].reshape(INNER, TAPS), TAPS)
    a["conv_b"] = chunks(i["L0_attn_conv_b"].reshape(INNER, 1), 1)
    a["W_xproj"] = chunks(i["L0_attn_W_xproj"], RANK + 2 * STATE)
    a["W_dt"] = i["L0_attn_W_dt"]
    a["b_dt"] = chunks(i["L0_attn_b_dt"].reshape(INNER, 1), 1)
    a["A_log"] = chunks(i["L0_attn_A_log"], STATE)
    a["Dskip"] = chunks(i["L0_attn_D"].reshape(INNER, 1), 1)
    a["W_out"] = chunks(i["L0_attn_W_out"], D)

    p, t = np.arange(128), np.arange(S)
    a["head_mask"] = (p[:, None] // DH == np.arange(H)).astype(np.float32)
    a["causal"] = np.where(t[None, :] > t[:, None], NEG, 0.0).astype(np.float32)
    a["flip"], a["causal_flip"] = a["ident"][::-1], a["causal"][::-1]
    a["strict"] = np.where(t[None, :] >= t[:, None], NEG, 0.0).astype(np.float32)
    a["row1"] = (t[:, None] > 0).astype(np.float32)
    a["iota16"] = np.tile(np.arange(16, dtype=np.float32), (128, 1))
    a["iota128"] = np.tile(np.arange(128, dtype=np.float32), (128, 1))
    w0 = (1.0 / 10000.0 ** (np.arange(1, DH + 1, 2, dtype=np.float32) / DH)).astype(np.float32)
    ang0 = np.arange(1, S + 1, dtype=np.float32)[:, None] * w0
    d = p % DH
    a["rope0c"] = np.cos(ang0).T[d // 2]
    a["rope0s"] = np.sin(ang0).T[d // 2] * np.where(d % 2, 1, -1)[:, None]
    w2 = (1.0 / 10000.0 ** (np.arange(DH // 2, dtype=np.float32) / (DH // 2))).astype(np.float32)
    ang2 = np.arange(S, dtype=np.float32)[:, None] * w2
    a["rope2c"] = np.cos(ang2).T[d % 4]
    a["rope2s"] = np.sin(ang2).T[d % 4] * np.where(d < 4, -1, 1)[:, None]
    f = np.arange(FREQ)
    theta = 2 * np.pi * (t[:, None] * f % S) / S
    a["dft_c"], a["dft_s"] = np.cos(theta), np.sin(theta)
    both = np.where((f == 0) | (f == S // 2), 1.0, 2.0)[:, None] / S
    a["inv_c"], a["inv_s"] = np.cos(theta).T * both, np.sin(theta).T * both
    a["invh_c"], a["invh_s"] = a["inv_c"] / DH, a["inv_s"] / DH
    a["L0f_sel"] = (np.arange(512) // 64 == np.arange(8)[:, None]).astype(np.float32)

    pairs = p ^ 1
    halves = p // DH * DH + (d + DH // 2) % DH
    wkv = i["L0_xattn_W_kv"]
    a["L0x_q"], a["L0x_k"], a["L0x_v"], a["L0x_o"] = i["L0_xattn_W_q"], wkv[:, :D], wkv[:, D:], i["L0_xattn_W_c"]
    a["L0x_qs"], a["L0x_ks"] = a["L0x_q"][:, pairs], a["L0x_k"][:, pairs]
    a["L0f_router"] = i["L0_ffn_gate_weight"].T
    a["L0f_g"] = np.concatenate([i["L0_ffn_w_gate"].reshape(512, D), i["L0_ffn_ws_gate"]]).T
    a["L0f_u"] = np.concatenate([i["L0_ffn_w_up"].reshape(512, D), i["L0_ffn_ws_up"]]).T
    a["L0f_d"] = chunks(np.concatenate([i["L0_ffn_w_down"].transpose(0, 2, 1).reshape(512, D),
                                        i["L0_ffn_ws_down"].T]), D)
    qkv, qb = i["L1_attn_qkv_w"], i["L1_attn_qkv_b"]
    a["L1a_q"], a["L1a_k"], a["L1a_v"], a["L1a_o"] = qkv[:D].T, qkv[D:2 * D].T, qkv[2 * D:].T, i["L1_attn_proj_w"].T
    a["L1a_bq"], a["L1a_bk"], a["L1a_bv"] = qb[:D, None], qb[D:2 * D, None], qb[2 * D:]
    a["L1a_bo"] = i["L1_attn_proj_b"]
    a["L1x_w1"], a["L1x_w2"], a["L1x_b"] = i["L1_xattn_W"][:, :D].T, i["L1_xattn_W"][:, D:].T, i["L1_xattn_b"]
    a["L1f_router"], a["L1f_bg"], a["L1f_bias"] = i["L1_ffn_Wg"], i["L1_ffn_bg"], i["L1_ffn_bias"]
    a["L1f_b2"] = i["L1_ffn_b2"]
    kv = p // DH % HG * DH + d
    a["L2a_q"], a["L2a_k"], a["L2a_v"], a["L2a_o"] = (
        i["L2_attn_wq"], i["L2_attn_wk"][:, kv], i["L2_attn_wv"][:, kv], i["L2_attn_wo"])
    a["L2a_qs"], a["L2a_ks"] = a["L2a_q"][:, halves], a["L2a_k"][:, halves]
    a["L2x_w1"], a["L2x_w2"], a["L2x_w3"] = i["L2_xattn_w_sim"].reshape(3, D, 1)
    a["L2x_bsim"], a["L2x_b"], a["L2x_wqv"] = i["L2_xattn_b_sim"], i["L2_xattn_b_qv"], chunks(i["L2_xattn_W_qv"], D)
    for k in (1, 2):
        a[f"L2n{k}_w"], a[f"L2n{k}_b"] = i[f"L2_ffn_ln{k}_w"][:, None], i[f"L2_ffn_ln{k}_b"][:, None]
    w, b = i["L2_ffn_Wqkv"], i["L2_ffn_bqkv"]
    a["L2f_q"], a["L2f_k"], a["L2f_v"], a["L2f_o"] = w[:, :D], w[:, D:2 * D], w[:, 2 * D:], i["L2_ffn_Wo"]
    a["L2f_bq"], a["L2f_bk"], a["L2f_bv"], a["L2f_bo"] = b[:D, None], b[D:2 * D, None], b[2 * D:], i["L2_ffn_bo"]
    a["L2f_router"] = i["L2_ffn_gate_W"]
    a["L2f_b2"] = i["L2_ffn_fc2_b"]
    w, b = i["L3_attn_W_attn"], i["L3_attn_b_attn"]
    a["L3a_q"], a["L3a_k"], a["L3a_bq"], a["L3a_bk"] = w[:, :D], w[:, D:], b[:D, None], b[D:, None]
    a["L3a_k2"], a["L3a_bk2"] = i["L3_attn_W_k2"], i["L3_attn_b_k2"][:, None]
    a["L3a_o"], a["L3a_bo"] = i["L3_attn_W_proj"], i["L3_attn_b_proj"]
    for n in "qkvo":
        a[f"L3x_{n}"], a[f"L3x_b{n}"] = i[f"L3_xattn_W{n}"].T, i[f"L3_xattn_b{n}"]
    a["L3f_router"] = i["L3_ffn_router_w"].T
    return a


def big_arrays(i):
    def by_chunks(w):
        e, f, n = w.shape
        return w.reshape(e, f // 128, 128, n).transpose(0, 2, 1, 3).reshape(e, 128, -1)

    rel = np.zeros((2 * S, D), np.float32)
    rel[:2 * S - 1] = i["L1_attn_rel_pos_emb"][::-1]
    out = {
        "mask": i["mask_BxS2_bf1"].reshape(1, T).view(np.uint8),
        "rel_pos": rel.reshape(2, 128, D).transpose(1, 0, 2),
        "L1f_w": np.concatenate([i["L1_ffn_W1"], by_chunks(i["L1_ffn_W2"]), by_chunks(i["L1_ffn_b1"][:, :, None])], axis=2),
        "L2f_w": np.concatenate([i["L2_ffn_fc1_w"].transpose(0, 2, 1),
                                 by_chunks(i["L2_ffn_fc2_w"].transpose(0, 2, 1)),
                                 by_chunks(i["L2_ffn_fc1_b"][:, :, None])], axis=2),
    }
    gate, up, down = (np.concatenate([i[f"L3_ffn_routed_{n}"], i[f"L3_ffn_shared_{n}"][None]]).transpose(0, 2, 1)
                      for n in ("gate", "up", "down"))
    out["L3f_w"] = np.concatenate([gate, up, by_chunks(down)], axis=2)
    return {k: np.ascontiguousarray(v) for k, v in out.items()}


def kernel(**inputs):
    import concourse.bacc as bacc
    from concourse.bass_utils import run_bass_kernel_spmd

    i = {k: np.asarray(v) for k, v in inputs.items()}
    a = host_arrays(i)
    arrays = {
        "x": np.ascontiguousarray(i["x"].transpose(1, 0, 2)),
        "ctx_feat": np.ascontiguousarray(i["ctx_1024"].transpose(2, 0, 1)).reshape(D, T),
        "ctx_tok": np.ascontiguousarray(i["ctx_1024"].transpose(1, 0, 2)),
        "mamba": pack(MAMBA_AT, MAMBA_N, a),
        "small": pack(SMALL_AT, SMALL_N, a),
        "rows": pack(ROWS_AT, ROWS_N, a, rows=1),
        **big_arrays(i),
    }
    nc = bacc.Bacc("TRN2", target_bir_lowering=False, num_devices=1)
    dram = {name: nc.dram_tensor(name, list(v.shape), mybir.dt.from_np(v.dtype), kind="ExternalInput").ap()
            for name, v in arrays.items()}
    dram["rel_table"] = nc.dram_tensor("rel_table", [H, 2 * S], F32, kind="Internal").ap()
    dram["out"] = nc.dram_tensor("out", [S, B, D], F32, kind="ExternalOutput").ap()
    build(nc, dram, N_STAGES)
    result = run_bass_kernel_spmd(nc, [arrays], core_ids=[0])
    return np.ascontiguousarray(np.asarray(result.results[0]["out"]).transpose(1, 0, 2))
```

```python
from contextlib import ExitStack

import numpy as np

import concourse.bass as bass
from concourse import mybir

F32 = mybir.dt.float32
BF16 = mybir.dt.bfloat16
U8 = mybir.dt.uint8
U32 = mybir.dt.uint32
ACT = mybir.ActivationFunctionType
ALU = mybir.AluOpType
AX = mybir.AxisListType

B, S, D = 8, 128, 128
T = B * S
HALF = 512
H, DH = 16, 8
HG = 4
NG = H // HG
EPS = 1e-5
NEG = -1.0e30
BIG = float(2 ** 30)
INNER, STATE, RANK, TAPS = 256, 64, 8, 4
IC = INNER // 128
FREQ = S // 2 + 1


class Steps:

    def __init__(self, sem):
        self.sem, self.n, self.i, self.k = sem, 0, None, 0

    def inc(self, instruction):
        instruction.then_inc(self.sem, 1)
        if self.i is None:
            self.n += 1
            return self.n
        self.k += 1
        return self.i * self.per + (self.n + self.k)

    def done(self, engine, instruction):
        engine.wait_ge(self.sem, self.inc(instruction))

    def enter(self, i, per):
        self.i, self.per, self.k = i, per, 0

    def leave(self, passes):
        assert self.k == self.per, (self.k, self.per)
        self.i = None
        self.n += passes * self.per


class Ring:

    def __init__(self, sem, depth, spare=0):
        self.sem, self.depth, self.spare = sem, depth, spare
        self.start = depth + spare

    def ended(self, n):
        return n + (self.start + 1)

    def free(self, n):
        return n + (self.spare + 1)


def layout(name_shapes):
    table, at = {}, 0
    for name, n in name_shapes:
        table[name] = (at, n)
        at += n
    return table, at


MAMBA = [("ident", 128), ("ln_w", 1), ("ln_b", 1), ("W_in", 2 * INNER), ("conv_w", IC * TAPS), ("conv_b", IC),
         ("W_xproj", IC * (RANK + 2 * STATE)), ("W_dt", INNER), ("b_dt", IC), ("A_log", IC * STATE), ("Dskip", IC),
         ("W_out", IC * D)]
SMALL = [("head_mask", H), ("causal", S), ("strict", S), ("flip", S), ("causal_flip", S), ("row1", 1), ("iota16", 16), ("iota128", 128),
         ("rope0c", S), ("rope0s", S), ("rope2c", S), ("rope2s", S),
         ("L0x_q", D), ("L0x_qs", D), ("L0x_k", D), ("L0x_ks", D), ("L0x_v", D), ("L0x_o", D),
         ("L0f_router", 8), ("L0f_g", 640), ("L0f_u", 640), ("L0f_d", 640), ("L0f_sel", 512),
         ("L1a_q", D), ("L1a_k", D), ("L1a_v", D), ("L1a_o", D), ("L1a_bq", 1), ("L1a_bk", 1),
         ("L1x_w1", D), ("L1x_w2", D),
         ("L1f_router", 16), ("L1f_b2", D),
         ("L2a_q", D), ("L2a_qs", D), ("L2a_k", D), ("L2a_ks", D), ("L2a_v", D), ("L2a_o", D),
         ("L2x_w1", 1), ("L2x_w2", 1), ("L2x_w3", 1), ("L2x_wqv", 4 * D),
         ("L2n1_w", 1), ("L2n1_b", 1), ("L2n2_w", 1), ("L2n2_b", 1),
         ("L2f_q", D), ("L2f_k", D), ("L2f_v", D), ("L2f_o", D), ("L2f_bq", 1), ("L2f_bk", 1),
         ("L2f_router", 8), ("L2f_b2", D),
         ("L3a_q", D), ("L3a_k", D), ("L3a_k2", D), ("L3a_o", D), ("L3a_bq", 1), ("L3a_bk", 1), ("L3a_bk2", 1),
         ("L3x_q", D), ("L3x_k", D), ("L3x_v", D), ("L3x_o", D),
         ("dft", S), ("dft_swapped", S), ("corr_same", S), ("corr_swapped", S), ("roll_same", S), ("roll_swapped", S),
         ("L3f_router", 7)]
ROWS = [("L1a_bv", D), ("L1a_bo", D), ("L1x_b", D), ("L1f_bg", 16), ("L1f_bias", 16), ("L2x_b", D), ("L2x_bsim", 1),
        ("L2f_bv", D), ("L2f_bo", D), ("L3a_bo", D),
        ("L3x_bq", D), ("L3x_bk", D), ("L3x_bv", D), ("L3x_bo", D)]
MAMBA_AT, MAMBA_N = layout(MAMBA)
SMALL_AT, SMALL_N = layout(SMALL)
ROWS_AT, ROWS_N = layout(ROWS)


class Model:

    def __init__(self, nc, ctx, dram):
        self.nc, self.dram = nc, dram
        self.n_norm = self.n_attn = self.n_tail = self.n_moe = self.n_route = 0

        def sb(name, shape, dt=F32):
            return ctx.enter_context(nc.sbuf_tensor(name, shape, dt))

        def sem(name):
            return ctx.enter_context(nc.semaphore(name))

        self.X = sb("X", [S, B, D])
        self.XN = sb("XN", [S, B, D])
        self.XNT = sb("XNT", [D, T])
        self.CT = sb("CT", [D, T])
        self.CTOK = sb("CTOK", [S, B, D])
        self.O = sb("O", [S, B, D])
        self.mamba_pack = sb("mamba_pack", [128, MAMBA_N])
        self.small_pack = sb("small_pack", [128, SMALL_N])
        self.row_pack = sb("row_pack", [128, ROWS_N])
        self.neghalf, self.scratch = sb("neghalf", [S, B]), sb("scratch", [S, 1])
        self.identb = sb("identb", [128, 128], BF16)
        self.select2 = sb("select2", [128, STATE], BF16)
        self.causal = lambda g, b: bcast_mid(self.w("causal"), HG)
        self.strict = lambda g, b: bcast_mid(self.w("strict"), HG)
        self.rel = sb("rel", [128, 2, D])
        self.pos_bias = sb("pos_bias", [S, H, S])
        self.mask8 = sb("mask8", [128, T], U8)
        self.masked_cos, self.masked_sin = sb("masked_cos", [D, B, S]), sb("masked_sin", [D, B, S])
        self.q_mask, self.k_mask = sb("q_mask", [128, T], BF16), sb("k_mask", [128, T], BF16)
        self.bias_loaded = sem("bias_loaded")
        self.ctx_mean = sb("ctx_mean", [D, B])
        self.loaded_x, self.loaded_mamba, self.loaded_rest = sem("loaded_x"), sem("loaded_mamba"), sem("loaded_rest")
        self.stored = sem("stored")
        self.pe_steps, self.act_steps = Steps(sem("pe_steps")), Steps(sem("act_steps"))
        self.dve_steps, self.pool_steps = Steps(sem("dve_steps")), Steps(sem("pool_steps"))
        self.stats_ready, self.rstd_ready = sem("stats_ready"), sem("rstd_ready")
        self.normed, self.turned = sem("normed"), sem("turned")
        self.kq = Ring(sem("kq_copied"), 2)
        self.scored = Ring(sem("scored"), 8)
        self.shifted = Ring(sem("shifted"), 4)
        self.exped = Ring(sem("exped"), 4)
        self.p_turned = Ring(sem("p_turned"), 4)
        self.pt_copied = Ring(sem("pt_copied"), 2)
        self.weighed = Ring(sem("weighed"), 2)
        self.out_done = Ring(sem("out_done"), 2)
        self.biased, self.maxed = sem("biased"), sem("maxed")
        self.proj, self.evac = sem("proj"), sem("evac")
        self.n_proj = self.n_evac = self.n_values = 0
        self.value_done = sem("value_done")
        self.w_loaded = [sem(f"w_loaded{e}") for e in range(2)]
        self.up_done = Ring(sem("up_done"), 2)
        self.act_done = Ring(sem("act_done"), 2)
        self.h_done = Ring(sem("h_done"), 2)
        self.y_done = Ring(sem("y_done"), 2, spare=1)
        self.added = Ring(sem("added"), 8)
        self.n_expert = self.n_unit = self.n_hunit = self.n_b2 = self.n_turn = 0
        self.logits_done, self.route_exped = sem("logits_done"), sem("route_exped")
        self.comb_turned, self.comb_copied, self.b2_done = sem("comb_turned"), sem("comb_copied"), sem("b2_done")
        self.rings = {"pool": [self.kq], "tensor": [self.scored, self.p_turned, self.weighed, self.up_done, self.y_done],
                      "vector": [self.shifted, self.out_done, self.h_done, self.added],
                      "scalar": [self.exped, self.pt_copied, self.act_done]}
        self.sem = sem

    def load_table(self, act, func):
        self.act_steps.done(act, self.nc.scalar.activation(self.scratch[:], self.neghalf[:, 0:1], func))

    def w(self, name, rows=slice(0, 128)):
        for table, pack in ((MAMBA_AT, self.mamba_pack), (SMALL_AT, self.small_pack)):
            if name in table:
                at, n = table[name]
                return pack[rows, at:at + n]
        raise KeyError(name)

    def row(self, name):
        at, n = ROWS_AT[name]
        return self.row_pack[:, at:at + n]


def bcast_mid(ap, n):
    return ap.unsqueeze(1).to_broadcast([ap.shape[0], n, ap.shape[1]])


def bcast_last(ap, n):
    return ap.unsqueeze(2).to_broadcast([ap.shape[0], ap.shape[1], n])


def start_stage(nc, m):
    d = m.dram
    with nc.Block() as block:
        @block.sync
        def _(sp):
            sp.dma_start(m.X[:], d["x"]).then_inc(m.loaded_x, 16)
            sp.dma_start(m.mamba_pack[:], d["mamba"]).then_inc(m.loaded_mamba, 16)
            sp.dma_start(m.small_pack[:], d["small"]).then_inc(m.loaded_rest, 16)
            sp.dma_start(m.row_pack[:], d["rows"].to_broadcast([128, ROWS_N])).then_inc(m.loaded_rest, 16)
            sp.dma_start(m.CT[:], d["ctx_feat"]).then_inc(m.loaded_rest, 16)
            sp.dma_start(m.CTOK[:], d["ctx_tok"]).then_inc(m.loaded_rest, 16)
            sp.dma_start(m.rel[:], d["rel_pos"]).then_inc(m.loaded_rest, 16)
            sp.dma_start(m.mask8[:], d["mask"].to_broadcast([128, T])).then_inc(m.loaded_rest, 16)

        @block.gpsimd
        def _(pool):
            for ring in m.rings["pool"]:
                pool.sem_inc(ring.sem, ring.start)
            nc.gpsimd.memset(m.neghalf[:], -0.5)

        @block.tensor
        def _(pe):
            for ring in m.rings["tensor"]:
                pe.sem_inc(ring.sem, ring.start)

        @block.scalar
        def _(act):
            for ring in m.rings["scalar"]:
                act.sem_inc(ring.sem, ring.start)

        @block.vector
        def _(dve):
            for ring in m.rings["vector"]:
                dve.sem_inc(ring.sem, ring.start)
            m.dve_steps.inc(nc.vector.memset(m.q_mask[:], 0.0))
            m.dve_steps.done(dve, nc.vector.memset(m.k_mask[:], 0.0))
            nc.vector.memset(m.q_mask[32:33, :], 1.0)
            nc.vector.memset(m.k_mask[32:33, :], -BIG)
            dve.wait_ge(m.loaded_x, 16)
            dve.wait_ge(m.loaded_mamba, 16)
            nc.vector.tensor_copy(m.identb[:], m.w("ident"))
            nc.vector.tensor_tensor(m.select2[:], m.w("ident")[:, 0:STATE], m.w("ident")[:, STATE:], ALU.add)


def norm_stage(nc, m, src, dst, weight=None, bias=None):
    with ExitStack() as ctx:
        norm = Norm(nc, m, ctx, src, dst, weight, bias)
        norm.emit(ctx.enter_context(nc.Block()))


class Norm:

    def __init__(self, nc, m, ctx, src, dst, weight=None, bias=None):
        n = m.n_norm
        m.n_norm += 1
        self.nc, self.m, self.n, self.src, self.dst, self.weight, self.bias = nc, m, n, src, dst, weight, bias
        self.stats = ctx.enter_context(nc.sbuf_tensor(f"stats{n}", [S, B, 6], F32))
        self.mv = ctx.enter_context(nc.sbuf_tensor(f"mv{n}", [S, B, 2], F32))
        self.ve = ctx.enter_context(nc.sbuf_tensor(f"ve{n}", [S, B], F32))
        self.rstd = ctx.enter_context(nc.sbuf_tensor(f"rstd{n}", [S, B], F32))
        self.ps = ctx.enter_context(nc.psum_tensor(f"norm_ps{n}", [D, T], F32))

    def emit(self, block, complete=None):
        nc, m, n, src, dst, ps = self.nc, self.m, self.n, self.src, self.dst, self.ps
        stats, mv, ve, rstd, weight, bias = self.stats, self.mv, self.ve, self.rstd, self.weight, self.bias
        HB = B // 2

        def copy_turned(engine, half):
            out, in_ = m.XNT[:, half * HALF:(half + 1) * HALF], ps[:, half * HALF:(half + 1) * HALF]
            if engine is nc.vector:
                if weight is None:
                    nc.vector.tensor_copy(out, in_)
                else:
                    nc.vector.tensor_scalar(out, in_, weight, bias, ALU.mult, ALU.add)
            elif weight is None:
                nc.scalar.activation(out, in_, ACT.Copy)
            else:
                nc.scalar.activation(out, in_, ACT.Identity, bias=bias, scale=weight)

        @block.vector
        def _(dve):
            for half in range(2):
                batches = range(half * HB, (half + 1) * HB)
                if complete is not None:
                    dve.wait_ge(*complete(dve, half))
                for b in batches:
                    v = m.dve_steps.inc(nc.vector.bn_stats(stats[:, b, :], src[:, b, :]))
                dve.wait_ge(m.dve_steps.sem, v)
                for b in batches:
                    v = m.dve_steps.inc(nc.vector.bn_aggr(mv[:, b, :], stats[:, b, :]))
                dve.wait_ge(m.dve_steps.sem, v)
                bs = slice(half * HB, (half + 1) * HB)
                nc.vector.tensor_scalar(ve[:, bs], mv[:, bs, 1], EPS, None, ALU.add).then_inc(m.stats_ready, 1)
            for b in range(B):
                if b % HB == 0:
                    dve.wait_ge(m.rstd_ready, 2 * n + b // HB + 1)
                nc.vector.tensor_scalar(dst[:, b, :], src[:, b, :], mv[:, b, 0:1], rstd[:, b:b + 1],
                                        ALU.subtract, ALU.mult).then_inc(m.normed, 1)
            dve.wait_ge(m.turned, 2 * n + 1)
            copy_turned(nc.vector, 0)

        @block.gpsimd
        def _(pool):
            for half in range(2):
                bs = slice(half * HB, (half + 1) * HB)
                pool.wait_ge(m.stats_ready, 2 * n + half + 1)
                nc.gpsimd.tensor_tensor(rstd[:, bs], ve[:, bs], m.neghalf[:, bs], ALU.pow).then_inc(m.rstd_ready, 1)

        @block.tensor
        def _(pe):
            for b in range(B):
                pe.wait_ge(m.normed, n * B + b + 1)
                t = nc.tensor.transpose(ps[:, b * S:(b + 1) * S], dst[:, b, :], m.w("ident"))
                if b % 4 == 3:
                    t.then_inc(m.turned, 1)

        @block.scalar
        def _(act):
            act.wait_ge(m.turned, 2 * n + 2)
            copy_turned(nc.scalar, 1)


def project(nc, m, jobs):
    with ExitStack() as ctx:
        ps = [ctx.enter_context(nc.psum_tensor(f"proj_ps{m.n_proj}_{i}", [128, HALF], F32)) for i in range(4)]
        block = ctx.enter_context(nc.Block())
        base_p, base_e = m.n_proj, m.n_evac
        units = [(j, half) for j in range(len(jobs)) for half in range(T // HALF)]
        m.n_proj += len(units)
        m.n_evac += len(units)
        cols = lambda half: slice(half * HALF, (half + 1) * HALF)

        @block.tensor
        def _(pe):
            for u, (j, half) in enumerate(units):
                weights, sources = jobs[j][1:3]
                if u >= 4:
                    pe.wait_ge(m.evac, base_e + u - 3)
                for i, (w, s) in enumerate(zip(weights, sources)):
                    t = nc.tensor.matmul(ps[u % 4][0:w.shape[1], :], w, s[:, cols(half)], start=(i == 0),
                                         stop=(i == len(weights) - 1))
                t.then_inc(m.proj, 1)

        @block.scalar
        def _(act):
            for u, (j, half) in enumerate(units):
                out, weights, sources, bias, func = (*jobs[j], None)[:5]
                act.wait_ge(m.proj, base_p + u + 1)
                in_ = ps[u % 4][0:weights[0].shape[1], :]
                out = out(half) if callable(out) else out[:, cols(half)]
                if len(out.shape) == 3:
                    in_ = in_.rearrange("p (b s) -> p b s", b=out.shape[1])
                if bias is None:
                    c = nc.scalar.activation(out, in_, func or ACT.Copy)
                else:
                    c = nc.scalar.activation(out, in_, func or ACT.Identity, bias=bias)
                c.then_inc(m.evac, 1)


def attention_inputs(nc, m, parts, V, v_source=None, v_weight=None, v_bias=None, turn=None, hidden=None,
                     flipped=None):
    call = m.n_proj
    slots = 2 if turn else 4
    units = [(j, half) for j in range(len(parts)) for half in range(2)]
    with ExitStack() as ctx:
        ps = [[ctx.enter_context(nc.psum_tensor(f"in_ps{call}_{i}_{k}", [128, HALF], F32))
               for k in range(2 if turn else 1)] for i in range(slots)]
        pv = ctx.enter_context(nc.psum_tensor(f"val_ps{call}", [S, B, D], F32))
        if hidden is not None:
            ph = ctx.enter_context(nc.psum_tensor(f"hidden_ps{call}", [S, B, S], F32))
            hidden_done = m.sem("hidden_done")
        if flipped is not None:
            pf = [ctx.enter_context(nc.psum_tensor(f"flip_ps{i}", [S, HG, S], F32)) for i in range(2)]
            flip_done, flip_copied = m.sem("flip_done"), m.sem("flip_copied")
        if turn:
            swapped = [ctx.enter_context(nc.sbuf_tensor(f"swapped{call}_{u}", [128, B // 2, S], F32))
                       for u in range(len(units))]
        block = ctx.enter_context(nc.Block())
        base_p, base_e, base_v = m.n_proj, m.n_evac, m.n_values
        m.n_proj += len(units)
        m.n_evac += len(units)
        m.n_values += 2 if v_source is not None else 0
        cols = lambda half: slice(half * HALF, (half + 1) * HALF)
        heads = lambda a: a.rearrange("p b (h d) -> p b h d", h=H)

        @block.tensor
        def _(pe):
            def product(u):
                out, source, *weights = parts[units[u][0]]
                if u >= slots:
                    pe.wait_ge(m.evac, base_e + u - slots + 1)
                for k, w in enumerate(weights[:2 if turn else 1]):
                    t = nc.tensor.matmul(ps[u % slots][k][:], w, source[:, cols(units[u][1])], start=True, stop=True)
                t.then_inc(m.proj, 1)

            for u in range(slots):
                product(u)
            if v_source is not None:
                for b in range(B):
                    t = nc.tensor.matmul(pv[:, b, :], v_source[:, b * S:(b + 1) * S], v_weight, start=True, stop=True)
                    if b % 4 == 3:
                        t.then_inc(m.value_done, 1)
            if hidden is not None:
                for b in range(B):
                    at = slice(b * S, (b + 1) * S)
                    t = nc.tensor.matmul(ph[:, b, :], m.q_mask[:, at], m.k_mask[:, at], start=True, stop=True)
                t.then_inc(hidden_done, 1)
            for u in range(slots, len(units)):
                product(u)
            if flipped is not None:
                for g in range(NG):
                    if g >= 2:
                        pe.wait_ge(flip_copied, g - 1)
                    nc.tensor.matmul(pf[g % 2][:], m.w("flip"), m.pos_bias[:, g * HG:(g + 1) * HG, :], start=True,
                                     stop=True).then_inc(flip_done, 1)

        def copy_values(half, with_bias):
            bs = slice(4 * half, 4 * half + 4)
            out, in_ = V[:, bs, :, 0:DH], heads(pv[:, bs, :])
            if with_bias:
                bias = v_bias.rearrange("p (h d) -> p h d", h=H).unsqueeze(1).to_broadcast([S, B // 2, H, DH])
                nc.vector.tensor_tensor(out, in_, bias, ALU.add)
            else:
                nc.scalar.activation(out, in_, ACT.Copy)

        @block.vector
        def _(dve):
            if turn:
                for u, (j, half) in enumerate(units):
                    out = parts[j][0][:, cols(half)].rearrange("p (b s) -> p b s", b=B // 2)
                    product = [t[:].rearrange("p (b s) -> p b s", b=B // 2) for t in ps[u % slots]]
                    dve.wait_ge(m.proj, base_p + u + 1)
                    nc.vector.tensor_tensor(out, product[0], turn[0](half), ALU.mult)
                    nc.vector.tensor_tensor(swapped[u][:], product[1], turn[1](half), ALU.mult).then_inc(m.evac, 1)
            if v_source is None:
                nc.vector.tensor_copy(V[:, :, :, 0:DH], heads(m.XN[:]))
            elif v_bias is not None:
                for half in range(2):
                    dve.wait_ge(m.value_done, base_v + half + 1)
                    copy_values(half, True)

        @block.gpsimd
        def _(pool):
            nc.gpsimd.memset(V[:, :, :, DH:DH + 1], 1.0)
            if turn:
                for u, (j, half) in enumerate(units):
                    pool.wait_ge(m.evac, base_e + u + 1)
                    out = parts[j][0][:, cols(half)].rearrange("p (b s) -> p b s", b=B // 2)
                    nc.gpsimd.tensor_tensor(out, out, swapped[u][:], ALU.add)

        @block.scalar
        def _(act):
            if not turn:
                for u, (j, half) in enumerate(units):
                    out, bias = parts[j][0][:, cols(half)], parts[j][3]
                    act.wait_ge(m.proj, base_p + u + 1)
                    nc.scalar.activation(out, ps[u % slots][0][:], ACT.Identity, bias=bias).then_inc(m.evac, 1)
            if v_source is not None and v_bias is None:
                for half in range(2):
                    act.wait_ge(m.value_done, base_v + half + 1)
                    copy_values(half, False)
            if hidden is not None:
                act.wait_ge(hidden_done, 1)
                nc.scalar.activation(hidden[:], ph[:], ACT.Copy)
            if flipped is not None:
                for g in range(NG):
                    act.wait_ge(flip_done, g + 1)
                    nc.scalar.activation(flipped[:, g * HG:(g + 1) * HG, :], pf[g % 2][:],
                                         ACT.Copy).then_inc(flip_copied, 1)


def attend(nc, m, QT, KT, V, O, bias):
    call = m.n_attn
    m.n_attn += 1
    U0, B0 = call * B * NG, call * B
    scale = float(DH) ** -0.5
    with ExitStack() as ctx:
        sb = lambda name, shape, dt=F32: ctx.enter_context(nc.sbuf_tensor(f"{name}_a{call}", shape, dt))
        Qs = [sb(f"Qs{i}", [D, S]) for i in range(2)]
        KH = [sb(f"KH{i}", [D, H, S]) for i in range(2)]
        shifted = [sb(f"shifted{i}", [S, HG, S]) for i in range(4)]
        PTs = [sb(f"PTs{i}", [S, HG, S]) for i in range(2)]
        nmax = sb("nmax", [S, 2, HG])
        rsum = sb("rsum", [S, 2, H])
        scores = [ctx.enter_context(nc.psum_tensor(f"scores{call}_{i}", [S, HG, S], F32)) for i in range(4)]
        PT = [ctx.enter_context(nc.psum_tensor(f"PT{call}_{i}", [S, HG, S], F32)) for i in range(2)]
        PO = ctx.enter_context(nc.psum_tensor(f"PO{call}", [S, 2, HALF], F32))
        block = ctx.enter_context(nc.Block())
        ident = m.w("ident")
        SC = 2 * NG
        LAST = B // 2 - 1


        def within(u, limit):
            return limit is None or u < limit

        @block.gpsimd
        def _(pool):
            with pool.Fori(0, B // 2) as i:
                for lane in range(2):
                    pool.wait_ge(m.scored.sem, i * SC + (U0 + NG * lane + NG))
                    at = bass.ds(i * (2 * S) + lane * S, S)
                    nc.gpsimd.tensor_copy(Qs[lane][:], QT[:, at]).then_inc(m.kq.sem, 1)
                    for g in range(NG):
                        heads = slice(g * HG, (g + 1) * HG)
                        nc.gpsimd.tensor_tensor(KH[lane][:, heads, :], bcast_mid(KT[:, at], HG),
                                                bcast_last(m.w("head_mask")[:, heads], S),
                                                ALU.mult).then_inc(m.kq.sem, 1)

        @block.tensor
        def _(pe):
            def score(i, u):
                lane, g = u // NG % 2, u % NG
                n = i * SC + (U0 + u)
                pe.wait_ge(m.kq.sem, i * (2 * (NG + 1)) + ((B0 + u // NG) * (NG + 1) + g + 2 + m.kq.depth))
                pe.wait_ge(m.shifted.sem, m.shifted.free(n))
                t = nc.tensor.matmul(scores[u % 4][:], Qs[lane][:], KH[lane][:, g * HG:(g + 1) * HG, :],
                                     start=True, stop=True)
                t.then_inc(m.scored.sem, 1)

            def turn(i, u):
                n = i * SC + (U0 + u)
                pe.wait_ge(m.exped.sem, m.exped.ended(n))
                pe.wait_ge(m.pt_copied.sem, m.pt_copied.free(n))
                for j in range(HG):
                    t = nc.tensor.transpose(PT[u % 2][:, j, :], shifted[u % 4][:, j, :], ident)
                t.then_inc(m.p_turned.sem, 1)

            def weigh(i, u):
                lane, g = u // NG, u % NG
                n = i * SC + (U0 + u)
                if g == 0:
                    pe.wait_ge(m.out_done.sem, m.out_done.free(i * 2 + (B0 + lane)))
                pe.wait_ge(m.pt_copied.sem, m.pt_copied.ended(n))
                for j in range(HG):
                    h = g * HG + j
                    t = nc.tensor.matmul(PO[:, lane, h * (DH + 1):(h + 1) * (DH + 1)], PTs[u % 2][:, j, :],
                                         V[:, bass.ds(i * 2 + lane, 1), h, :].squeeze(1), start=True, stop=True)
                t.then_inc(m.weighed.sem, 1)

            def body(i, limit):
                for u in range(SC):
                    if within(u + 4, limit):
                        score(i, u + 4)
                    weigh(i, u)
                    if within(u + 2, limit):
                        turn(i, u + 2)

            for u in range(4):
                score(0, u)
            for u in range(2):
                turn(0, u)
            with pe.Fori(0, LAST) as i:
                body(i, None)
            body(LAST, SC)

        @block.vector
        def _(dve):
            def add(i, u):
                n = i * SC + (U0 + u)
                dve.wait_ge(m.scored.sem, m.scored.ended(n))
                dve.wait_ge(m.p_turned.sem, m.p_turned.free(n))
                nc.vector.tensor_tensor(shifted[u % 4][:], scores[u % 4][:], bias(u % NG, i * 2 + u // NG),
                                        ALU.add).then_inc(m.biased, 1)

            def shift(i, u, limit):
                n = i * SC + (U0 + u)
                x = shifted[u % 4][:]
                dve.wait_ge(m.biased, n + 1)
                nc.vector.tensor_reduce(nmax[:, u % 2, :], x, AX.X, ALU.max).then_inc(m.maxed, 1)
                if within(u + 1, limit):
                    add(i, u + 1)
                dve.wait_ge(m.maxed, n + 1)
                nc.vector.tensor_tensor(x, x, bcast_last(nmax[:, u % 2, :], S), ALU.subtract).then_inc(m.shifted.sem, 1)

            def normalise(i, lane):
                n = i * SC + (U0 + NG * lane + NG - 1)
                dve.wait_ge(m.weighed.sem, m.weighed.ended(n))
                po = PO[:, lane, 0:H * (DH + 1)].rearrange("p (h e) -> p h e", h=H)
                m.dve_steps.done(dve, nc.vector.reciprocal(rsum[:, lane, :], po[:, :, DH]))
                nc.vector.tensor_tensor(
                    O[:, bass.ds(i * 2 + lane, 1), :].squeeze(1).rearrange("p (h d) -> p h d", h=H),
                    po[:, :, 0:DH], bcast_last(rsum[:, lane, :], DH), ALU.mult).then_inc(m.out_done.sem, 1)

            def body(i, limit):
                for u in range(SC):
                    if within(u + NG, limit):
                        shift(i, u + NG, limit)
                    if u % NG == NG - 1:
                        normalise(i, u // NG)

            add(0, 0)
            for u in range(NG):
                shift(0, u, None)
            with dve.Fori(0, LAST) as i:
                m.dve_steps.enter(i, 2)
                body(i, None)
                m.dve_steps.leave(LAST)
            body(LAST, SC)

        @block.scalar
        def _(act):
            def exp(i, u):
                n = i * SC + (U0 + u)
                act.wait_ge(m.shifted.sem, m.shifted.ended(n))
                nc.scalar.activation(shifted[u % 4][:], shifted[u % 4][:], ACT.Exp,
                                     scale=scale).then_inc(m.exped.sem, 1)

            def copy(i, u):
                n = i * SC + (U0 + u)
                act.wait_ge(m.p_turned.sem, m.p_turned.ended(n))
                act.wait_ge(m.weighed.sem, m.weighed.free(n))
                nc.scalar.activation(PTs[u % 2][:], PT[u % 2][:], ACT.Copy).then_inc(m.pt_copied.sem, 1)

            def body(i, limit):
                for u in range(SC):
                    if within(u + 3, limit):
                        exp(i, u + 3)
                    if within(u + 2, limit):
                        copy(i, u + 2)

            m.load_table(act, ACT.Exp)
            exp(0, 0)
            for u in range(2):
                exp(0, u + 1)
                copy(0, u)
            with act.Fori(0, LAST) as i:
                m.act_steps.enter(i, 1)
                m.load_table(act, ACT.Exp)
                body(i, None)
                m.act_steps.leave(LAST)
            body(LAST, SC)


def out_project(nc, m, O, weight, bias_row=None, bias_times=1.0, target=None, norm=None):
    Y = m.X if target is None else target
    n = m.n_tail
    m.n_tail += 1
    with ExitStack() as ctx:
        OT = ctx.enter_context(nc.sbuf_tensor(f"OT{n}", [D, T], F32))
        ps = ctx.enter_context(nc.psum_tensor(f"tail_t{n}", [D, T], F32))
        py = ctx.enter_context(nc.psum_tensor(f"tail_y{n}", [S, B, D], F32))
        norm = Norm(nc, m, ctx, *(norm or (m.X, m.XN)))
        block = ctx.enter_context(nc.Block())
        base_p, base_e = m.n_proj, m.n_evac
        m.n_proj += 4
        m.n_evac += 2
        halves = [slice(0, HALF), slice(HALF, T)]

        @block.tensor
        def _(pe):
            for b in range(B):
                t = nc.tensor.transpose(ps[:, b * S:(b + 1) * S], O[:, b, :], m.w("ident"))
                if b % 4 == 3:
                    t.then_inc(m.proj, 1)
            for b in range(B):
                if b % 4 == 0:
                    pe.wait_ge(m.evac, base_e + b // 4 + 1)
                t = nc.tensor.matmul(py[:, b, :], OT[:, b * S:(b + 1) * S], weight, start=True, stop=True)
                if b % 4 == 3:
                    t.then_inc(m.proj, 1)

        @block.scalar
        def _(act):
            for half in range(2):
                act.wait_ge(m.proj, base_p + half + 1)
                nc.scalar.activation(OT[:, halves[half]], ps[:, halves[half]], ACT.Copy).then_inc(m.evac, 1)

        @block.vector
        def _(dve):
            if bias_row is not None:
                m.dve_steps.done(dve, nc.vector.scalar_tensor_tensor(
                    out=Y[:], in0=bcast_mid(bias_row, B), scalar=bias_times, in1=Y[:], op0=ALU.mult, op1=ALU.add))

        def add(dve, half):
            dve.wait_ge(m.proj, base_p + 3 + half)
            bs = slice(4 * half, 4 * half + 4)
            return m.dve_steps.sem, m.dve_steps.inc(
                nc.vector.tensor_tensor(Y[:, bs, :], Y[:, bs, :], py[:, bs, :], ALU.add))

        norm.emit(block, add)


class EarlyWork:

    def __init__(self, nc, m, ctx, ps):
        self.nc, self.m, self.ps = nc, m, ps[0:H, 0:2 * S]
        self.table = ctx.enter_context(nc.sbuf_tensor("table", [128, 2, H], F32))
        self.tableT = ctx.enter_context(nc.sbuf_tensor("tableT", [H, 2 * S], F32))
        self.mask = m.O[:].rearrange("p b d -> p (b d)")

    def emit(self, block):
        nc, m, table, tableT, mask, ps = self.nc, self.m, self.table, self.tableT, self.mask, self.ps
        summed, turned, copied, stored = (m.sem(n) for n in ("table_summed", "table_turned", "table_copied",
                                                             "table_stored"))
        widened = m.sem("mask_widened")
        tab = m.dram["rel_table"]

        @block.sync
        def _(sp):
            sp.wait_ge(copied, 1)
            sp.dma_start(tab, tableT[:]).then_inc(stored, 16)
            sp.wait_ge(stored, 16)
            sp.dma_start(m.pos_bias[:], bass.AP(tab.tensor, tab.offset, [[1, S], [2 * S, H], [1, S]])
                         ).then_inc(m.bias_loaded, 16)

        @block.vector
        def _(dve):
            dve.wait_ge(m.loaded_rest, 96)
            nc.vector.tensor_reduce(table[:], m.rel[:].rearrange("p c (h d) -> p c h d", h=H), AX.X,
                                    ALU.add).then_inc(summed, 1)

        @block.tensor
        def _(pe):
            pe.wait_ge(summed, 1)
            for c in range(2):
                t = nc.tensor.transpose(ps[:, c * 128:(c + 1) * 128], table[:, c, :], m.w("ident"))
            t.then_inc(turned, 1)
            pe.wait_ge(copied, 1)

        @block.scalar
        def _(act):
            act.wait_ge(m.loaded_rest, 96)
            nc.scalar.activation(mask, m.mask8[:], ACT.Copy).then_inc(widened, 1)
            act.wait_ge(widened, 1)
            nc.scalar.activation(m.q_mask[0:1, :], mask[0:1, :], ACT.Copy)
            nc.scalar.activation(m.k_mask[0:1, :], mask[0:1, :], ACT.Copy, scale=BIG)
            act.wait_ge(turned, 1)
            nc.scalar.activation(tableT[:], ps, ACT.Copy).then_inc(copied, 1)

        @block.gpsimd
        def _(pool):
            pool.wait_ge(widened, 1)
            view = mask.rearrange("p (b s) -> p b s", b=B)
            for out, name in ((m.masked_cos, "rope0c"), (m.masked_sin, "rope0s")):
                nc.gpsimd.tensor_tensor(out[:], view, bcast_mid(m.w(name), B), ALU.mult)


def add_products(nc, m, terms, bias_row=None):
    with ExitStack() as ctx:
        py = ctx.enter_context(nc.psum_tensor(f"sum_y{m.n_proj}", [S, B, D], F32))
        norm = Norm(nc, m, ctx, m.X, m.XN)
        block = ctx.enter_context(nc.Block())
        base = m.n_proj
        m.n_proj += 2

        @block.tensor
        def _(pe):
            for b in range(B):
                for k, (source, w) in enumerate(terms):
                    t = nc.tensor.matmul(py[:, b, :], source(b), w, start=(k == 0), stop=(k == len(terms) - 1))
                if b % 4 == 3:
                    t.then_inc(m.proj, 1)

        @block.vector
        def _(dve):
            if bias_row is not None:
                m.dve_steps.done(dve, nc.vector.tensor_tensor(m.X[:], m.X[:], bcast_mid(bias_row, B), ALU.add))

        def add(dve, half):
            dve.wait_ge(m.proj, base + half + 1)
            bs = slice(4 * half, 4 * half + 4)
            return m.dve_steps.sem, m.dve_steps.inc(
                nc.vector.tensor_tensor(m.X[:, bs, :], m.X[:, bs, :], py[:, bs, :], ALU.add))

        norm.emit(block, add)


def mamba_stage(nc, m):
    norm_stage(nc, m, m.X, m.XN)
    norm_stage(nc, m, m.XN, m.O, m.w("ln_w"), m.w("ln_b"))
    with ExitStack() as outer:
        sb = lambda name, shape, dt=F32: outer.enter_context(nc.sbuf_tensor(name, shape, dt))
        u = sb("u", [128, IC, T])
        gate = sb("gate", [128, IC, T])
        delta = sb("delta", [128, IC, T])
        du = sb("du", [128, IC, T])
        A = sb("A", [128, IC, STATE])
        BC = [sb(f"BC{i}", [2 * STATE, T], BF16) for i in range(3)]
        y = sb("y", [128, IC, T])
        mamba_inputs(nc, m, u, gate, delta, du, A, BC, y)
        Y = [outer.enter_context(nc.psum_tensor(f"Y{c}", [128, T], F32)) for c in range(IC)]
        scan_block(nc, m, outer, delta, du, A, BC, y, Y)
        mamba_output(nc, m, gate, y, Y)


def mamba_inputs(nc, m, u, gate, delta, du, A, BC, y):
    with ExitStack() as ctx:
        sb = lambda name, shape, dt=F32: ctx.enter_context(nc.sbuf_tensor(name, shape, dt))
        ps = lambda name, rows=128: ctx.enter_context(nc.psum_tensor(name, [rows, HALF], F32))
        padded = [sb(f"padded{c}", [128, B, S + TAPS - 1]) for c in range(IC)]
        conv = sb("conv", [128, IC, T])
        BCf, dt_low = sb("BCf", [2 * STATE, T]), sb("dt_low", [RANK, T])
        low, e, w, ln_w = (sb(name, [128, IC, T]) for name in ("low", "e", "w", "ln_w_"))
        rest, mid = sb("rest", [2 * STATE, T]), sb("mid", [2 * STATE, T], BF16)
        Xp, Gp, Dp = ([ps(f"{name}{c}") for c in range(IC)] for name in ("Xp", "Gp", "Dp"))
        BCp, DTp = ps("BCp"), ps("DTp", RANK)
        (pads_ready, x_done, x_copied, g_done, g_copied, conv_done, u_ready, dt_done, dt_copied, bc_done, bc_copied,
         delta_done, delta_copied, low_ready, e_ready, w_ready, ln_ready, delta_ready, high_ready, rest_ready,
         mid_ready) = (m.sem(f"mamba_{n}") for n in (
             "pads_ready", "x_done", "x_copied", "g_done", "g_copied", "conv_done", "u_ready", "dt_done", "dt_copied",
             "bc_done", "bc_copied", "delta_done", "delta_copied", "low_ready", "e_ready", "w_ready", "ln_ready",
             "delta_ready", "high_ready", "rest_ready", "mid_ready"))
        is_b, is_c = slice(0, STATE), slice(STATE, 2 * STATE)
        conv_w = m.w("conv_w").rearrange("p (c k) -> p c k", c=IC)
        W_in, W_dt = m.w("W_in"), m.w("W_dt", slice(0, RANK))
        W_x = m.w("W_xproj").rearrange("p (c n) -> p c n", c=IC)
        cols = [slice(0, HALF), slice(HALF, T)]
        HB = B // 2
        halves = range(2)
        block = ctx.enter_context(nc.Block())

        @block.tensor
        def _(pe):
            for ps, at, done, copied in ((Xp, 0, x_done, x_copied), (Gp, INNER, g_done, g_copied)):
                for h in halves:
                    for c in range(IC):
                        if h:
                            pe.wait_ge(copied, c + 1)
                        weight = W_in[:, at + c * 128:at + (c + 1) * 128]
                        nc.tensor.matmul(ps[c][:], weight, m.XNT[:, cols[h]], start=True, stop=True).then_inc(done, 1)
            for h in halves:
                pe.wait_ge(u_ready, h + 1)
                if h:
                    pe.wait_ge(bc_copied, 1)
                for ps, at, done in ((DTp, slice(0, RANK), dt_done), (BCp, slice(RANK, RANK + 2 * STATE), bc_done)):
                    for c in range(IC):
                        t = nc.tensor.matmul(ps[:], W_x[:, c, at], u[:, c, cols[h]], start=(c == 0), stop=(c == IC - 1))
                    t.then_inc(done, 1)
                pe.wait_ge(dt_copied, h + 1)
                if h:
                    pe.wait_ge(delta_copied, IC)
                for c in range(IC):
                    nc.tensor.matmul(Dp[c][:], W_dt[:, c * 128:(c + 1) * 128], dt_low[:, cols[h]], start=True,
                                     stop=True).then_inc(delta_done, 1)

        @block.scalar
        def _(act):
            for h in halves:
                for c in range(IC):
                    act.wait_ge(x_done, h * IC + c + 1)
                    nc.scalar.activation(padded[c][:, h * HB:(h + 1) * HB, TAPS - 1:],
                                         Xp[c][:].rearrange("p (b s) -> p b s", b=HB), ACT.Copy).then_inc(x_copied, 1)
            for h in halves:
                for c in range(IC):
                    act.wait_ge(g_done, h * IC + c + 1)
                    nc.scalar.activation(gate[:, c, cols[h]], Gp[c][:], ACT.Silu).then_inc(g_copied, 1)
            def silu(h):
                act.wait_ge(conv_done, (h + 1) * IC)
                nc.scalar.activation(u[:, :, cols[h]], conv[:, :, cols[h]], ACT.Silu).then_inc(u_ready, 1)

            silu(0)
            for h in halves:
                act.wait_ge(dt_done, h + 1)
                nc.scalar.activation(dt_low[:, cols[h]], DTp[:], ACT.Copy).then_inc(dt_copied, 1)
                if h == 0:
                    silu(1)
                act.wait_ge(bc_done, h + 1)
                nc.scalar.activation(BCf[:, cols[h]], BCp[:], ACT.Copy).then_inc(bc_copied, 1)
                for c in range(IC):
                    act.wait_ge(delta_done, h * IC + c + 1)
                    nc.scalar.activation(delta[:, c, cols[h]], Dp[c][:], ACT.Identity,
                                         bias=m.w("b_dt")[:, c:c + 1]).then_inc(delta_copied, 1)
            act.wait_ge(bc_copied, 2)
            for rows, out in ((is_b, BC[0]), (is_c, BC[1])):
                nc.scalar.activation(out[rows, :], BCf[rows, :], ACT.Copy).then_inc(high_ready, 1)
            for h in halves:
                act.wait_ge(low_ready, h + 1)
                nc.scalar.activation(e[:, :, cols[h]], low[:, :, cols[h]], ACT.Exp).then_inc(e_ready, 1)
            a = A[:].rearrange("p c n -> p (c n)")
            m.act_steps.done(act, nc.scalar.activation(a, m.w("A_log"), ACT.Exp))
            nc.scalar.activation(a, a, ACT.Copy, scale=-1.0)
            for h in halves:
                act.wait_ge(w_ready, h + 1)
                nc.scalar.activation(ln_w[:, :, cols[h]], w[:, :, cols[h]], ACT.Ln).then_inc(ln_ready, 1)
            act.wait_ge(rest_ready, 2)
            nc.scalar.activation(mid[:], rest[:], ACT.Copy).then_inc(mid_ready, 1)
            act.wait_ge(u_ready, 2)
            nc.scalar.activation(y[:, 0, :], u[:, 0, :], ACT.Copy, scale=m.w("Dskip")[:, 0:1])
            act.wait_ge(mid_ready, 1)
            nc.scalar.activation(BC[0][is_c, :], mid[is_b, :], ACT.Copy)
            nc.scalar.activation(BC[1][is_b, :], mid[is_c, :], ACT.Copy)

        @block.vector
        def _(dve):
            steps = m.dve_steps
            before = [None] * IC
            dve.wait_ge(pads_ready, IC)
            for h in halves:
                for k in range(TAPS):
                    for c in range(IC):
                        if k == 0:
                            dve.wait_ge(x_copied, h * IC + c + 1)
                        else:
                            dve.wait_ge(steps.sem, before[c])
                        out = conv[:, c, cols[h]].rearrange("p (b s) -> p b s", b=HB)
                        tap = padded[c][:, h * HB:(h + 1) * HB, k:k + S]
                        if k == 0:
                            t = nc.vector.tensor_scalar(out, tap, conv_w[:, c, 0:1], m.w("conv_b")[:, c:c + 1],
                                                        ALU.mult, ALU.add)
                        else:
                            t = nc.vector.scalar_tensor_tensor(out=out, in0=tap, scalar=conv_w[:, c, k:k + 1],
                                                               in1=out, op0=ALU.mult, op1=ALU.add)
                        if k == TAPS - 1:
                            t.then_inc(conv_done, 1)
                        else:
                            before[c] = steps.inc(t)
            at = lambda a, h: a[:, :, cols[h]]
            for h in halves:
                dve.wait_ge(delta_copied, (h + 1) * IC)
                nc.vector.scalar_tensor_tensor(out=at(low, h), in0=at(delta, h), scalar=-1.0, in1=at(delta, h),
                                               op0=ALU.mult, op1=ALU.min).then_inc(low_ready, 1)
            for h in halves:
                dve.wait_ge(e_ready, h + 1)
                nc.vector.tensor_scalar(at(w, h), at(e, h), 1.0, None, ALU.add).then_inc(w_ready, 1)
            v = []
            for h in halves:
                dve.wait_ge(w_ready, h + 1)
                v.append(steps.inc(nc.vector.scalar_tensor_tensor(out=at(low, h), in0=at(w, h), scalar=-1.0, in1=at(e, h),
                                                                  op0=ALU.add, op1=ALU.subtract)))
            for h in halves:
                dve.wait_ge(steps.sem, v[h])
                dve.wait_ge(ln_ready, h + 1)
                v[h] = steps.inc(nc.vector.tensor_tensor(at(low, h), at(ln_w, h), at(low, h), ALU.subtract))
            for h in halves:
                dve.wait_ge(steps.sem, v[h])
                nc.vector.scalar_tensor_tensor(out=at(delta, h), in0=at(delta, h), scalar=0.0, in1=at(low, h),
                                               op0=ALU.max, op1=ALU.add).then_inc(delta_ready, 1)
            for h in halves:
                dve.wait_ge(delta_ready, h + 1)
                nc.vector.tensor_tensor(at(du, h), at(delta, h), at(u, h), ALU.mult)

        @block.gpsimd
        def _(pool):
            for c in range(IC):
                nc.gpsimd.memset(padded[c][:, :, 0:TAPS - 1], 0.0).then_inc(pads_ready, 1)
            nc.gpsimd.tensor_tensor(m.X[:], m.X[:], m.XN[:], ALU.add)
            pool.wait_ge(u_ready, 2)
            m.pool_steps.done(pool, nc.gpsimd.tensor_scalar(y[:, 1, :], u[:, 1, :], m.w("Dskip")[:, 1:2], None,
                                                            ALU.mult))
            for k, (rows, high) in enumerate(((is_b, BC[0]), (is_c, BC[1]))):
                pool.wait_ge(high_ready, k + 1)
                nc.gpsimd.tensor_tensor(rest[rows, :], BCf[rows, :], high[rows, :], ALU.subtract).then_inc(rest_ready, 1)
            pool.wait_ge(rest_ready, 2)
            pool.wait_ge(mid_ready, 1)
            nc.gpsimd.tensor_tensor(BC[2][:], rest[:], mid[:], ALU.subtract)


def mamba_output(nc, m, gate, y, Y):
    W_out = m.w("W_out").rearrange("p (c n) -> p c n", c=IC)
    with ExitStack() as ctx:
        py = ctx.enter_context(nc.psum_tensor("mamba_y", [S, B, D], F32))
        norm = Norm(nc, m, ctx, m.X, m.XN)
        early = EarlyWork(nc, m, ctx, norm.ps)
        gated = m.sem("mamba_gated")
        block = ctx.enter_context(nc.Block())
        base = m.n_proj
        m.n_proj += 2

        @block.vector
        def _(dve):
            for half in range(2):
                at = slice(half * HALF, (half + 1) * HALF)
                v = m.dve_steps.inc(nc.vector.tensor_tensor(y[:, 0, at], y[:, 0, at], Y[0][:, at], ALU.add))
                nc.vector.tensor_tensor(y[:, 1, at], Y[1][:, at], gate[:, 1, at], ALU.mult).then_inc(gated, 1)
                dve.wait_ge(m.dve_steps.sem, v)
                nc.vector.tensor_tensor(y[:, 0, at], y[:, 0, at], gate[:, 0, at], ALU.mult).then_inc(gated, 1)

        @block.tensor
        def _(pe):
            for b in range(B):
                if b % 4 == 0:
                    pe.wait_ge(gated, 2 * (b // 4 + 1))
                for c in range(IC):
                    t = nc.tensor.matmul(py[:, b, :], y[:, c, b * S:(b + 1) * S], W_out[:, c, :], start=(c == 0),
                                         stop=(c == IC - 1))
                if b % 4 == 3:
                    t.then_inc(m.proj, 1)

        early.emit(block)

        def add(dve, half):
            dve.wait_ge(m.proj, base + half + 1)
            bs = slice(4 * half, 4 * half + 4)
            return m.dve_steps.sem, m.dve_steps.inc(
                nc.vector.tensor_tensor(m.X[:, bs, :], m.X[:, bs, :], py[:, bs, :], ALU.add))

        norm.emit(block, add)


def scan_block(nc, m, outer, delta, du, A, BC, y, Y):
    sb = lambda name, shape, dt=F32: outer.enter_context(nc.sbuf_tensor(name, shape, dt))
    decay = [[sb(f"decay{c}{p}", [128, B, S]) for p in range(2)] for c in range(IC)]
    inp = [sb(f"inp{c}", [128, T]) for c in range(IC)]
    h = [[sb(f"h{c}{p}", [128, T]) for p in range(2)] for c in range(IC)]
    hC = [[sb(f"hC{c}{p}", [128, T]) for p in range(2)] for c in range(IC)]
    Cs = [sb(f"Cs{p}", [128, T]) for p in range(2)]
    ps_ctx = ExitStack()
    Bp = ps_ctx.enter_context(nc.psum_tensor("Bp", [128, T], F32))
    Cp = ps_ctx.enter_context(nc.psum_tensor("Cp", [128, T], F32))
    PASS = 4
    spread_b, spread_c = Ring(m.sem("spread_b"), 1), Ring(m.sem("spread_c"), 1)
    c_copied, decayed = Ring(m.sem("c_copied"), 2), Ring(m.sem("decayed"), 4)
    fed, scanned, weighed = Ring(m.sem("fed"), 4), Ring(m.sem("scanned"), 4), Ring(m.sem("c_weighed"), 4)
    zeroed = m.sem("zeroed")
    first_summed, others_summed, summed1 = m.sem("first_summed"), m.sem("others_summed"), m.sem("summed1")
    halves = [slice(0, HALF), slice(HALF, T)]
    with nc.Block() as block:
        @block.gpsimd
        def _(pool):
            for ring in (weighed,):
                pool.sem_inc(ring.sem, ring.start)
            for c in range(IC):
                for p in range(2):
                    nc.gpsimd.memset(decay[c][p][:, :, 0:1], 0.0)
            for c in range(IC):
                nc.gpsimd.memset(hC[c][0][:], 0.0)

        @block.tensor
        def _(pe):
            for ring in (spread_b, spread_c):
                pe.sem_inc(ring.sem, ring.start)
            for half in halves:
                nc.tensor.matmul(Y[1][:, half], m.w("ident"), y[:, 1, half], start=True, stop=False,
                                 skip_group_check=True)
            pe.wait_ge(zeroed, 1)
            for half in halves:
                nc.tensor.matmul(Y[0][:, half], m.identb[:], hC[0][1][:, 0:HALF // 2].bitcast(BF16), start=True,
                                 stop=False, skip_group_check=True)

        @block.scalar
        def _(act):
            for ring in (c_copied, decayed):
                act.sem_inc(ring.sem, ring.start)

        @block.vector
        def _(dve):
            for ring in (fed, scanned):
                dve.sem_inc(ring.sem, ring.start)
            dve.sem_inc(first_summed, 1)
            for c in range(IC):
                nc.vector.memset(hC[c][1][:], 0.0).then_inc(zeroed, 1)

    with nc.Block() as block:
        @block.tensor
        def _(pe):
            def spread(out, n, c):
                for half in range(2):
                    for part, row in ((m.select2[:, bass.ds(n, 1)], BC[c]),
                                      (m.identb[:, bass.ds(n + c * STATE, 1)], BC[2])):
                        t = nc.tensor.matmul(out[:, halves[half]], part.to_broadcast([128, 128]),
                                             row[:, halves[half]], start=(row is BC[c]), stop=(row is BC[2]))
                return t

            def add(c, p, stop=False):
                for half in range(2):
                    t = nc.tensor.matmul(Y[c][:, halves[half]], m.w("ident"), hC[c][p][:, halves[half]],
                                         start=False, stop=stop, skip_group_check=True)
                return t

            with pe.Fori(0, STATE // PASS) as i:
                for k in range(PASS):
                    n, p = i * PASS + k, k % 2
                    if k != 2:
                        pe.wait_ge(weighed.sem, i * (2 * PASS) + (2 * k + 1))
                        add(0, p).then_inc(others_summed, 1)
                    pe.wait_ge(fed.sem, i * (2 * PASS) + (2 * k + 4))
                    spread(Bp, n, 0).then_inc(spread_b.sem, 1)
                    pe.wait_ge(c_copied.sem, n + 2)
                    spread(Cp, n, 1).then_inc(spread_c.sem, 1)
                    pe.wait_ge(weighed.sem, i * (2 * PASS) + (2 * k + 2))
                    add(1, p).then_inc(summed1, 1)
            pe.wait_ge(weighed.sem, 2 * STATE + weighed.depth)
            for c in range(IC):
                add(c, 0)
                add(c, 1, stop=True)

        @block.scalar
        def _(act):
            with act.Fori(0, STATE // PASS) as i:
                for k in range(PASS):
                    n, p = i * PASS + k, k % 2
                    for c in range(IC):
                        use = i * (2 * PASS) + (2 * k + c)
                        act.wait_ge(scanned.sem, scanned.free(use))
                        nc.scalar.activation(
                            decay[c][p][:, :, 1:S], delta[:, c, :].rearrange("p (b s) -> p b s", b=B)[:, :, 1:S],
                            ACT.Exp, scale=A[:, c, bass.ds(n, 1)]).then_inc(decayed.sem, 1)
                        if c == 0:
                            act.wait_ge(spread_c.sem, spread_c.ended(n))
                            act.wait_ge(weighed.sem, i * (2 * PASS) + (2 * k + 2))
                            nc.scalar.activation(Cs[p][:], Cp[:], ACT.Copy).then_inc(c_copied.sem, 1)

        @block.vector
        def _(dve):
            with dve.Fori(0, STATE // PASS) as i:
                for k in range(PASS):
                    n, p = i * PASS + k, k % 2
                    dve.wait_ge(spread_b.sem, spread_b.ended(n))
                    for c in range(IC):
                        use = i * (2 * PASS) + (2 * k + c)
                        dve.wait_ge(scanned.sem, scanned.ended(use) - 2)
                        nc.vector.tensor_tensor(inp[c][:], du[:, c, :], Bp[:], ALU.mult).then_inc(fed.sem, 1)
                    for c in range(IC):
                        use = i * (2 * PASS) + (2 * k + c)
                        dve.wait_ge(fed.sem, fed.ended(use))
                        dve.wait_ge(decayed.sem, decayed.ended(use))
                        dve.wait_ge(weighed.sem, weighed.free(use))
                        nc.vector.tensor_tensor_scan(
                            h[c][p][:], decay[c][p][:].rearrange("p b s -> p (b s)"), inp[c][:], 0.0,
                            ALU.mult, ALU.add).then_inc(scanned.sem, 1)
                    if k == 1:
                        dve.wait_ge(weighed.sem, i * (2 * PASS) + (2 * k - 1 + weighed.depth))
                        dve.wait_ge(first_summed, i + 1)
                        nc.vector.tensor_tensor(y[:, 0, :], y[:, 0, :], hC[0][0][:], ALU.add).then_inc(first_summed, 1)

        @block.gpsimd
        def _(pool):
            with pool.Fori(0, STATE // PASS) as i:
                for k in range(PASS):
                    n, p = i * PASS + k, k % 2
                    pool.wait_ge(c_copied.sem, c_copied.ended(n))
                    for c in range(IC):
                        use = i * (2 * PASS) + (2 * k + c)
                        pool.wait_ge(scanned.sem, scanned.ended(use))
                        if c == 1:
                            pool.wait_ge(summed1, n + 1)
                        elif k == 2:
                            pool.wait_ge(first_summed, i + 2)
                        else:
                            pool.wait_ge(others_summed, i * (PASS - 1) + (k + 1 - k // 2))
                        nc.gpsimd.tensor_tensor(hC[c][p][:], h[c][p][:], Cs[p][:], ALU.mult).then_inc(weighed.sem, 1)
    ps_ctx.close()


class Route:

    def __init__(self, nc, m, ctx, E, weight, kind, comb, rows=()):
        self.nc, self.m, self.E, self.weight, self.kind, self.comb, self.rows = nc, m, E, weight, kind, comb, rows
        self.n = n = m.n_route
        m.n_route += 1
        self.EP = EP = 16 if E > 8 else 8
        sb = lambda name, shape, dt=F32: ctx.enter_context(nc.sbuf_tensor(f"{name}_r{n}", shape, dt))
        self.val, self.eq = sb("val", [S, B, EP]), sb("eq", [S, B, EP])
        self.best, self.index = sb("best", [S, B, 8]), sb("index", [S, B, 8], U32)
        self.indexf, self.wt, self.tmp = sb("indexf", [S, B, 2]), sb("wt", [S, B, 2]), sb("tmp", [S, B])
        self.ps = ctx.enter_context(nc.psum_tensor(f"logits{n}", [S, B, EP], F32))

    def emit(self, block):
        nc, m, n, E, EP, kind, comb = self.nc, self.m, self.n, self.E, self.EP, self.kind, self.comb
        val, eq, best, index, indexf = self.val, self.eq, self.best, self.index, self.indexf
        wt, tmp, ps = self.wt, self.tmp, self.ps
        v = {}

        @block.vector
        def _(dve):
            steps = m.dve_steps
            dve.wait_ge(m.logits_done, n + 1)
            if kind == "sigmoid":
                dve.wait_ge(m.route_exped, n + 1)
                steps.done(dve, nc.vector.tensor_scalar(val[:], val[:], 1.0, None, ALU.add))
                steps.done(dve, nc.vector.reciprocal(val[:], val[:]))
            elif kind == "softmax_all":
                steps.done(dve, nc.vector.memset(val[:], -1.0))
                steps.done(dve, nc.vector.tensor_reduce(tmp[:], ps[:, :, 0:E], AX.X, ALU.max))
                v["shifted"] = steps.inc(nc.vector.tensor_tensor(val[:, :, 0:E], ps[:, :, 0:E], bcast_last(tmp[:], E),
                                                                 ALU.subtract))
                dve.wait_ge(m.route_exped, n + 1)
                steps.done(dve, nc.vector.tensor_reduce(tmp[:], val[:, :, 0:E], AX.X, ALU.add))
                steps.done(dve, nc.vector.reciprocal(tmp[:], tmp[:]))
                steps.done(dve, nc.vector.tensor_tensor(val[:, :, 0:E], val[:, :, 0:E], bcast_last(tmp[:], E),
                                                        ALU.mult))
            else:
                steps.done(dve, nc.vector.tensor_copy(val[:], ps[:]))
                for row in self.rows:
                    steps.done(dve, nc.vector.tensor_tensor(val[:], val[:], bcast_mid(row, B), ALU.add))
            for b in range(B):
                k = steps.inc(nc.vector.max(best[:, b, :], val[:, b, :]))
            dve.wait_ge(steps.sem, k)
            if kind == "softmax_two":
                v["second"] = steps.inc(nc.vector.tensor_tensor(tmp[:], best[:, :, 1], best[:, :, 0], ALU.subtract))
            for b in range(B):
                k = steps.inc(nc.vector.max_index(index[:, b, :], best[:, b, :], val[:, b, :]))
            dve.wait_ge(steps.sem, k)
            steps.done(dve, nc.vector.tensor_copy(indexf[:], index[:, :, 0:2]))
            if kind in ("sigmoid", "softmax_all"):
                eps, times = (1e-20, 2.5) if kind == "sigmoid" else (1e-9, 1.0)
                steps.done(dve, nc.vector.scalar_tensor_tensor(out=tmp[:], in0=best[:, :, 0], scalar=eps,
                                                               in1=best[:, :, 1], op0=ALU.add, op1=ALU.add))
                steps.done(dve, nc.vector.reciprocal(tmp[:], tmp[:]))
                for k in range(2):
                    steps.done(dve, nc.vector.scalar_tensor_tensor(
                        out=wt[:, :, k], in0=best[:, :, k], scalar=times, in1=tmp[:], op0=ALU.mult, op1=ALU.mult))
            else:
                dve.wait_ge(m.route_exped, n + 1)
                steps.done(dve, nc.vector.tensor_scalar(wt[:, :, 0], tmp[:], 1.0, None, ALU.add))
                steps.done(dve, nc.vector.reciprocal(wt[:, :, 0], wt[:, :, 0]))
                steps.done(dve, nc.vector.tensor_tensor(wt[:, :, 1], wt[:, :, 0], tmp[:], ALU.mult))
            for k in range(2):
                out = comb if k == 0 else eq[:]
                steps.done(dve, nc.vector.tensor_tensor(out, bcast_mid(m.w("iota16")[:, 0:EP], B),
                                                        bcast_last(indexf[:, :, k], EP), ALU.is_equal))
                steps.done(dve, nc.vector.tensor_tensor(out, out, bcast_last(wt[:, :, k], EP), ALU.mult))
            steps.done(dve, nc.vector.tensor_tensor(comb, comb, eq[:], ALU.add))
            if kind == "softmax_all":
                steps.done(dve, nc.vector.memset(comb[:, :, E:E + 1], 1.0))
        self.comb_value = m.dve_steps.n

        @block.tensor
        def _(pe):
            for b in range(B):
                t = nc.tensor.matmul(ps[:, b, 0:E], m.XNT[:, b * S:(b + 1) * S], self.weight, start=True, stop=True)
            t.then_inc(m.logits_done, 1)

        @block.scalar
        def _(act):
            if kind == "sigmoid":
                act.wait_ge(m.logits_done, n + 1)
                t = nc.scalar.activation(val[:], ps[:], ACT.Exp, scale=-1.0)
            elif kind == "softmax_all":
                act.wait_ge(m.dve_steps.sem, v["shifted"])
                t = nc.scalar.activation(val[:, :, 0:E], val[:, :, 0:E], ACT.Exp)
            else:
                act.wait_ge(m.dve_steps.sem, v["second"])
                t = nc.scalar.activation(tmp[:], tmp[:], ACT.Exp)
            t.then_inc(m.route_exped, 1)


def expert_stage(nc, m, layer, routed, FC, kind, func, weights, rows=(), b2=None, gated=False, last=False,
                 residual=None):
    E = 8 if gated else routed
    EP = 16 if E > 8 else 8
    E0, S0, U0, H0 = m.n_expert, 2 * m.n_expert, m.n_unit, m.n_hunit
    m.n_expert += E
    m.n_unit += 2 * E * FC
    m.n_hunit += 2 * E * FC if gated else 0
    call = m.n_moe
    m.n_moe += 1
    F = FC * 128
    down = 2 * F if gated else F
    with ExitStack() as ctx:
        sb = lambda name, shape, dt=F32: ctx.enter_context(nc.sbuf_tensor(f"{name}_e{call}", shape, dt))
        comb = sb("comb", [S, B, EP])
        route = Route(nc, m, ctx, routed, m.w(f"{layer}_router"), kind, comb[:], rows)
        W = [sb(f"W{i}", [128, down + F + (0 if gated else FC)]) for i in range(2)]
        hid = [sb(f"hid{i}", [128, FC, HALF]) for i in range(2)]
        silu = [sb(f"silu{i}", [128, HALF]) for i in range(2)]
        G = [ctx.enter_context(nc.psum_tensor(f"G{call}_{i}", [128, HALF], F32)) for i in range(2)]
        U = [ctx.enter_context(nc.psum_tensor(f"U{call}_{i}", [128, HALF], F32)) for i in range(2)] if gated else G
        Y = [ctx.enter_context(nc.psum_tensor(f"Y{call}_{i}", [S, B // 2, D], F32)) for i in range(2)]
        norm = None if last else Norm(nc, m, ctx, m.X, m.XN)
        block = ctx.enter_context(nc.Block())
        route.emit(block)
        unit = lambda i, s, fc: i * (4 * FC) + (s * FC + fc)
        order = [("up", 0), ("up", 1), ("down", 0), ("up", 2), ("down", 1), ("up", 3), ("down", 2), ("down", 3)]

        @block.sync
        def _(sp):
            with sp.Fori(0, E // 2) as i:
                for e in range(2):
                    sp.wait_ge(m.y_done.sem, i * 4 + m.y_done.ended(S0 + 2 * e - 3))
                    sp.dma_start(W[e][:], weights[bass.ds(i * 2 + e, 1)].squeeze(0)).then_inc(m.w_loaded[e], 16)

        @block.tensor
        def _(pe):
            with pe.Fori(0, E // 2) as i:
                def up(s):
                    e, half = s // 2, s % 2
                    if half == 0:
                        pe.wait_ge(m.w_loaded[e], i * 16 + 16 * (E0 // 2 + 1))
                    for fc in range(FC):
                        u = unit(i, s, fc)
                        pe.wait_ge(m.act_done.sem, m.act_done.free(u + U0))
                        at = slice(fc * 128, (fc + 1) * 128)
                        cols = slice(half * HALF, (half + 1) * HALF)
                        t = nc.tensor.matmul(G[fc % 2][:], W[e][:, at], m.XNT[:, cols], start=True, stop=True)
                        if gated:
                            pe.wait_ge(m.h_done.sem, m.h_done.free(u + H0))
                            at = slice(F + fc * 128, F + (fc + 1) * 128)
                            t = nc.tensor.matmul(U[fc % 2][:], W[e][:, at], m.XNT[:, cols], start=True, stop=True)
                        t.then_inc(m.up_done.sem, 1)

                def to_down(s):
                    e = s // 2
                    last = unit(i, s, FC - 1)
                    if gated:
                        pe.wait_ge(m.h_done.sem, m.h_done.ended(last + H0))
                    else:
                        pe.wait_ge(m.act_done.sem, m.act_done.ended(last + U0))
                    pe.wait_ge(m.added.sem, m.added.free(i * 16 + (4 * (S0 + s) + 3)))
                    for b in range(B // 2):
                        for fc in range(FC):
                            t = nc.tensor.matmul(Y[s % 2][:, b, :], hid[s % 2][:, fc, b * S:(b + 1) * S],
                                                 W[e][:, down + fc * 128:down + (fc + 1) * 128],
                                                 start=(fc == 0), stop=(fc == FC - 1))
                    t.then_inc(m.y_done.sem, 1)

                for what, s in order:
                    (up if what == "up" else to_down)(s)

        @block.scalar
        def _(act):
            with act.Fori(0, E // 2) as i:
                m.act_steps.enter(i, 1)
                m.load_table(act, func)
                m.act_steps.leave(E // 2)
                for s in range(4):
                    for fc in range(FC):
                        u = unit(i, s, fc)
                        act.wait_ge(m.up_done.sem, m.up_done.ended(u + U0))
                        if gated:
                            act.wait_ge(m.h_done.sem, m.h_done.free(u + H0))
                            t = nc.scalar.activation(silu[fc % 2][:], G[fc % 2][:], func)
                        else:
                            if fc == 0:
                                act.wait_ge(m.y_done.sem, m.y_done.free(i * 4 + (S0 + s)))
                            t = nc.scalar.activation(hid[s % 2][:, fc, :], G[fc % 2][:], func,
                                                     bias=W[s // 2][:, down + F + fc:down + F + fc + 1])
                        t.then_inc(m.act_done.sem, 1)

        if residual is not None:
            residual_added = m.sem("residual_added")

            @block.gpsimd
            def _(pool):
                nc.gpsimd.tensor_tensor(m.X[:], m.X[:], residual[:], ALU.add).then_inc(residual_added, 1)

        @block.vector
        def _(dve):
            if residual is not None:
                dve.wait_ge(residual_added, 1)
            with dve.Fori(0, E // 2) as i:
                def gate(s):
                    for fc in range(FC):
                        u = unit(i, s, fc)
                        if fc == 0:
                            dve.wait_ge(m.y_done.sem, m.y_done.free(i * 4 + (S0 + s)))
                        dve.wait_ge(m.act_done.sem, m.act_done.ended(u + U0))
                        nc.vector.tensor_tensor(hid[s % 2][:, fc, :], silu[fc % 2][:], U[fc % 2][:],
                                                ALU.mult).then_inc(m.h_done.sem, 1)

                def add(s):
                    n = i * 16 + 4 * (S0 + s)
                    dve.wait_ge(m.y_done.sem, m.y_done.ended(i * 4 + (S0 + s)))
                    dve.wait_ge(m.added.sem, m.added.ended(n - 1))
                    for b in range(B // 2):
                        x = m.X[:, (s % 2) * (B // 2) + b, :]
                        at = i * 2 + ((s % 2) * (B // 2) + b) * EP + s // 2
                        nc.vector.scalar_tensor_tensor(
                            out=x, in0=Y[s % 2][:, b, :], scalar=comb[:].rearrange("p b e -> p (b e)")[:, bass.ds(at, 1)],
                            in1=x, op0=ALU.mult, op1=ALU.add).then_inc(m.added.sem, 1)

                for what, s in order:
                    if what == "down":
                        add(s)
                    elif gated:
                        gate(s)

        done = m.added.ended(8 * (E0 + E) - 1)
        complete = lambda dve, half: (m.added.sem, done - 4 + 4 * half)
        if b2 is not None:
            combT = sb("combT", [EP, T])
            k, k2 = m.n_turn, m.n_b2
            m.n_turn += 2
            m.n_b2 += 2

            @block.tensor
            def _(pe):
                pe.wait_ge(m.dve_steps.sem, route.comb_value)
                for b in range(B):
                    t = nc.tensor.transpose(norm.ps[0:EP, b * S:(b + 1) * S], comb[:, b, :], m.w("ident"))
                    if b % 4 == 3:
                        t.then_inc(m.comb_turned, 1)
                pe.wait_ge(m.act_done.sem, m.act_done.ended(2 * E * FC - 1 + U0))
                for b in range(B):
                    if b % 4 == 0:
                        pe.wait_ge(m.comb_copied, k + b // 4 + 1)
                    t = nc.tensor.matmul(G[b // 4][:, b % 4 * D:(b % 4 + 1) * D], combT[:, b * S:(b + 1) * S], b2,
                                         start=True, stop=True)
                    if b % 4 == 3:
                        t.then_inc(m.b2_done, 1)

            @block.scalar
            def _(act):
                for half in range(2):
                    act.wait_ge(m.comb_turned, k + half + 1)
                    cols = slice(half * HALF, (half + 1) * HALF)
                    nc.scalar.activation(combT[:, cols], norm.ps[0:EP, cols], ACT.Copy).then_inc(m.comb_copied, 1)

            def complete(dve, half):
                dve.wait_ge(m.added.sem, done - 4 + 4 * half)
                dve.wait_ge(m.b2_done, k2 + half + 1)
                x = m.X[:, half * (B // 2):(half + 1) * (B // 2), :]
                term = G[half][:].rearrange("p (b d) -> p b d", b=B // 2)
                return m.dve_steps.sem, m.dve_steps.inc(nc.vector.tensor_tensor(x, x, term, ALU.add))

        if norm is not None:
            norm.emit(block, complete)


def ffn0_stage(nc, m):
    C, EC = 5, 4
    units = [(c, half) for c in range(C) for half in range(2)]
    spreads = [(c, half) for c in range(EC) for half in range(2)]
    cols = lambda half: slice(half * HALF, (half + 1) * HALF)
    with ExitStack() as ctx:
        sb = lambda name, shape, dt=F32: ctx.enter_context(nc.sbuf_tensor(f"{name}_f0", shape, dt))
        comb, combT = sb("comb", [S, B, 8]), sb("combT", [128, T])
        hid, up = sb("hid", [128, C, T]), sb("up", [128, C, T])
        wg, wu, wd = (m.w(f"L0f_{k}") for k in "gud")
        at = lambda c: slice(c * 128, (c + 1) * 128)
        hid_ready, spread_done, spread_used = (m.sem(n) for n in ("f0_hidden", "f0_spread", "f0_spread_used"))
        with ExitStack() as inner:
            psum = lambda name: [inner.enter_context(nc.psum_tensor(f"{name}_f0_{i}", [128, HALF], F32))
                                 for i in range(2)]
            G, U, P = psum("G"), psum("U"), psum("P")
            route = Route(nc, m, inner, 8, m.w("L0f_router"), "sigmoid", comb[:])
            block = inner.enter_context(nc.Block())
            base_p, base_e = m.n_proj, m.n_evac
            m.n_proj += len(units)
            m.n_evac += len(units)
            k = m.n_turn
            m.n_turn += 2
            route.emit(block)

            @block.tensor
            def _(pe):
                for u, (c, half) in enumerate(units):
                    if u >= 2:
                        pe.wait_ge(m.evac, base_e + u - 1)
                    for ps, w in ((G, wg), (U, wu)):
                        t = nc.tensor.matmul(ps[u % 2][:], w[:, at(c)], m.XNT[:, cols(half)], start=True, stop=True)
                    t.then_inc(m.proj, 1)
                    if u == 5:
                        pe.wait_ge(m.dve_steps.sem, route.comb_value)
                        for b in range(B):
                            t = nc.tensor.transpose(P[b // 4][0:8, b % 4 * S:(b % 4 + 1) * S], comb[:, b, :],
                                                    m.w("ident"))
                            if b % 4 == 3:
                                t.then_inc(m.comb_turned, 1)
                pe.wait_ge(m.comb_copied, k + 2)
                for u, (c, half) in enumerate(spreads):
                    if u >= 2:
                        pe.wait_ge(spread_used, u - 1)
                    nc.tensor.matmul(P[u % 2][:], m.w("L0f_sel")[:, at(c)], combT[:, cols(half)], start=True,
                                     stop=True).then_inc(spread_done, 1)

            @block.scalar
            def _(act):
                for u, (c, half) in enumerate(units):
                    act.wait_ge(m.proj, base_p + u + 1)
                    nc.scalar.activation(hid[:, c, cols(half)], G[u % 2][:], ACT.Silu)
                    nc.scalar.activation(up[:, c, cols(half)], U[u % 2][:], ACT.Copy).then_inc(m.evac, 1)

            @block.gpsimd
            def _(pool):
                for u, (c, half) in enumerate(units):
                    pool.wait_ge(m.evac, base_e + u + 1)
                    x = hid[:, c, cols(half)]
                    nc.gpsimd.tensor_tensor(x, x, up[:, c, cols(half)], ALU.mult).then_inc(hid_ready, 1)

            @block.vector
            def _(dve):
                dve.wait_ge(m.bias_loaded, 16)
                nc.vector.scalar_tensor_tensor(out=m.pos_bias[:], in0=m.pos_bias[:], scalar=float(DH) ** 0.5,
                                               in1=bcast_mid(m.w("causal_flip"), H), op0=ALU.mult, op1=ALU.add)
                m.dve_steps.done(dve, nc.vector.tensor_reduce(
                    m.ctx_mean[:], m.CT[:].rearrange("p (b s) -> p b s", b=B), AX.X, ALU.add))
                nc.vector.tensor_scalar(m.ctx_mean[:], m.ctx_mean[:], 1.0 / S, None, ALU.mult)
                m.dve_steps.done(dve, nc.vector.memset(combT[:], 0.0))
                for half in range(2):
                    dve.wait_ge(m.comb_turned, k + half + 1)
                    nc.vector.tensor_copy(combT[0:8, cols(half)], P[half][0:8, :]).then_inc(m.comb_copied, 1)
                for u, (c, half) in enumerate(spreads):
                    dve.wait_ge(spread_done, u + 1)
                    dve.wait_ge(hid_ready, u + 1)
                    x = hid[:, c, cols(half)]
                    nc.vector.tensor_tensor(x, x, P[u % 2][:], ALU.mult).then_inc(spread_used, 1)
        add_products(nc, m, [((lambda b, c=c: hid[:, c, b * S:(b + 1) * S]), wd[:, at(c)]) for c in range(C)])


def cross_attention0(nc, m):
    with ExitStack() as ctx:
        sb = lambda name, shape, dt=F32: ctx.enter_context(nc.sbuf_tensor(f"{name}_x0", shape, dt))
        QT, KT = sb("QT", [D, T]), sb("KT", [D, T])
        V = sb("V", [S, B, H, DH + 1])
        hidden = sb("hidden", [S, B, S])
        four = lambda a: (lambda half: a[:, half * (B // 2):(half + 1) * (B // 2), :])
        attention_inputs(nc, m, [(QT, m.XNT, m.w("L0x_q"), m.w("L0x_qs")), (KT, m.CT, m.w("L0x_k"), m.w("L0x_ks"))],
                         V, m.CT, m.w("L0x_v"), turn=(four(m.masked_cos), four(m.masked_sin)),
                         hidden=hidden)
        attend(nc, m, QT, KT, V, m.O,
               bias=lambda g, b: bcast_mid(hidden[:, bass.ds(b, 1), :].squeeze(1), HG))
    out_project(nc, m, m.O, m.w("L0x_o"))


def attention1(nc, m):
    with ExitStack() as ctx:
        sb = lambda name, shape, dt=F32: ctx.enter_context(nc.sbuf_tensor(f"{name}_a1", shape, dt))
        QT, KT = sb("QT", [D, T]), sb("KT", [D, T])
        V = sb("V", [S, B, H, DH + 1])
        BN = HALF // S
        bias = sb("bias", [S, H, S])
        attention_inputs(nc, m, [(QT, m.XNT, m.w("L1a_q"), m.w("L1a_bq")), (KT, m.XNT, m.w("L1a_k"), m.w("L1a_bk"))],
                         V, m.XNT, m.w("L1a_v"), m.row("L1a_bv"), flipped=bias)
        attend(nc, m, QT, KT, V, m.O, bias=lambda g, b: bias[:, g * HG:(g + 1) * HG, :])
    out_project(nc, m, m.O, m.w("L1a_o"), m.row("L1a_bo"))


def mix_stage1(nc, m):
    add_products(nc, m, [((lambda b: m.XNT[:, b * S:(b + 1) * S]), m.w("L1x_w1")),
                         ((lambda b: m.ctx_mean[:, b:b + 1].to_broadcast([D, S])), m.w("L1x_w2"))],
                 bias_row=m.row("L1x_b"))


def ffn1_stage(nc, m):
    expert_stage(nc, m, "L1f", 16, 2, "softmax_two", ACT.Relu, m.dram["L1f_w"],
                 rows=(m.row("L1f_bg"), m.row("L1f_bias")), b2=m.w("L1f_b2", slice(0, 16)))


def attention2(nc, m):
    with ExitStack() as ctx:
        sb = lambda name, shape, dt=F32: ctx.enter_context(nc.sbuf_tensor(f"{name}_a2", shape, dt))
        QT, KT = sb("QT", [D, T]), sb("KT", [D, T])
        V = sb("V", [S, B, H, DH + 1])
        attention_inputs(nc, m, [(QT, m.XNT, m.w("L2a_q"), m.w("L2a_qs")), (KT, m.XNT, m.w("L2a_k"), m.w("L2a_ks"))],
                         V, m.XNT, m.w("L2a_v"),
                         turn=[lambda half, t=t: bcast_mid(m.w(t), B // 2) for t in ("rope2c", "rope2s")])
        attend(nc, m, QT, KT, V, m.O, bias=m.causal)
    out_project(nc, m, m.O, m.w("L2a_o"))


def bidirectional2(nc, m):
    with ExitStack() as outer:
        sb = lambda name, shape, dt=F32: outer.enter_context(nc.sbuf_tensor(f"{name}_x2", shape, dt))
        hw, P, PTs = sb("hw", [D, T]), sb("P", [S, B, S]), sb("PTs", [S, T])
        F2, F3, F4 = (sb(name, [D, T]) for name in ("F2", "F3", "F4"))
        top, total, best = sb("top", [S, B]), sb("total", [S, B]), sb("best", [S, B])
        batt, btop, btotal = sb("batt", [B, S]), sb("btop", [B, 1]), sb("btotal", [B, 1])
        battT, hc = sb("battT", [S, B]), sb("hc", [D, B])
        steps = m.dve_steps
        halves = [slice(0, HALF), slice(HALF, T)]
        with ExitStack() as ctx:
            sim = ctx.enter_context(nc.psum_tensor("sim", [S, B, S], F32))
            small = ctx.enter_context(nc.psum_tensor("small_x2", [S, 256], F32))
            base_p, base_e = m.n_proj, m.n_evac
            m.n_proj += 3
            m.n_evac += 2
            v = {}
            with nc.Block() as block:
                @block.vector
                def _(dve):
                    v["hw"] = steps.inc(nc.vector.tensor_scalar(hw[:], m.XNT[:], m.w("L2x_w3"), m.w("L2x_w2"),
                                                                ALU.mult, ALU.add))
                    dve.wait_ge(m.proj, base_p + 1)
                    steps.done(dve, nc.vector.tensor_reduce(top[:], sim[:], AX.X, ALU.max))
                    v["shift"] = steps.inc(nc.vector.tensor_tensor(P[:], sim[:], bcast_last(top[:], S), ALU.subtract))
                    steps.done(dve, nc.vector.tensor_tensor(best[:], top[:], small[:, 0:B], ALU.add))
                    v["best"] = steps.inc(nc.vector.tensor_scalar(best[:], best[:], m.row("L2x_bsim"), None, ALU.add))
                    dve.wait_ge(m.proj, base_p + 2)
                    steps.done(dve, nc.vector.tensor_reduce(btop[:], small[0:B, 128:256], AX.X, ALU.max))
                    v["bshift"] = steps.inc(nc.vector.tensor_scalar(batt[:], small[0:B, 128:256], btop[:], None,
                                                                    ALU.subtract))
                    dve.wait_ge(m.evac, base_e + 2)
                    steps.done(dve, nc.vector.tensor_reduce(total[:], P[:], AX.X, ALU.add))
                    steps.done(dve, nc.vector.reciprocal(total[:], total[:]))
                    steps.done(dve, nc.vector.tensor_tensor(P[:], P[:], bcast_last(total[:], S), ALU.mult))
                    steps.done(dve, nc.vector.tensor_reduce(btotal[:], batt[:], AX.X, ALU.add))
                    steps.done(dve, nc.vector.reciprocal(btotal[:], btotal[:]))
                    nc.vector.tensor_scalar(batt[:], batt[:], btotal[:], None, ALU.mult)

                @block.tensor
                def _(pe):
                    for b in range(B):
                        nc.tensor.matmul(small[:, b:b + 1], m.XNT[:, b * S:(b + 1) * S], m.w("L2x_w1"),
                                         start=True, stop=True)
                    pe.wait_ge(steps.sem, v["hw"])
                    for b in range(B):
                        t = nc.tensor.matmul(sim[:, b, :], hw[:, b * S:(b + 1) * S], m.CT[:, b * S:(b + 1) * S],
                                             start=True, stop=True)
                    t.then_inc(m.proj, 1)
                    pe.wait_ge(steps.sem, v["best"])
                    nc.tensor.transpose(small[0:B, 128:256], best[:], m.w("ident")).then_inc(m.proj, 2)

                @block.scalar
                def _(act):
                    act.wait_ge(steps.sem, v["shift"])
                    nc.scalar.activation(P[:], P[:], ACT.Exp).then_inc(m.evac, 1)
                    act.wait_ge(steps.sem, v["bshift"])
                    nc.scalar.activation(batt[:], batt[:], ACT.Exp).then_inc(m.evac, 1)
        with ExitStack() as ctx:
            pt = ctx.enter_context(nc.psum_tensor("pt_x2", [S, T], F32))
            hat = ctx.enter_context(nc.psum_tensor("hat", [D, T], F32))
            small = ctx.enter_context(nc.psum_tensor("small2", [S, 256], F32))
            base_p, base_e = m.n_proj, m.n_evac
            m.n_proj += 6
            m.n_evac += 5
            with nc.Block() as block:
                @block.tensor
                def _(pe):
                    nc.tensor.transpose(small[:, 0:B], batt[:], m.w("ident", slice(0, B))[:, 0:B]).then_inc(m.proj, 1)
                    for b in range(B):
                        t = nc.tensor.transpose(pt[:, b * S:(b + 1) * S], P[:, b, :], m.w("ident"))
                        if b % 4 == 3:
                            t.then_inc(m.proj, 1)
                    pe.wait_ge(m.evac, base_e + 1)
                    for b in range(B):
                        t = nc.tensor.matmul(small[:, 128 + b:129 + b], m.XN[:, b, :], battT[:, b:b + 1],
                                             start=True, stop=True)
                    t.then_inc(m.proj, 1)
                    for b in range(B):
                        if b % 4 == 0:
                            pe.wait_ge(m.evac, base_e + 2 + b // 4)
                        t = nc.tensor.matmul(hat[:, b * S:(b + 1) * S], m.CTOK[:, b, :], PTs[:, b * S:(b + 1) * S],
                                             start=True, stop=True)
                        if b % 4 == 3:
                            t.then_inc(m.proj, 1)

                @block.scalar
                def _(act):
                    act.wait_ge(m.proj, base_p + 1)
                    nc.scalar.activation(battT[:], small[:, 0:B], ACT.Copy).then_inc(m.evac, 1)
                    for half in range(2):
                        act.wait_ge(m.proj, base_p + 2 + half)
                        nc.scalar.activation(PTs[:, halves[half]], pt[:, halves[half]], ACT.Copy).then_inc(m.evac, 1)
                    for half in range(2):
                        act.wait_ge(m.proj, base_p + 5 + half)
                        nc.scalar.activation(F2[:, halves[half]], hat[:, halves[half]], ACT.Copy).then_inc(m.evac, 1)

                @block.vector
                def _(dve):
                    dve.wait_ge(m.proj, base_p + 4)
                    steps.done(dve, nc.vector.tensor_copy(hc[:], small[:, 128:128 + B]))
                    nc.vector.tensor_tensor(F4[:].rearrange("p (b s) -> p b s", b=B),
                                            m.XNT[:].rearrange("p (b s) -> p b s", b=B), bcast_last(hc[:], S), ALU.mult)
                    for half in range(2):
                        dve.wait_ge(m.evac, base_e + 4 + half)
                        nc.vector.tensor_tensor(F3[:, halves[half]], m.XNT[:, halves[half]], F2[:, halves[half]],
                                                ALU.mult)
        w = m.w("L2x_wqv")
        add_products(nc, m, [((lambda b, f=f: f[:, b * S:(b + 1) * S]), w[:, k * D:(k + 1) * D])
                             for k, f in enumerate((m.XNT, F2, F3, F4))], bias_row=m.row("L2x_b"))


def block2(nc, m):
    norm_stage(nc, m, m.XN, m.O, m.w("L2n1_w"), m.w("L2n1_b"))
    with ExitStack() as ctx:
        sb = lambda name, shape, dt=F32: ctx.enter_context(nc.sbuf_tensor(f"{name}_b2", shape, dt))
        QT, KT = sb("QT", [D, T]), sb("KT", [D, T])
        V = sb("V", [S, B, H, DH + 1])
        attention_inputs(nc, m, [(QT, m.XNT, m.w("L2f_q"), m.w("L2f_bq")), (KT, m.XNT, m.w("L2f_k"), m.w("L2f_bk"))],
                         V, m.XNT, m.w("L2f_v"), m.row("L2f_bv"))
        attend(nc, m, QT, KT, V, m.O, bias=m.causal)
    out_project(nc, m, m.O, m.w("L2f_o"), m.row("L2f_bo"), target=m.XN,
                norm=(m.XN, m.O, m.w("L2n2_w"), m.w("L2n2_b")))
    expert_stage(nc, m, "L2f", 8, 4, "softmax_two", ACT.Gelu, m.dram["L2f_w"],
                 b2=m.w("L2f_b2", slice(0, 8)), residual=m.XN)


def attention3(nc, m):
    with ExitStack() as ctx:
        sb = lambda name, shape, dt=F32: ctx.enter_context(nc.sbuf_tensor(f"{name}_a3", shape, dt))
        QT, KT, K2T = sb("QT", [D, T]), sb("KT", [D, T]), sb("K2T", [D, T])
        V, O2 = sb("V", [S, B, H, DH + 1]), sb("O2", [S, B, D])
        attention_inputs(nc, m, [(QT, m.XNT, m.w("L3a_q"), m.w("L3a_bq")), (KT, m.XNT, m.w("L3a_k"), m.w("L3a_bk")),
                                 (K2T, m.XNT, m.w("L3a_k2"), m.w("L3a_bk2"))], V)
        attend(nc, m, QT, KT, V, m.O, bias=m.causal)
        with ExitStack() as inner:
            later = inner.enter_context(nc.psum_tensor("later", [S, B, D], F32))
            base = m.n_proj
            m.n_proj += 1
            with nc.Block() as block:
                @block.tensor
                def _(pe):
                    for b in range(B):
                        t = nc.tensor.transpose(later[0:S - 1, b, :], m.XNT[:, b * S + 1:(b + 1) * S], m.w("ident"))
                    t.then_inc(m.proj, 1)

                @block.vector
                def _(dve):
                    dve.wait_ge(m.proj, base + 1)
                    v4 = lambda a: a.rearrange("p b (h d) -> p b h d", h=H)
                    for b in range(B):
                        heads = lambda a: a[0:S - 1, b, :].rearrange("p (h d) -> p h d", h=H)
                        nc.vector.tensor_tensor(V[0:S - 1, b, :, 0:DH], heads(later), heads(m.O), ALU.subtract)
        attend(nc, m, QT, K2T, V, O2, bias=m.strict)
        with nc.Block() as block:
            @block.vector
            def _(dve):
                nc.vector.scalar_tensor_tensor(out=m.O[:], in0=O2[:], scalar=m.w("row1"), in1=m.O[:], op0=ALU.mult,
                                               op1=ALU.add)
    out_project(nc, m, m.O, m.w("L3a_o"), m.row("L3a_bo"), bias_times=2.0)


def autocorrelation3(nc, m):
    steps = m.dve_steps
    TOP = 4
    with ExitStack() as outer:
        sb = lambda name, shape, dt=F32: outer.enter_context(nc.sbuf_tensor(f"{name}_x3", shape, dt))
        fq, fq_swapped, fk, fv = (sb(name, [S, T]) for name in ("fq", "fq_swapped", "fk", "fv"))
        same, swapped = sb("same", [S, T]), sb("swapped", [S, T])
        sums, sums_swapped = sb("sums", [S, B * H]), sb("sums_swapped", [S, B * H])
        corr, best, index = sb("corr", [128, S]), sb("best", [128, 8]), sb("index", [128, 8], U32)
        indexf, wt, one = sb("indexf", [128, TOP]), sb("wt", [128, TOP]), sb("one", [128, 1])
        wvec, wtmp, wT = sb("wvec", [128, S]), sb("wtmp", [128, S]), sb("wT", [S, 128])
        autocorrelation_inputs(nc, m, (fq, fq_swapped, fk, fv))
        ps_ctx = ExitStack()
        pc = ps_ctx.enter_context(nc.psum_tensor("corr_ps", [128, S], F32))
        pw = ps_ctx.enter_context(nc.psum_tensor("w_ps", [128, 3 * 128], F32))
        base_p, base_e = m.n_proj, m.n_evac
        m.n_proj += 3
        m.n_evac += 2
        v = {}
        with nc.Block() as block:
            @block.vector
            def _(dve):
                tt = lambda out, a, b, op: steps.inc(nc.vector.tensor_tensor(out, a, b, op))
                heads = lambda a: a[:].rearrange("p (g d) -> p g d", d=DH)
                v1 = tt(same[:], fq[:], fk[:], ALU.mult)
                v2 = tt(swapped[:], fq_swapped[:], fk[:], ALU.mult)
                dve.wait_ge(steps.sem, v1)
                v["sums"] = steps.inc(nc.vector.tensor_reduce(sums[:], heads(same), AX.X, ALU.add))
                dve.wait_ge(steps.sem, v2)
                v["sums"] = steps.inc(nc.vector.tensor_reduce(sums_swapped[:], heads(swapped), AX.X, ALU.add))
                dve.wait_ge(m.proj, base_p + 1)
                steps.done(dve, nc.vector.tensor_copy(corr[:], pc[:]))
                steps.done(dve, nc.vector.max(best[:], corr[:]))
                v["shift"] = steps.inc(nc.vector.tensor_scalar(wt[:], best[:, 0:TOP], best[:, 0:1], None, ALU.subtract))
                steps.done(dve, nc.vector.max_index(index[:], best[:], corr[:]))
                steps.done(dve, nc.vector.tensor_copy(indexf[:], index[:, 0:TOP]))
                dve.wait_ge(m.evac, base_e + 1)
                steps.done(dve, nc.vector.tensor_reduce(one[:], wt[:], AX.X, ALU.add))
                steps.done(dve, nc.vector.reciprocal(one[:], one[:]))
                steps.done(dve, nc.vector.tensor_scalar(wt[:], wt[:], one[:], None, ALU.mult))
                for k in range(TOP):
                    out = wvec if k == 0 else wtmp
                    steps.done(dve, nc.vector.tensor_scalar(out[:], m.w("iota128"), indexf[:, k:k + 1], wt[:, k:k + 1],
                                                            ALU.is_equal, ALU.mult))
                    if k:
                        dve.wait_ge(steps.sem, tt(wvec[:], wvec[:], wtmp[:], ALU.add))
                v["wvec"] = steps.n
                dve.wait_ge(m.proj, base_p + 2)
                v["wT"] = steps.inc(nc.vector.tensor_copy(wT[:], pw[:, 0:128]))
                dve.wait_ge(m.proj, base_p + 3)
                tt(heads(same), heads(fv), bcast_last(pw[:, 128:256], DH), ALU.mult)
                tt(heads(swapped), heads(fv), bcast_last(pw[:, 256:384], DH), ALU.mult)

            @block.tensor
            def _(pe):
                pe.wait_ge(steps.sem, v["sums"])
                nc.tensor.matmul(pc[:], sums[:], m.w("corr_same"), start=True, stop=False)
                nc.tensor.matmul(pc[:], sums_swapped[:], m.w("corr_swapped"), start=False, stop=True).then_inc(m.proj, 1)
                pe.wait_ge(steps.sem, v["wvec"])
                nc.tensor.transpose(pw[:, 0:128], wvec[:], m.w("ident")).then_inc(m.proj, 1)
                pe.wait_ge(steps.sem, v["wT"])
                nc.tensor.matmul(pw[:, 128:256], m.w("dft"), wT[:], start=True, stop=True)
                nc.tensor.matmul(pw[:, 256:384], m.w("dft_swapped"), wT[:], start=True, stop=True).then_inc(m.proj, 1)

            @block.scalar
            def _(act):
                m.load_table(act, ACT.Exp)
                act.wait_ge(steps.sem, v["shift"])
                nc.scalar.activation(wt[:], wt[:], ACT.Exp).then_inc(m.evac, 2)
        ps_ctx.close()
        project(nc, m, [(m.O[:].rearrange("p b d -> p (b d)"), [m.w("roll_same"), m.w("roll_swapped")],
                         [same[:], swapped[:]], None)])
    out_project(nc, m, m.O, m.w("L3x_o"), m.row("L3x_bo"))


def autocorrelation_inputs(nc, m, transforms):
    with ExitStack() as ctx:
        tok = [ctx.enter_context(nc.sbuf_tensor(f"tok{k}_x3", [S, B, D], F32)) for k in range(3)]
        pl = [ctx.enter_context(nc.psum_tensor(f"lin_ps{k}", [S, B, D], F32)) for k in range(2)]
        pt = [ctx.enter_context(nc.psum_tensor(f"dft_ps{k}", [S, HALF], F32)) for k in range(4)]
        lin_done, tok_ready = m.sem("lin_done"), m.sem("tok_ready")
        base_p, base_e = m.n_proj, m.n_evac
        units = [(k, w, x, half) for k, (w, x) in enumerate((("dft", 0), ("dft_swapped", 0), ("dft", 1), ("dft", 2)))
                 for half in range(2)]
        m.n_proj += len(units)
        m.n_evac += len(units)
        cols = lambda half: slice(half * HALF, (half + 1) * HALF)
        block = ctx.enter_context(nc.Block())

        @block.tensor
        def _(pe):
            def linear(k):
                source = m.XNT if k == 0 else m.CT
                if k == 2:
                    pe.wait_ge(tok_ready, 2)
                for b in range(B):
                    t = nc.tensor.matmul(pl[k % 2][:, b, :], source[:, b * S:(b + 1) * S], m.w("L3x_" + "qkv"[k]),
                                         start=True, stop=True)
                    if b % 4 == 3:
                        t.then_inc(lin_done, 1)

            linear(0)
            linear(1)
            for u, (k, w, x, half) in enumerate(units):
                if u == 4:
                    linear(2)
                pe.wait_ge(tok_ready, 2 * x + half + 1)
                if u >= 4:
                    pe.wait_ge(m.evac, base_e + u - 3)
                flat = tok[x][:].rearrange("p b d -> p (b d)")
                nc.tensor.matmul(pt[u % 4][:], m.w(w), flat[:, cols(half)], start=True, stop=True).then_inc(m.proj, 1)

        @block.vector
        def _(dve):
            for k in range(3):
                for half in range(2):
                    dve.wait_ge(lin_done, 2 * k + half + 1)
                    bs = slice(4 * half, 4 * half + 4)
                    nc.vector.tensor_tensor(tok[k][:, bs, :], pl[k % 2][:, bs, :],
                                            bcast_mid(m.row("L3x_b" + "qkv"[k]), B // 2), ALU.add).then_inc(tok_ready, 1)

        @block.scalar
        def _(act):
            for u, (k, w, x, half) in enumerate(units):
                act.wait_ge(m.proj, base_p + u + 1)
                nc.scalar.activation(transforms[k][:, cols(half)], pt[u % 4][:], ACT.Copy).then_inc(m.evac, 1)


def ffn3_stage(nc, m):
    expert_stage(nc, m, "L3f", 7, 4, "softmax_all", ACT.Silu, m.dram["L3f_w"], gated=True, last=True)


def build(nc, dram, stages):
    with ExitStack() as ctx:
        m = Model(nc, ctx, dram)
        start_stage(nc, m)
        todo = [lambda: mamba_stage(nc, m)] + [lambda f=f: f(nc, m) for f in STAGES]
        for k in range(stages):
            todo[k]()
        with nc.Block() as block:
            @block.sync
            def _(sp):
                if stages < 3:
                    sp.wait_ge(m.bias_loaded, 16)
                sp.dma_start(dram["out"], m.X[:]).then_inc(m.stored, 16)
                sp.wait_ge(m.stored, 16)


STAGES = [cross_attention0, ffn0_stage, attention1, mix_stage1, ffn1_stage, attention2, bidirectional2, block2, attention3,
          autocorrelation3, ffn3_stage]
N_STAGES = 12


def pack(table, total, arrays, rows=128):
    out = np.zeros((rows, total), np.float32)
    for name, (at, n) in table.items():
        a = np.asarray(arrays[name]).reshape(-1, n)
        out[:a.shape[0], at:at + n] = a
    return out


def host_arrays(i):
    def chunks(a, width):
        return a.reshape(-1, 128, width).transpose(1, 0, 2).reshape(128, -1)

    a = {}
    a["ident"] = np.eye(128, dtype=np.float32)
    a["ln_w"], a["ln_b"] = (i[f"L0_attn_{n}"].reshape(128, 1) for n in ("ln_w", "ln_b"))
    a["W_in"] = i["L0_attn_W_in"]
    a["conv_w"] = chunks(i["L0_attn_conv_w"].reshape(INNER, TAPS), TAPS)
    a["conv_b"] = chunks(i["L0_attn_conv_b"].reshape(INNER, 1), 1)
    a["W_xproj"] = chunks(i["L0_attn_W_xproj"], RANK + 2 * STATE)
    a["W_dt"] = i["L0_attn_W_dt"]
    a["b_dt"] = chunks(i["L0_attn_b_dt"].reshape(INNER, 1), 1)
    a["A_log"] = chunks(i["L0_attn_A_log"], STATE)
    a["Dskip"] = chunks(i["L0_attn_D"].reshape(INNER, 1), 1)
    a["W_out"] = chunks(i["L0_attn_W_out"], D)

    p, t = np.arange(128), np.arange(S)
    a["head_mask"] = (p[:, None] // DH == np.arange(H)).astype(np.float32)
    a["causal"] = np.where(t[None, :] > t[:, None], NEG, 0.0).astype(np.float32)
    a["flip"], a["causal_flip"] = a["ident"][::-1], a["causal"][::-1]
    a["strict"] = np.where(t[None, :] >= t[:, None], NEG, 0.0).astype(np.float32)
    a["row1"] = (t[:, None] > 0).astype(np.float32)
    a["iota16"] = np.tile(np.arange(16, dtype=np.float32), (128, 1))
    a["iota128"] = np.tile(np.arange(128, dtype=np.float32), (128, 1))
    w0 = (1.0 / 10000.0 ** (np.arange(1, DH + 1, 2, dtype=np.float32) / DH)).astype(np.float32)
    ang0 = np.arange(1, S + 1, dtype=np.float32)[:, None] * w0
    d = p % DH
    a["rope0c"] = np.cos(ang0).T[d // 2]
    a["rope0s"] = np.sin(ang0).T[d // 2] * np.where(d % 2, 1, -1)[:, None]
    w2 = (1.0 / 10000.0 ** (np.arange(DH // 2, dtype=np.float32) / (DH // 2))).astype(np.float32)
    ang2 = np.arange(S, dtype=np.float32)[:, None] * w2
    a["rope2c"] = np.cos(ang2).T[d % 4]
    a["rope2s"] = np.sin(ang2).T[d % 4] * np.where(d < 4, -1, 1)[:, None]
    f = np.arange(FREQ)
    theta = 2 * np.pi * (t[:, None] * f % S) / S
    inner = slice(1, FREQ - 1)
    cos, sin = np.cos(theta), np.sin(theta)
    sin[:, 0] = sin[:, FREQ - 1] = 0.0
    a["dft"] = np.concatenate([cos, sin[:, inner]], axis=1)
    a["dft_swapped"] = np.concatenate([sin, cos[:, inner]], axis=1)
    both = np.where((f == 0) | (f == S // 2), 1.0, 2.0)[:, None] / S
    inv_c, inv_s = cos.T * both, sin.T * both
    a["corr_same"] = np.concatenate([inv_c, inv_c[inner]]) / DH
    a["corr_swapped"] = np.concatenate([inv_s, -inv_s[inner]]) / DH
    a["roll_same"] = np.concatenate([inv_c, -inv_c[inner]])
    a["roll_swapped"] = np.concatenate([inv_s, inv_s[inner]])
    a["L0f_sel"] = (np.arange(512) // 64 == np.arange(8)[:, None]).astype(np.float32)

    pairs = p ^ 1
    halves = p // DH * DH + (d + DH // 2) % DH
    wkv = i["L0_xattn_W_kv"]
    a["L0x_q"], a["L0x_k"], a["L0x_v"], a["L0x_o"] = i["L0_xattn_W_q"], wkv[:, :D], wkv[:, D:], i["L0_xattn_W_c"]
    a["L0x_qs"], a["L0x_ks"] = a["L0x_q"][:, pairs], a["L0x_k"][:, pairs]
    a["L0f_router"] = i["L0_ffn_gate_weight"].T
    a["L0f_g"] = np.concatenate([i["L0_ffn_w_gate"].reshape(512, D), i["L0_ffn_ws_gate"]]).T
    a["L0f_u"] = np.concatenate([i["L0_ffn_w_up"].reshape(512, D), i["L0_ffn_ws_up"]]).T
    a["L0f_d"] = chunks(np.concatenate([i["L0_ffn_w_down"].transpose(0, 2, 1).reshape(512, D),
                                        i["L0_ffn_ws_down"].T]), D)
    qkv, qb = i["L1_attn_qkv_w"], i["L1_attn_qkv_b"]
    a["L1a_q"], a["L1a_k"], a["L1a_v"], a["L1a_o"] = qkv[:D].T, qkv[D:2 * D].T, qkv[2 * D:].T, i["L1_attn_proj_w"].T
    a["L1a_bq"], a["L1a_bk"], a["L1a_bv"] = qb[:D, None], qb[D:2 * D, None], qb[2 * D:]
    a["L1a_bo"] = i["L1_attn_proj_b"]
    a["L1x_w1"], a["L1x_w2"], a["L1x_b"] = i["L1_xattn_W"][:, :D].T, i["L1_xattn_W"][:, D:].T, i["L1_xattn_b"]
    a["L1f_router"], a["L1f_bg"], a["L1f_bias"] = i["L1_ffn_Wg"], i["L1_ffn_bg"], i["L1_ffn_bias"]
    a["L1f_b2"] = i["L1_ffn_b2"]
    kv = p // DH % HG * DH + d
    a["L2a_q"], a["L2a_k"], a["L2a_v"], a["L2a_o"] = (
        i["L2_attn_wq"], i["L2_attn_wk"][:, kv], i["L2_attn_wv"][:, kv], i["L2_attn_wo"])
    a["L2a_qs"], a["L2a_ks"] = a["L2a_q"][:, halves], a["L2a_k"][:, halves]
    a["L2x_w1"], a["L2x_w2"], a["L2x_w3"] = i["L2_xattn_w_sim"].reshape(3, D, 1)
    a["L2x_bsim"], a["L2x_b"], a["L2x_wqv"] = i["L2_xattn_b_sim"], i["L2_xattn_b_qv"], chunks(i["L2_xattn_W_qv"], D)
    for k in (1, 2):
        a[f"L2n{k}_w"], a[f"L2n{k}_b"] = i[f"L2_ffn_ln{k}_w"][:, None], i[f"L2_ffn_ln{k}_b"][:, None]
    w, b = i["L2_ffn_Wqkv"], i["L2_ffn_bqkv"]
    a["L2f_q"], a["L2f_k"], a["L2f_v"], a["L2f_o"] = w[:, :D], w[:, D:2 * D], w[:, 2 * D:], i["L2_ffn_Wo"]
    a["L2f_bq"], a["L2f_bk"], a["L2f_bv"], a["L2f_bo"] = b[:D, None], b[D:2 * D, None], b[2 * D:], i["L2_ffn_bo"]
    a["L2f_router"] = i["L2_ffn_gate_W"]
    a["L2f_b2"] = i["L2_ffn_fc2_b"]
    w, b = i["L3_attn_W_attn"], i["L3_attn_b_attn"]
    a["L3a_q"], a["L3a_k"], a["L3a_bq"], a["L3a_bk"] = w[:, :D], w[:, D:], b[:D, None], b[D:, None]
    a["L3a_k2"], a["L3a_bk2"] = i["L3_attn_W_k2"], i["L3_attn_b_k2"][:, None]
    a["L3a_o"], a["L3a_bo"] = i["L3_attn_W_proj"], i["L3_attn_b_proj"]
    for n in "qkvo":
        a[f"L3x_{n}"], a[f"L3x_b{n}"] = i[f"L3_xattn_W{n}"].T, i[f"L3_xattn_b{n}"]
    a["L3f_router"] = i["L3_ffn_router_w"].T
    return a


def big_arrays(i):
    def by_chunks(w):
        e, f, n = w.shape
        return w.reshape(e, f // 128, 128, n).transpose(0, 2, 1, 3).reshape(e, 128, -1)

    rel = np.zeros((2 * S, D), np.float32)
    rel[:2 * S - 1] = i["L1_attn_rel_pos_emb"][::-1]
    out = {
        "mask": i["mask_BxS2_bf1"].reshape(1, T).view(np.uint8),
        "rel_pos": rel.reshape(2, 128, D).transpose(1, 0, 2),
        "L1f_w": np.concatenate([i["L1_ffn_W1"], by_chunks(i["L1_ffn_W2"]), by_chunks(i["L1_ffn_b1"][:, :, None])], axis=2),
        "L2f_w": np.concatenate([i["L2_ffn_fc1_w"].transpose(0, 2, 1),
                                 by_chunks(i["L2_ffn_fc2_w"].transpose(0, 2, 1)),
                                 by_chunks(i["L2_ffn_fc1_b"][:, :, None])], axis=2),
    }
    gate, up, down = (np.concatenate([i[f"L3_ffn_routed_{n}"], i[f"L3_ffn_shared_{n}"][None]]).transpose(0, 2, 1)
                      for n in ("gate", "up", "down"))
    out["L3f_w"] = np.concatenate([gate, up, by_chunks(down)], axis=2)
    return {k: np.ascontiguousarray(v) for k, v in out.items()}


def kernel(**inputs):
    import concourse.bacc as bacc
    from concourse.bass_utils import run_bass_kernel_spmd

    i = {k: np.asarray(v) for k, v in inputs.items()}
    a = host_arrays(i)
    arrays = {
        "x": np.ascontiguousarray(i["x"].transpose(1, 0, 2)),
        "ctx_feat": np.ascontiguousarray(i["ctx_1024"].transpose(2, 0, 1)).reshape(D, T),
        "ctx_tok": np.ascontiguousarray(i["ctx_1024"].transpose(1, 0, 2)),
        "mamba": pack(MAMBA_AT, MAMBA_N, a),
        "small": pack(SMALL_AT, SMALL_N, a),
        "rows": pack(ROWS_AT, ROWS_N, a, rows=1),
        **big_arrays(i),
    }
    nc = bacc.Bacc("TRN2", target_bir_lowering=False, num_devices=1)
    dram = {name: nc.dram_tensor(name, list(v.shape), mybir.dt.from_np(v.dtype), kind="ExternalInput").ap()
            for name, v in arrays.items()}
    dram["rel_table"] = nc.dram_tensor("rel_table", [H, 2 * S], F32, kind="Internal").ap()
    dram["out"] = nc.dram_tensor("out", [S, B, D], F32, kind="ExternalOutput").ap()
    build(nc, dram, N_STAGES)
    result = run_bass_kernel_spmd(nc, [arrays], core_ids=[0])
    return np.ascontiguousarray(np.asarray(result.results[0]["out"]).transpose(1, 0, 2))
```
